# Optimizing a Trainium2 kernel written in Bass

```python
import numpy as np
import jax
import jax.numpy as jnp

def _softmax(x, axis=-1):
    return jax.nn.softmax(x, axis=axis)

def _gelu(x):
    return jax.nn.gelu(x, approximate=True)

def _silu(x):
    return jax.nn.silu(x)

def _sigmoid(x):
    return jax.nn.sigmoid(x)

def _layernorm(x, axis=-1, eps=1e-05):
    m = jnp.mean(x, axis=axis, keepdims=True)
    v = jnp.var(x, axis=axis, keepdims=True)
    return (x - m) / jnp.sqrt(v + eps)

def _scatter_add(tgt, idx, src, axis=0):
    return tgt.at[idx].add(src)

def _segment_sum(src, seg, n):
    return jax.ops.segment_sum(src, seg, n)
kernel_name = 'mk_adaln_d2_jaxref_r8_a43de1'

def setup_inputs(seed: int=0):
    np.random.seed(seed)
    _w = jnp.asarray

    def _L0_attn_setup():
        import jax, jax.numpy as jnp
        import numpy as np
        B, S, DIM = (2, 256, 256)
        NUM_HEADS, HEAD_DIM, KV_PER = (16, 128, 1)
        NUM_KV = NUM_HEADS * KV_PER
        QKV_OUT = (NUM_HEADS + 2 * NUM_KV) * HEAD_DIM
        key = jax.random.key(seed)
        k1, k2, k3 = jax.random.split(key, 3)
        x = jax.random.normal(k1, (B, S, DIM), dtype=jnp.float32)
        w_qkv = jax.random.normal(k2, (DIM, QKV_OUT), dtype=jnp.float32) * DIM ** (-0.5)
        w_out = jax.random.normal(k3, (NUM_HEADS * HEAD_DIM, DIM), dtype=jnp.float32) * (NUM_HEADS * HEAD_DIM) ** (-0.5)
        return {'x': x, 'w_qkv': w_qkv, 'w_out': w_out}
    _L0_attn_in = _L0_attn_setup()

    def _L0_ffn_setup():
        import jax, jax.numpy as jnp
        import numpy as np
        HIDDEN = 256
        INTER = 688
        LUT_SIZE = 16

        def _ghost_linear(x, idx, lut):
            w = lut[idx]
            return jnp.einsum('bsh,oh->bso', x, w)
        key = jax.random.key(seed)
        k_x, k_lut, k_g, k_u, k_d = jax.random.split(key, 5)
        x = jax.random.normal(k_x, (2, 512, HIDDEN), dtype=jnp.float32)
        lut = jax.random.normal(k_lut, (LUT_SIZE,), dtype=jnp.float32) * 0.02
        gate_idx = jax.random.randint(k_g, (INTER, HIDDEN), 0, LUT_SIZE, dtype=jnp.int32)
        up_idx = jax.random.randint(k_u, (INTER, HIDDEN), 0, LUT_SIZE, dtype=jnp.int32)
        down_idx = jax.random.randint(k_d, (HIDDEN, INTER), 0, LUT_SIZE, dtype=jnp.int32)
        return {'x': x, 'lut': lut, 'gate_idx': gate_idx, 'up_idx': up_idx, 'down_idx': down_idx}
    _L0_ffn_in = _L0_ffn_setup()
    _L0_c = _w((lambda *s: np.random.randn(*s).astype(np.float32) * 0.05)(8, 256))
    _L0_wmod = _w((lambda *s: np.random.randn(*s).astype(np.float32) * 0.05)(256, 6 * 256) * 256 ** (-0.5))

    def _L1_attn_setup():
        import jax, jax.numpy as jnp
        import numpy as np
        import math
        N_EMBED = 256
        N_HEAD = 16
        HEAD_DIM = N_EMBED // N_HEAD // 2
        LAYER = 2
        LAMBDA_INIT = 0.8 - 0.6 * math.exp(-0.3 * (LAYER - 1))
        B, T = (2, 256)
        EPS = 1e-05

        def _causal_sdpa(q, k, v):
            Tq = q.shape[2]
            scale = 1.0 / math.sqrt(q.shape[-1])
            scores = jnp.einsum('bhqd,bhkd->bhqk', q, k) * scale
            mask = jnp.tril(jnp.ones((Tq, Tq), dtype=bool))
            scores = jnp.where(mask, scores, -jnp.inf)
            probs = jax.nn.softmax(scores, axis=-1)
            return jnp.einsum('bhqk,bhkv->bhqv', probs, v)
        key = jax.random.key(seed)
        ks = jax.random.split(key, 7)
        s = 1.0 / math.sqrt(N_EMBED)
        return {'x': jax.random.normal(ks[0], (B, T, N_EMBED), dtype=jnp.float32), 'Wqkv': jax.random.normal(ks[1], (N_EMBED, 3 * N_EMBED), dtype=jnp.float32) * s, 'Wproj': jax.random.normal(ks[2], (N_EMBED, N_EMBED), dtype=jnp.float32) * s, 'lambda_q1': jax.random.normal(ks[3], (HEAD_DIM,), dtype=jnp.float32) * 0.1, 'lambda_k1': jax.random.normal(ks[4], (HEAD_DIM,), dtype=jnp.float32) * 0.1, 'lambda_q2': jax.random.normal(ks[5], (HEAD_DIM,), dtype=jnp.float32) * 0.1, 'lambda_k2': jax.random.normal(ks[6], (HEAD_DIM,), dtype=jnp.float32) * 0.1}
    _L1_attn_in = _L1_attn_setup()

    def _L1_ffn_setup():
        import jax, jax.numpy as jnp
        import numpy as np
        TOP_K = 2
        key = jax.random.key(seed)
        k1, k2, k3, k4 = jax.random.split(key, 4)
        B, S, H, I, E = (2, 128, 256, 176, 8)
        hidden_states = jax.random.normal(k1, (B, S, H), dtype=jnp.float32)
        gate_w = jax.random.normal(k2, (E, H), dtype=jnp.float32) * (1.0 / np.sqrt(H))
        w1 = jax.random.normal(k3, (E, 2 * I, H), dtype=jnp.float32) * (1.0 / np.sqrt(H))
        w2 = jax.random.normal(k4, (E, H, I), dtype=jnp.float32) * (1.0 / np.sqrt(I))
        return {'hidden_states': hidden_states, 'gate_w': gate_w, 'w1': w1, 'w2': w2}
    _L1_ffn_in = _L1_ffn_setup()
    _L1_c = _w((lambda *s: np.random.randn(*s).astype(np.float32) * 0.05)(8, 256))
    _L1_wmod = _w((lambda *s: np.random.randn(*s).astype(np.float32) * 0.05)(256, 6 * 256) * 256 ** (-0.5))
    _d = {'L0_attn_x': _L0_attn_in['x'], 'L0_attn_w_qkv': _L0_attn_in['w_qkv'], 'L0_attn_w_out': _L0_attn_in['w_out'], 'L0_ffn_lut': _L0_ffn_in['lut'], 'L0_ffn_gate_idx': _L0_ffn_in['gate_idx'], 'L0_ffn_up_idx': _L0_ffn_in['up_idx'], 'L0_ffn_down_idx': _L0_ffn_in['down_idx'], 'L0_c': _L0_c, 'L0_wmod': _L0_wmod, 'L1_attn_Wqkv': _L1_attn_in['Wqkv'], 'L1_attn_Wproj': _L1_attn_in['Wproj'], 'L1_attn_lambda_q1': _L1_attn_in['lambda_q1'], 'L1_attn_lambda_k1': _L1_attn_in['lambda_k1'], 'L1_attn_lambda_q2': _L1_attn_in['lambda_q2'], 'L1_attn_lambda_k2': _L1_attn_in['lambda_k2'], 'L1_ffn_gate_w': _L1_ffn_in['gate_w'], 'L1_ffn_w1': _L1_ffn_in['w1'], 'L1_ffn_w2': _L1_ffn_in['w2'], 'L1_c': _L1_c, 'L1_wmod': _L1_wmod}
    _x0 = _d['L0_attn_x']
    _d['L0_attn_x'] = jax.random.normal(jax.random.fold_in(jax.random.key(seed), 1), (8, 256, 256), dtype=_x0.dtype)
    del _x0
    return _d

def reference(L0_attn_x, L0_attn_w_qkv, L0_attn_w_out, L0_ffn_lut, L0_ffn_gate_idx, L0_ffn_up_idx, L0_ffn_down_idx, L0_c, L0_wmod, L1_attn_Wqkv, L1_attn_Wproj, L1_attn_lambda_q1, L1_attn_lambda_k1, L1_attn_lambda_q2, L1_attn_lambda_k2, L1_ffn_gate_w, L1_ffn_w1, L1_ffn_w2, L1_c, L1_wmod):

    def _L0_attn_ref(x, w_qkv, w_out):
        import jax, jax.numpy as jnp
        import numpy as np
        B, S, DIM = (2, 256, 256)
        NUM_HEADS, HEAD_DIM, KV_PER = (16, 128, 1)
        NUM_KV = NUM_HEADS * KV_PER
        QKV_OUT = (NUM_HEADS + 2 * NUM_KV) * HEAD_DIM
        b, s, _ = x.shape
        qkv = (x @ w_qkv).reshape(b, s, NUM_HEADS + 2 * NUM_KV, HEAD_DIM)
        q = qkv[:, :, :NUM_HEADS]
        k = qkv[:, :, NUM_HEADS:NUM_HEADS + NUM_KV]
        v = qkv[:, :, NUM_HEADS + NUM_KV:]
        q = q.reshape(b, s, NUM_KV, KV_PER, HEAD_DIM).transpose(0, 2, 3, 1, 4)
        k = k.transpose(0, 2, 1, 3)
        v = v.transpose(0, 2, 1, 3)
        scale = 1.0 / HEAD_DIM ** 0.5
        logits = jnp.einsum('bkpsd,bktd->bkpst', q, k) * scale
        attn = jax.nn.softmax(logits.astype(jnp.float32), axis=-1)
        combined = jnp.einsum('bkpst,bktd->bkpsd', attn, v.astype(jnp.float32)).astype(v.dtype)
        combined = combined.transpose(0, 3, 1, 2, 4).reshape(b, s, NUM_KV * KV_PER * HEAD_DIM)
        return combined @ w_out

    def _L0_ffn_ref(x, lut, gate_idx, up_idx, down_idx):
        import jax, jax.numpy as jnp
        import numpy as np
        HIDDEN = 256
        INTER = 688
        LUT_SIZE = 16

        def _ghost_linear(x, idx, lut):
            w = lut[idx]
            return jnp.einsum('bsh,oh->bso', x, w)
        gate = _ghost_linear(x, gate_idx, lut)
        up = _ghost_linear(x, up_idx, lut)
        h = jax.nn.silu(gate) * up
        return _ghost_linear(h, down_idx, lut)

    def _L1_attn_ref(x, Wqkv, Wproj, lambda_q1, lambda_k1, lambda_q2, lambda_k2):
        import jax, jax.numpy as jnp
        import numpy as np
        import math
        N_EMBED = 256
        N_HEAD = 16
        HEAD_DIM = N_EMBED // N_HEAD // 2
        LAYER = 2
        LAMBDA_INIT = 0.8 - 0.6 * math.exp(-0.3 * (LAYER - 1))
        B, T = (2, 256)
        EPS = 1e-05

        def _causal_sdpa(q, k, v):
            Tq = q.shape[2]
            scale = 1.0 / math.sqrt(q.shape[-1])
            scores = jnp.einsum('bhqd,bhkd->bhqk', q, k) * scale
            mask = jnp.tril(jnp.ones((Tq, Tq), dtype=bool))
            scores = jnp.where(mask, scores, -jnp.inf)
            probs = jax.nn.softmax(scores, axis=-1)
            return jnp.einsum('bhqk,bhkv->bhqv', probs, v)
        Bx, Tx, Cfull = x.shape
        C = Cfull // 2
        qkv = x @ Wqkv
        q1, k1, q2, k2, v = jnp.split(qkv, [C, 2 * C, 3 * C, 4 * C], axis=-1)

        def heads(t, d):
            return t.reshape(Bx, Tx, N_HEAD, d).transpose(0, 2, 1, 3)
        q1, k1, q2, k2 = (heads(t, HEAD_DIM) for t in (q1, k1, q2, k2))
        v = heads(v, 2 * HEAD_DIM)
        lam = jnp.exp(jnp.dot(lambda_q1, lambda_k1)) - jnp.exp(jnp.dot(lambda_q2, lambda_k2)) + LAMBDA_INIT
        A1 = _causal_sdpa(q1, k1, v)
        A2 = _causal_sdpa(q2, k2, v)
        diff = A1 - lam * A2
        rms = jnp.sqrt(jnp.mean(diff * diff, axis=-1, keepdims=True) + EPS)
        diff = diff / rms
        diff = (1.0 - LAMBDA_INIT) * diff
        out = diff.transpose(0, 2, 1, 3).reshape(Bx, Tx, Cfull)
        return out @ Wproj

    def _L1_ffn_ref(hidden_states, gate_w, w1, w2):
        import jax, jax.numpy as jnp
        import numpy as np
        TOP_K = 2
        B, S, H = hidden_states.shape
        E = gate_w.shape[0]
        T = B * S
        x = hidden_states.reshape(T, H)
        logits = jnp.einsum('th,eh->te', x, gate_w)
        probs = jax.nn.softmax(logits, axis=-1)
        topw, sel = jax.lax.top_k(probs, TOP_K)
        topw = topw / jnp.sum(topw, axis=-1, keepdims=True)
        combine = jnp.zeros((T, E), dtype=x.dtype).at[jnp.arange(T)[:, None], sel].add(topw)
        gate_up = jnp.einsum('th,eoh->eto', x, w1)
        g, u = jnp.split(gate_up, 2, axis=-1)
        act = jax.nn.silu(g) * u
        expert_out = jnp.einsum('eti,ehi->eth', act, w2)
        out = jnp.einsum('eth,te->th', expert_out, combine)
        return out.reshape(B, S, H)
    x = L0_attn_x
    mod = (_silu(L0_c) @ L0_wmod).reshape(L0_c.shape[0], 6, 1, -1)
    sa, ca, ga, sb, cb, gb = (mod[:, 0], mod[:, 1], mod[:, 2], mod[:, 3], mod[:, 4], mod[:, 5])
    ga = (2 * (ga >= 0) - 1) * jnp.maximum(jnp.abs(ga), 0.25)
    gb = (2 * (gb >= 0) - 1) * jnp.maximum(jnp.abs(gb), 0.25)
    h = _layernorm(x, axis=-1) * (1 + ca) + sa
    x = x + ga * _L0_attn_ref(h, L0_attn_w_qkv, L0_attn_w_out)
    h = _layernorm(x, axis=-1) * (1 + cb) + sb
    x = x + gb * _L0_ffn_ref(h, L0_ffn_lut, L0_ffn_gate_idx, L0_ffn_up_idx, L0_ffn_down_idx)
    mod = (_silu(L1_c) @ L1_wmod).reshape(L1_c.shape[0], 6, 1, -1)
    sa, ca, ga, sb, cb, gb = (mod[:, 0], mod[:, 1], mod[:, 2], mod[:, 3], mod[:, 4], mod[:, 5])
    ga = (2 * (ga >= 0) - 1) * jnp.maximum(jnp.abs(ga), 0.25)
    gb = (2 * (gb >= 0) - 1) * jnp.maximum(jnp.abs(gb), 0.25)
    h = _layernorm(x, axis=-1) * (1 + ca) + sa
    x = x + ga * _L1_attn_ref(h, L1_attn_Wqkv, L1_attn_Wproj, L1_attn_lambda_q1, L1_attn_lambda_k1, L1_attn_lambda_q2, L1_attn_lambda_k2)
    h = _layernorm(x, axis=-1) * (1 + cb) + sb
    x = x + gb * _L1_ffn_ref(h, L1_ffn_gate_w, L1_ffn_w1, L1_ffn_w2)
    return x

_drawn_inputs = setup_inputs


def setup_inputs(seed=0):
    import zlib

    import numpy as np

    out = dict(_drawn_inputs(seed))
    spreads = {}
    factors = {'L0_ffn_lut': 4.476,
     'L1_attn_lambda_q1': 35.68,
     'L1_attn_lambda_k1': 64.0,
     'L1_attn_lambda_q2': 8.0,
     'L1_attn_lambda_k2': 8.0}
    for name, (base, spread) in spreads.items():
        noise = np.random.default_rng([zlib.crc32(name.encode()), seed]).standard_normal(out[name].shape)
        drawn = base * np.exp(spread * noise) if base else spread * noise
        out[name] = jnp.asarray(drawn.astype(out[name].dtype))
    for name, factor in factors.items():
        out[name] = (out[name] * factor).astype(out[name].dtype)
    return out
```

```python
from contextlib import ExitStack

import concourse.bass as bass
from concourse import mybir

F32 = mybir.dt.float32
F32R = mybir.dt.float32r
I32 = mybir.dt.int32
ALU = mybir.AluOpType
ACT = mybir.ActivationFunctionType
AX = mybir.AxisListType.X

P = 128
B, T, C = 8, 256, 256
CC = C // P
TT = T // P
H0, D0 = 16, 128
SCALE0 = D0 ** -0.5
LUT, INTER = 16, 688
FK = -(-INTER // P)
FP = FK * P
H1, D1 = 16, 8
SCALE1 = D1 ** -0.5
LAMBDA_INIT = 0.8 - 0.6 * 2.718281828459045 ** (-0.3)
EPS = 1e-5
E1, I1 = 8, 176
EI = E1 * I1
EK = EI // P
NARROW_AT = {0: (1, 0), 2: (1, 1), 4: (2, 0), 6: (2, 1), 8: (3, 0), 10: (3, 1)}
DIFF_AT = 7
PREP_AT = 10
STEPS = 4 * B
OFF = 8
PIECE = 1024
RING = 3
NEG = -(2.0 ** 100)
FLAT_B = 2 * CC * FP + FK * C
SIX = FLAT_B // B
NB = -(-FLAT_B // PIECE)
NGU = -(-2 * CC * EI // PIECE)




def repeat(ap, axis, n):
    ap = ap.unsqueeze(axis)
    shape = list(ap.shape)
    shape[axis] = n
    return ap.broadcast_to(shape)


def program(nc, x_in, c_t0, c_t1, wmod0, wmod1, wqkv0, wout0, lut_b, ffn_idx, w_c, w_vp, lam_v, gatew, w_gu, w_d, out,
            phases=4):
    ctx = ExitStack()
    with ctx:
        def sb(name, shape, dt=F32):
            return ctx.enter_context(nc.sbuf_tensor(name, shape, dt))

        per, ahead = {}, {}

        def sem(name, events=1, head=0):
            made = ctx.enter_context(nc.semaphore(name))
            per[name], ahead[name] = events, head
            names[id(made)] = name
            return made

        def at(s, step, n=0):
            name = names[id(s)]
            return step * per[name] + (n + 1 + ahead[name])

        names = {}

        bank = [ctx.enter_context(nc.psum_tensor(f"bank{i}", [P, 512], F32)) for i in range(8)]
        tr_ps, y_ps = bank[6], bank[7]
        x_dram = nc.dram_tensor("x_steps", ((STEPS + 2) * T, C), F32).ap()
        out_steps = out.rearrange("(s t p) c -> s p t c", t=TT, p=P)
        x_steps = x_dram.rearrange("(s t p) c -> s p t c", t=TT, p=P)

        ident = sb("ident", [P, P])
        raw = sb("raw", [P, RING, PIECE])
        mod = sb("mod", [P, STEPS + 2, 6])
        mod_now = sb("mod_now", [P, 4])
        gate_now = sb("gate_now", [P, 2])
        c_sb = sb("c_sb", [P, 2, CC, B])
        cs = sb("cs", [P, 2, CC, B])
        x_cur = sb("x_cur", [P, TT, C])
        x_next = sb("x_next", [P, TT, C])
        xn = sb("xn", [P, TT, C])
        x_out = xn
        h_f = sb("h_f", [P, CC, T])
        y_t = sb("y_t", [P, CC, T])
        stats = sb("stats", [P, TT, 6])
        mv = sb("mv", [P, TT, 2])
        ve = sb("ve", [P, TT])
        rstd = sb("rstd", [P, TT])
        mhalf = sb("mhalf", [P, 32])
        work = sb("work", [P, 2048])
        probs = work[:, 0:1024].rearrange("p (s t n) -> p s t n", s=2, t=TT)
        nmax = sb("nmax", [P, 2, TT])
        den = sb("den", [P, 2, TT])
        rden = sb("rden", [P, 2, TT])
        warm = sb("warm", [P, 1])
        lut_sb = sb("lut_sb", [P, LUT])
        mask_f = sb("mask_f", [P, P])
        lanes = sb("lanes", [P, 1], I32)
        lane_bit = sb("lane_bit", [P, 2], I32)
        low_q = sb("low_q", [P, 1])
        low_k = sb("low_k", [P, 1])
        lam_sb = sb("lam_sb", [P, 4, D1])
        lam_p = sb("lam_p", [P, 2, D1])
        lam_e = sb("lam_e", [P, 2])
        nlam = sb("nlam", [P, 1])
        nmax1 = sb("nmax1", [P, 2, TT, 2])
        den1 = sb("den1", [P, 2, TT, 2])
        rall = sb("rall", [P, H1, TT, 2])
        rall_old = sb("rall_old", [P, H1, TT])
        ratio = sb("ratio", [P, 2, TT])
        ssum = sb("ssum", [P, 32])
        tri = sb("tri", [P, E1, E1])
        gw_sb = sb("gw_sb", [P, CC, E1])
        r_max = sb("r_max", [P, TT])
        r_e = sb("r_e", [P, TT, E1])
        r_w = sb("r_w", [P, TT, E1])
        r_rank = sb("r_rank", [P, TT, E1])
        r_sum = sb("r_sum", [P, TT])

        W = sb("W", [P, 32768], F32R)
        h = sb("h", [P, 2, CC, T], F32R)
        qk = sb("qk", [P, 2, 2, 2, T], F32R)
        v = sb("v", [P, 2, 2, TT, 512], F32R)
        pt = sb("pt", [P, 2, 2, TT, T], F32R)
        mask_r = sb("mask_r", [P, P], F32R)
        ident_r = sb("ident_r", [P, P], F32R)
        with nc.sbuf_tensor("ot", [P, 4, 2, T], F32R) as ot:
            pass
        spare = sb("spare", [P, 2048])

        WQK = W[:, 0:16384].rearrange("p (l c m n) -> p l c m n", l=2, c=CC, m=2)
        WV = W[:, 16384:24576].rearrange("p (l c n) -> p l c n", l=2, c=CC)
        WO = W[:, 24576:32768].rearrange("p (l h n) -> p l h n", l=2, h=H0)

        WB = W[:, 0:2 * FLAT_B].rearrange("p (l n) -> p l n", l=2)
        WG = WB[:, :, 0:CC * FP].rearrange("p l (c n) -> p l c n", c=CC)
        WU = WB[:, :, CC * FP:2 * CC * FP].rearrange("p l (c n) -> p l c n", c=CC)
        WD = WB[:, :, 2 * CC * FP:FLAT_B].rearrange("p l (k n) -> p l k n", k=FK)
        C0 = 2 * FLAT_B
        WC = W[:, C0:C0 + 8192].rearrange("p (l m c n) -> p l m c n", l=2, m=4, c=CC)
        WVP = W[:, C0 + 8192:C0 + 10240].rearrange("p (l n) -> p l n", l=2)
        WV1 = WVP[:, :, 0:512].rearrange("p l (c n) -> p l c n", c=CC)
        WP1 = WVP[:, :, 512:1024].rearrange("p l (c n) -> p l c n", c=CC)
        G0 = C0 + 10240
        WGU = W[:, G0:G0 + 4 * CC * EI].rearrange("p (l n) -> p l n", l=2)
        WG1 = WGU[:, :, 0:CC * EI].rearrange("p l (c n) -> p l c n", c=CC)
        WU1 = WGU[:, :, CC * EI:2 * CC * EI].rearrange("p l (c n) -> p l c n", c=CC)
        WDD = W[:, 0:2 * EK * C].rearrange("p (l n) -> p l n", l=2)
        WD1 = WDD.rearrange("p l (k n) -> p l k n", k=EK)
        sel = W[0:E1, G0 + 4 * CC * EI:G0 + 4 * CC * EI + EI]
        gur = pt
        def gu_slot(k, part):
            return pt[:, k % 2, part, k // 2 % 2, :]
        sg = work[:, 0:512].rearrange("p (s n) -> p s n", s=2)
        guf = work[:, 512:1024].rearrange("p (s n) -> p s n", s=2)
        pc = work[:, 0:1536].rearrange("p (s m n) -> p s m n", s=2, m=2)
        v1 = work[:, 1536:2048].rearrange("p (t n) -> p t n", t=TT)
        ptf = raw[:, 2, 0:768].rearrange("p (s n) -> p s n", s=2)
        x_early = spare[:, 0:512].rearrange("p (t n) -> p t n", t=TT)
        xn_early = spare[:, 512:1024].rearrange("p (t n) -> p t n", t=TT)
        square = spare[:, 1024:1536].rearrange("p (t n) -> p t n", t=TT)
        dr = pt[:, 0]
        comb = work[:, 1024:1280].rearrange("p (t n) -> p t n", t=TT)
        r_gt = work[:, 1280:1408].rearrange("p (t e j) -> p t e j", t=TT, e=E1)
        r_eq = work[:, 1408:1536].rearrange("p (t e j) -> p t e j", t=TT, e=E1)
        comb_r = qk[0:E1, 0, :, 0, :]

        s_const = sem("s_const")
        s_pool = sem("s_pool")
        raw_in = [sem(f"raw_in{i}") for i in range(RING)]
        raw_used = sem("raw_used")
        raw_hi = sem("raw_hi")
        c_in = sem("c_in")
        c_silu = sem("c_silu")
        mod_ps = sem("mod_ps")
        mod_set = sem("mod_set")
        x_first = sem("x_first")
        x_copy = sem("x_copy")
        x_load = sem("x_load", 16, 16)
        x_store = sem("x_store", 16, 16)
        dchain = sem("dchain")
        mod_cp = sem("mod_cp")
        var_ok = sem("var_ok")
        rstd_ok = sem("rstd_ok")
        xn_ok = sem("xn_ok")
        xnt_full = sem("xnt_full")
        h_hi = sem("h_hi")
        h_high = sem("h_high")
        h_ok = sem("h_ok")
        y_full = sem("y_full", 1, -B)
        y_ev = sem("y_ev", 1, OFF)
        yt_full = sem("yt_full")
        x_moved = sem("x_moved", 1, OFF)
        gate_ok = sem("gate_ok")
        p_carrier = sem("p_carrier")
        carrier = sem("carrier")
        sp_carrier = sem("sp_carrier")
        dcom2 = sem("dcom2")
        dcom = sem("dcom")

        block = ctx.enter_context(nc.Block())

        def cols(w, lo, n):
            return w.rearrange("(c p) n -> p c n", p=P)[:, :, lo:lo + n]

        pieces = []
        for w in (wmod0, wmod1):
            for k in range(3):
                pieces.append((cols(w, 512 * k, 512), CC))
        N_MOD = len(pieces)
        for g in range(4):
            for m in range(3):
                pieces.append((cols(wqkv0, m * H0 * D0 + 512 * g, 512), CC))
        for g in range(4):
            pieces.append((wout0[512 * g:512 * (g + 1), :].rearrange("(h p) n -> p h n", p=P), 4))
        N_A = len(pieces)

        def slot(n, dim):
            return raw[:, n % RING, :].rearrange("p (c n) -> p c n", c=dim)

        flat = raw[:, :, :].rearrange("p s n -> p (s n)")
        idx = flat[:, 0:SIX].bitcast(I32)
        decoded = flat[:, SIX:2 * SIX]

        def entries(j):
            return decoded if j == 0 else flat[:, (2 + j % 3) * SIX:(3 + j % 3) * SIX]

        def wa(n, part):
            k = n - N_MOD
            if k < 12:
                g, m = k // 3, k % 3
                if m < 2:
                    return WQK[:, part, :, m, 512 * g:512 * (g + 1)]
                return WV[:, part, :, 512 * g:512 * (g + 1)]
            return WO[:, part, 4 * (k - 12):4 * (k - 11), :]

        qk_full, qk_hi, qk_lo = sem("qk_full", H0), sem("qk_hi", H0), sem("qk_lo", H0, OFF)
        s_full, s_max, s_exp = sem("s_full", H0), sem("s_max", H0), sem("s_exp", H0, OFF)
        s_rden, s_norm = sem("s_rden", H0), sem("s_norm", H0)
        pt_full, pt_hi, pt_lo = sem("pt_full", H0), sem("pt_hi", H0), sem("pt_lo", H0, OFF)
        o_full, o_hi, o_lo = sem("o_full", H0), sem("o_hi", H0), sem("o_lo", H0, OFF)
        v_full, v_hi, v_lo = sem("v_full", 8), sem("v_hi", 8), sem("v_lo", 8, OFF)
        proj_done = sem("proj_done", H0, OFF)

        ffn_w = nc.dram_tensor("ffn_w", (P, FLAT_B), F32).ap()
        raw2_in = [sem(f"raw2_in{i}") for i in range(RING)]
        raw2_used = sem("raw2_used")
        small_in = sem("small_in")
        idx_in, dec_out = sem("idx_in"), sem("dec_out")
        entry = sem("entry", LUT, OFF)
        pchain = sem("pchain", LUT - 1, OFF)
        pchain2 = sem("pchain2")
        bc_hi = sem("bc_hi")
        wc_ok, wd_ok, lam_ok, lam_exp, lane_ok = (sem(n) for n in ("wc_ok", "wd_ok", "lam_ok", "lam_exp", "lane_ok"))
        gu_full, gu_silu, gu_mul = sem("gu_full", FK), sem("gu_silu", FK), sem("gu_mul", FK, OFF)
        gu_hi, gu_lo, down_done = sem("gu_hi", FK), sem("gu_lo", FK, OFF), sem("down_done", FK - 1)
        eg_full, eg_silu, eg_up, eg_mul = sem("eg_full", EK), sem("eg_silu", EK), sem("eg_up", EK), sem("eg_mul", EK, OFF)
        eg_hi, eg_lo, edown = sem("eg_hi", EK), sem("eg_lo", EK, OFF), sem("edown", EK - 1)
        bc_full = sem("bc_full", EK)
        lg_full, lg_max, lg_exp, cb_ok, cbt_full, cb_hi, cb_lo = (
            sem("lg_full"), sem("lg_max"), sem("lg_exp"), sem("cb_ok"), sem("cbt_full"), sem("cb_hi"), sem("cb_lo", 1, OFF))
        dr_chain = sem("dr_chain", 7)
        v1_full, v1_ok = sem("v1_full"), sem("v1_ok", 1, OFF)
        c_full, c_hi, c_ok = sem("c_full", 8), sem("c_hi", 8), sem("c_ok", 8, OFF)
        e_full, e_max, e_exp, e_diff = sem("e_full", H1), sem("e_max", H1), sem("e_exp", H1, OFF), sem("e_diff", H1)
        e_rec, e_rat = sem("e_rec", H1), sem("e_rat", H1)
        t_full, t_ok, av_done = sem("t_full", H1), sem("t_ok", H1, OFF), sem("av_done", H1, OFF)
        rms_in, rms_ok, d_ok, dt_full, dr_hi, dr_lo = (sem(n) for n in ("rms_in", "rms_ok", "d_ok", "dt_full", "dr_hi", "dr_lo"))
        early_in = sem("early_in", 16)
        d_chain, d_square, r_moved, d_read = sem("d_chain"), sem("d_square"), sem("r_moved"), sem("d_read", 1, OFF)

        def narrow_ps(g, m):
            return tr_ps if (g, m) == (0, 1) else bank[0]

        @block.sync
        def _(sp):
            sp.sem_inc(x_store, 16)
            sp.sem_inc(x_load, 16)
            x9 = x_in.rearrange("(s t p) c -> s p t c", t=TT, p=P)
            sp.dma_start(x_cur[:, :, :], x9[0]).then_inc(x_first, 16)
            for n in range(N_A):
                src, dim = pieces[n]
                if RING <= n < RING + N_MOD:
                    sp.wait_ge(mod_ps, n - RING + 1)
                elif n >= RING:
                    sp.wait_ge(raw_used, n - RING - N_MOD + 1)
                sp.dma_start(slot(n, dim), src).then_inc(raw_in[n % RING], 16)
                if n == RING:
                    sp.dma_start(x_next[:, :, :], x9[1]).then_inc(x_first, 16)
            sp.wait_ge(x_copy, 32)
            for first, last in ((0, min(3, phases) * B), (3 * B, phases * B)):
                if first == last or phases < 4 and first:
                    continue
                to = x_steps if first == 0 else None
                with sp.Fori(first, last) as s:
                    sp.wait_ge(x_moved, at(x_moved, s))
                    sp.sem_inc(sp_carrier, 1)
                    dst = x_steps[s + B] if first == 0 else out_steps[s - 3 * B]
                    sp.dma_start(dst, x_out[:, :, :]).then_inc(x_store, 16)
                    sp.dma_start(x_next[:, :, :], x_steps[s + 2]).then_inc(x_load, 16)
                    sp.wait_ge(x_store, at(x_store, s, 15))
                    sp.sem_inc(sp_carrier, 1)
            if phases < 4:
                sp.dma_start(out, x_dram[8 * phases * T:8 * (phases + 1) * T, :]).then_inc(x_first, 16)
                sp.wait_ge(x_first, 48)
            sp.wait_ge(x_load, 16 * 8 * phases + 16)

        @block.gpsimd
        def _(pool):
            pool.dma_start(x_dram[0:B * T, :], x_in[0:B * T, :]).then_inc(x_copy, 16)
            pool.dma_start(x_dram[STEPS * T:(STEPS + 2) * T, :], x_in[0:2 * T, :]).then_inc(x_copy, 16)
            nc.gpsimd.memset(ident[:, :], 0.0).then_inc(s_pool, 1)
            nc.gpsimd.memset(mhalf[:, :], -0.5).then_inc(s_pool, 1)
            pool.wait_ge(s_pool, 2)
            nc.gpsimd.affine_select(out=ident[:, :], in_=ident[:, :], compare_op=ALU.not_equal, fill=1.0, base=0,
                                    pattern=[[-1, P]], channel_multiplier=1).then_inc(s_const, 1)

            pool.sem_inc(pchain, OFF)

            def rstd_stage(s):
                pool.wait_ge(var_ok, at(var_ok, s))
                nc.gpsimd.tensor_tensor(rstd[:, :], ve[:, :], mhalf[:, 0:TT], ALU.pow).then_inc(rstd_ok, 1)

            nc.gpsimd.memset(mask_f[:, :], 0.0).then_inc(s_pool, 1)
            nc.gpsimd.memset(tri[:, :, :], 0.0).then_inc(s_pool, 1)
            nc.gpsimd.iota(lanes[:, :], [[0, 1]], base=0, channel_multiplier=1).then_inc(lane_ok, 1)
            pool.wait_ge(s_pool, 4)
            nc.gpsimd.affine_select(out=mask_f[:, :], in_=mask_f[:, :], compare_op=ALU.is_ge, fill=NEG, base=0,
                                    pattern=[[-1, P]], channel_multiplier=1).then_inc(lane_ok, 1)
            nc.gpsimd.affine_select(out=tri[:, :, :], in_=tri[:, :, :], compare_op=ALU.is_ge, fill=1.0, base=0,
                                    pattern=[[-1, E1], [1, E1]], channel_multiplier=0).then_inc(lane_ok, 1)
            pool.dma_start(lut_sb[:, :], lut_b).then_inc(small_in, 16)
            pool.dma_start(lam_sb[:, :, :].rearrange("p a b -> p (a b)"), lam_v).then_inc(small_in, 16)
            pool.dma_start(gw_sb[:, :, :].rearrange("p a b -> p (a b)"), gatew).then_inc(small_in, 16)
            pool.wait_ge(small_in, 48)
            rstd_stage(0)
            pool.wait_ge(raw_used, N_A - N_MOD)
            ffn_parts = ffn_idx.rearrange("p (b n) -> b p n", b=B + 1)
            pool.dma_start(idx, ffn_parts[0]).then_inc(idx_in, 16)
            with pool.Fori(0, B) as b:
                for j in range(1, LUT):
                    pool.wait_ge(entry, at(entry, b, j))
                    if j > 1:
                        pool.sem_inc(p_carrier, 1)
                        pool.wait_ge(pchain, at(pchain, b, j - 2))
                    nc.gpsimd.tensor_tensor(decoded, decoded, entries(j), ALU.add).then_inc(pchain, 1)
                pool.wait_ge(pchain, at(pchain, b, LUT - 2))
                pool.sem_inc(p_carrier, 1)
                pool.dma_start(ffn_w.rearrange("p (b n) -> b p n", b=B)[b], decoded).then_inc(dec_out, 16)
                pool.dma_start(idx, ffn_parts[b + 1]).then_inc(idx_in, 16)
                pool.wait_ge(dec_out, b * 16 + 16)
                pool.sem_inc(p_carrier, 1)
                rstd_stage(b + 1)

            if phases > 1:
                def load2(n, src, width):
                    pool.dma_start(raw[:, n % RING, 0:width], src).then_inc(raw2_in[n % RING], 16)

                pool.wait_ge(idx_in, 16 * (B + 1))
                for n in range(NB):
                    if n >= RING:
                        pool.wait_ge(raw2_used, n - RING + 1)
                    load2(n, ffn_w[:, n * PIECE:min((n + 1) * PIECE, FLAT_B)], min(PIECE, FLAT_B - n * PIECE))
                chain = [0]

                def link(ins):
                    chain[0] += 1
                    ins.then_inc(pchain2, 1)
                    pool.wait_ge(pchain2, chain[0])

                def split_flat(n, dst, lo, width, done):
                    link(nc.gpsimd.tensor_copy(dst[:, 0, lo:lo + width], raw[:, n % RING, 0:width]))
                    link(nc.gpsimd.tensor_tensor(dst[:, 1, lo:lo + width], raw[:, n % RING, 0:width],
                                                 dst[:, 0, lo:lo + width].bitcast(F32), ALU.subtract))
                    pool.sem_inc(done, 1)

                pool.wait_ge(raw2_used, NB)
                pool.wait_ge(proj_done, at(proj_done, B - 1, H0 - 1))
                load2(NB, w_c, 1024)
                load2(NB + 1, w_vp, 1024)
                later = [(w_gu, n * PIECE, min(PIECE, 2 * CC * EI - n * PIECE)) for n in range(NGU)]
                for b in range(B):
                    if b == 0:
                        n = NB
                        pool.wait_ge(raw2_in[n % RING], 16 * (n // RING + 1))
                        q = raw[:, n % RING, :].rearrange("p (m c n) -> p m c n", m=4, c=CC)
                        for m in (0, 2):
                            link(nc.gpsimd.tensor_scalar(q[:, m], q[:, m], SCALE1, None, ALU.mult))
                    if b in (0, 1):
                        for m in (2 * b, 2 * b + 1):
                            for c in range(CC):
                                src = repeat(q[:, m, c].rearrange("p (h d) -> p h d", d=D1), 2, 4)
                                hi = WC[:, 0, m, c].rearrange("p (h r d) -> p h r d", r=4, d=D1)
                                lo = WC[:, 1, m, c].rearrange("p (h r d) -> p h r d", r=4, d=D1)
                                link(nc.gpsimd.tensor_copy(hi, src))
                                link(nc.gpsimd.tensor_tensor(lo, src, hi.bitcast(F32), ALU.subtract))
                        pool.sem_inc(wc_ok, 1)
                    if b == 2:
                        n = NB + 1
                        load2(NB + 2, *[w_gu[:, 0:PIECE], PIECE])
                        pool.wait_ge(raw2_in[n % RING], 16 * (n // RING + 1))
                        split_flat(n, WVP, 0, 1024, wc_ok)
                    if b >= 2:
                        k = b - 2
                        n = NB + 2 + k
                        if k + 1 < NGU:
                            load2(n + 1, w_gu[:, (k + 1) * PIECE:min((k + 2) * PIECE, 2 * CC * EI)],
                                  min(PIECE, 2 * CC * EI - (k + 1) * PIECE))
                        pool.wait_ge(raw2_in[n % RING], 16 * (n // RING + 1))
                        split_flat(n, WGU, k * PIECE, later[k][2], wd_ok)
                    rstd_stage(B + b + 1)
            if phases > 2:
                pool.wait_ge(y_full, at(y_full, 2 * B - 1))
                for b in range(B + 1):
                    if b < B:
                        pool.wait_ge(xn_ok, at(xn_ok, 2 * B + b))
                        pool.wait_ge(x_store, at(x_store, B + b + 1, 15))
                        pool.dma_start(x_early, x_steps[2 * B + b + 1]).then_inc(early_in, 16)
                    if b:
                        pool.wait_ge(d_read, at(d_read, b - 1))
                        nc.gpsimd.tensor_tensor(square[:, :, :], y_t[:, :, :], y_t[:, :, :], ALU.mult
                                                ).then_inc(d_square, 1)
                        pool.wait_ge(rms_in, at(rms_in, b - 1))
                        nc.gpsimd.tensor_tensor(ssum[:, :], ssum[:, :], mhalf[:, :], ALU.pow).then_inc(rms_ok, 1)
                        pool.wait_ge(rms_ok, at(rms_ok, b - 1))
                        yv = y_t[:, :, :].rearrange("p t (h d) -> p t h d", h=H1)
                        rr = repeat(ssum[:, :].rearrange("p (t h) -> p t h", t=TT), 3, 16)
                        nc.gpsimd.tensor_tensor(yv, yv, rr, ALU.mult).then_inc(d_ok, 1)
                    if b == 0:
                        link(nc.gpsimd.memset(flat[0:E1, 0:EI], 1.0))
                        for cmp, base, sign in ((ALU.is_ge, 0, 1), (ALU.is_ge, I1 - 1, -1)):
                            link(nc.gpsimd.affine_select(out=flat[0:E1, 0:EI], in_=flat[0:E1, 0:EI], compare_op=cmp,
                                                         fill=0.0, base=base, pattern=[[sign, EI]],
                                                         channel_multiplier=-sign * I1))
                        link(nc.gpsimd.tensor_copy(sel, flat[0:E1, 0:EI]))
                    if 1 <= b <= 3:
                        lo = (b - 1) * PIECE
                        width = min(PIECE, EK * C - lo)
                        pool.dma_start(raw[:, b % 2, 0:width], w_d[:, lo:lo + width]).then_inc(idx_in, 16)
                        pool.wait_ge(idx_in, 16 * (B + 1 + b))
                        link(nc.gpsimd.tensor_copy(WDD[:, 0, lo:lo + width], raw[:, b % 2, 0:width]))
                        link(nc.gpsimd.tensor_tensor(WDD[:, 1, lo:lo + width], raw[:, b % 2, 0:width],
                                                     WDD[:, 0, lo:lo + width].bitcast(F32), ALU.subtract))
                        pool.sem_inc(wd_ok, 1)
                    if b < B:
                        rstd_stage(2 * B + b + 1)
            if phases > 3:
                with pool.Fori(3 * B, 4 * B) as s:
                    rstd_stage(s + 1)

        @block.scalar
        def _(act):
            act.sem_inc(s_exp, OFF)
            act.sem_inc(e_exp, OFF)
            act.sem_inc(t_ok, OFF)
            act.sem_inc(v1_ok, OFF)
            act.sem_inc(y_ev, OFF)
            act.dma_start(c_sb[:, 0], c_t0.rearrange("(c p) b -> p c b", p=P)).then_inc(c_in, 16)
            act.dma_start(c_sb[:, 1], c_t1.rearrange("(c p) b -> p c b", p=P)).then_inc(c_in, 16)
            act.wait_ge(c_in, 32)
            nc.scalar.activation(cs[:, :, :, :], c_sb[:, :, :, :], ACT.Silu).then_inc(c_silu, 1)
            for n in range(N_MOD, N_A):
                dim = pieces[n][1]
                act.wait_ge(raw_in[n % RING], 16 * (n // RING + 1))
                k = n - N_MOD
                act.activation(wa(n, 0), slot(n, dim), ACT.Copy,
                               scale=SCALE0 if k < 12 and k % 3 == 0 else 1.0).then_inc(raw_hi, 1)

            def prep(s):
                act.wait_ge(xnt_full, at(xnt_full, s))
                act.wait_ge(mod_cp, at(mod_cp, s))
                for c in range(CC):
                    last = nc.scalar.activation(h_f[:, c, :], tr_ps[:, c * T:(c + 1) * T], ACT.Identity,
                                                bias=mod_now[:, c:c + 1], scale=mod_now[:, 2 + c:3 + c])
                last.then_inc(h_hi, 1)

            def finish(s, y_ps=y_ps, of_heads=False):
                if of_heads:
                    act.wait_ge(proj_done, at(proj_done, s, H0 - 1))
                else:
                    act.wait_ge(y_full, at(y_full, s))
                act.wait_ge(gate_ok, at(gate_ok, s))
                for c in range(CC):
                    last = nc.scalar.activation(y_t[:, c, :], y_ps[:, c * T:(c + 1) * T], ACT.Copy,
                                                scale=gate_now[:, c:c + 1])
                last.then_inc(y_ev, 1)

            prep(0)
            act.wait_ge(lam_ok, 1)
            nc.scalar.activation(lam_e[:, :], lam_e[:, :], ACT.Exp).then_inc(lam_exp, 1)

            def head_step(b, i, cur=True, prev=True):
                if cur:
                    act.wait_ge(qk_full, at(qk_full, b, i))
                    nc.scalar.activation(qk[:, i % 2, 0].rearrange("p m n -> p (m n)"), bank[i % 2][:, :], ACT.Copy
                                         ).then_inc(qk_hi, 1)
                if cur and i == H0 - 1:
                    prep(b + 1)
                n = i - 3
                if n >= 0 and cur or n < 0 and prev:
                    act.wait_ge(o_full, at(o_full, b, n))
                    act.wait_ge(proj_done, at(proj_done, b, n - 4))
                    nc.scalar.activation(ot[:, n % 4, 0, :], bank[4][:, 0:T], ACT.Copy).then_inc(o_hi, 1)
                n = i - 1
                if n >= 0 and cur or n < 0 and prev:
                    act.wait_ge(s_max, at(s_max, b, n))
                    for t in range(TT):
                        last = nc.scalar.activation(probs[:, n % 2, t, :], bank[2][:, t * T:(t + 1) * T], ACT.Exp,
                                                    bias=nmax[:, n % 2, t:t + 1], accum_out=den[:, n % 2, t:t + 1])
                    last.then_inc(s_exp, 1)
                if cur and i % 2 == 0:
                    act.wait_ge(v_full, at(v_full, b, i // 2))
                    nc.scalar.activation(v[:, i // 4 % 2, 0, i // 2 % 2, :], bank[5][:, :], ACT.Copy).then_inc(v_hi, 1)
                n = i - 2
                if n >= 0 and cur or n < 0 and prev:
                    act.wait_ge(pt_full, at(pt_full, b, n))
                    nc.scalar.activation(pt[:, n % 2, 0].rearrange("p t n -> p (t n)"), bank[3][:, :], ACT.Copy
                                         ).then_inc(pt_hi, 1)
                if i == 3 and prev:
                    finish(b - 1, of_heads=True)

            nc.scalar.activation(warm[:, :], mhalf[:, 0:1], ACT.Exp)
            for i in range(H0):
                head_step(0, i, prev=False)
            with act.Fori(1, B) as b:
                for i in range(H0):
                    head_step(b, i)
            for i in range(4):
                head_step(B, i, cur=False)

            if phases > 1:
                for n in range(NB):
                    lo, width = n * PIECE, min(PIECE, FLAT_B - n * PIECE)
                    act.wait_ge(raw2_in[n % RING], 16 * (n // RING + 1))
                    nc.scalar.activation(WB[:, 0, lo:lo + width], raw[:, n % RING, 0:width], ACT.Copy).then_inc(bc_hi, 1)
                with act.Fori(0, B) as b:
                    for k in range(FK + 1):
                        if k < FK:
                            act.wait_ge(gu_full, at(gu_full, b, k))
                            nc.scalar.activation(sg[:, k % 2, :], bank[k % 4][:, 0:T], ACT.Silu).then_inc(gu_silu, 1)
                        if k == FK - 1:
                            prep(b + B + 1)
                        if k >= 1:
                            act.wait_ge(gu_mul, at(gu_mul, b, k - 1))
                            if k >= 5:
                                act.wait_ge(down_done, at(down_done, b, k - 5))
                            nc.scalar.activation(gu_slot(k - 1, 0), guf[:, (k - 1) % 2, :], ACT.Copy).then_inc(gu_hi, 1)
                    finish(b + B)

            if phases > 2:
                nc.scalar.activation(warm[:, :], mhalf[:, 0:1], ACT.Exp)
                def narrow(b, g, m):
                    act.wait_ge(c_full, at(c_full, b, 2 * g + m))
                    nc.scalar.activation(qk[:, m, 0].rearrange("p x n -> p (x n)"), narrow_ps(g, m)[:, :], ACT.Copy
                                         ).then_inc(c_hi, 1)

                def head_step(b, i, cur=True, prev=True, following=True):
                    n = i - 2
                    if n >= 0 and cur or n < 0 and prev:
                        act.wait_ge(t_full, at(t_full, b, n))
                        act.wait_ge(av_done, at(av_done, b, n - 2))
                        nc.scalar.activation(ptf[:, n % 2, :], bank[4][:, 0:384], ACT.Copy).then_inc(t_ok, 1)
                    if i == 2 and cur:
                        act.wait_ge(v1_full, at(v1_full, b))
                        act.wait_ge(av_done, at(av_done, b - 1, H1 - 1))
                        nc.scalar.activation(v1[:, :, :].rearrange("p t n -> p (t n)"), tr_ps[:, :], ACT.Copy
                                             ).then_inc(v1_ok, 1)
                    if cur and i in NARROW_AT:
                        narrow(b, *NARROW_AT[i])
                    if i == 15 and following:
                        narrow(b + 1, 0, 1)
                    if i == PREP_AT + 2 and cur:
                        prep(b + 2 * B + 1)
                    if cur:
                        act.wait_ge(e_max, at(e_max, b, i))
                        for t in range(TT):
                            keys = (t + 1) * P
                            ps = bank[(1, 3)[i % 2] if t else (2, 5)[i % 2]]
                            for m in range(2):
                                last = nc.scalar.activation(pc[:, i % 2, m, t * P:t * P + keys],
                                                            ps[:, m * keys:(m + 1) * keys], ACT.Exp,
                                                            bias=nmax1[:, i % 2, t, m:m + 1],
                                                            accum_out=den1[:, i % 2, t, m:m + 1])
                        last.then_inc(e_exp, 1)
                    if i == DIFF_AT + 2 and prev:
                        finish(b + 2 * B - 1, tr_ps)
                    if i == 13 and following:
                        narrow(b + 1, 0, 0)
                    if i == DIFF_AT and prev:
                        act.wait_ge(dt_full, at(dt_full, b - 1))
                        nc.scalar.activation(dr[:, 0].rearrange("p c n -> p (c n)"), tr_ps[:, :], ACT.Copy
                                             ).then_inc(dr_hi, 1)

                narrow(0, 0, 0)
                narrow(0, 0, 1)
                for i in range(H1):
                    head_step(0, i, prev=False)
                with act.Fori(1, B - 1) as b:
                    for i in range(H1):
                        head_step(b, i)
                for i in range(H1):
                    head_step(B - 1, i, following=False)
                for i in range(DIFF_AT + 4):
                    head_step(B, i, cur=False, following=False)

            if phases > 3:
                with act.Fori(0, B) as b:
                    act.wait_ge(lg_max, at(lg_max, b))
                    for t in range(TT):
                        last = nc.scalar.activation(r_e[:, t, :], bank[3][:, t * E1:(t + 1) * E1], ACT.Exp,
                                                    bias=r_max[:, t:t + 1])
                    last.then_inc(lg_exp, 1)
                    for k in range(EK + 1):
                        if k < EK:
                            act.wait_ge(eg_full, at(eg_full, b, k))
                            nc.scalar.activation(sg[:, k % 2, :], bank[k % 3][:, 0:T], ACT.Silu).then_inc(eg_silu, 1)
                        if k == 0:
                            act.wait_ge(cbt_full, at(cbt_full, b))
                            nc.scalar.activation(comb_r[:, 0], bank[3][0:E1, 0:T], ACT.Copy).then_inc(cb_hi, 1)
                        if k == EK - 1:
                            prep(b + 3 * B + 1)
                        if k >= 1:
                            act.wait_ge(eg_mul, at(eg_mul, b, k - 1))
                            if k >= 5:
                                act.wait_ge(edown, at(edown, b, k - 5))
                            nc.scalar.activation(gu_slot(k - 1, 0), guf[:, (k - 1) % 2, :], ACT.Copy).then_inc(eg_hi, 1)
                    finish(b + 3 * B)

        @block.vector
        def _(dve):
            seq = [0]

            def link(ins):
                seq[0] += 1
                ins.then_inc(dchain, 1)
                dve.wait_ge(dchain, seq[0])

            for s_ in (qk_lo, pt_lo, o_lo, v_lo, x_moved, d_read, entry, gu_lo, eg_lo, gu_mul, eg_mul, c_ok, cb_lo):
                dve.sem_inc(s_, OFF)
            link(nc.vector.memset(mod[:, STEPS:, :], 0.0))
            for l in range(2):
                dve.wait_ge(mod_ps, 3 * (l + 1))
                src = bank[l][:, 0:96].rearrange("p (u k b) -> p u b k", u=2, k=6)
                for u in range(2):
                    last = nc.vector.tensor_copy(mod[:, 16 * l + 8 * u:16 * l + 8 * u + 8, :], src[:, u])
                link(last)
            link(nc.vector.tensor_scalar(mod[:, :, 2:4], mod[:, :, 2:4], 1.0, None, ALU.add))
            gt = probs[:, 0].rearrange("p t n -> p (t n)")[:, 0:2 * (STEPS + 2)].rearrange("p (s k) -> p s k", k=2)
            ga = mod[:, :, 4:6]
            link(nc.vector.tensor_scalar(gt, ga, 0.0, 2.0, ALU.is_ge, ALU.mult))
            link(nc.vector.tensor_scalar(gt, gt, -1.0, None, ALU.add))
            link(nc.vector.tensor_tensor(ga, ga, gt, ALU.mult))
            link(nc.vector.tensor_scalar(ga, ga, 0.25, None, ALU.max))
            link(nc.vector.tensor_tensor(ga, ga, gt, ALU.mult))
            dve.wait_ge(x_first, 32)
            dve.wait_ge(lane_ok, 3)
            for x in range(2):
                last = nc.vector.tensor_scalar(lane_bit[:, x:x + 1], lanes[:, :], (16, 8)[x], None, ALU.bitwise_and)
            link(last)
            nc.vector.tensor_scalar(low_q[:, :], lane_bit[:, 0:1], -1.0 / 16, None, ALU.mult)
            nc.vector.tensor_scalar(low_k[:, :], lane_bit[:, 1:2], -1.0 / 8, None, ALU.mult)
            nc.vector.tensor_copy(mask_r[:, :], mask_f[:, :])
            dve.wait_ge(s_const, 1)
            link(nc.vector.tensor_copy(ident_r[:, :], ident[:, :]))
            dve.wait_ge(small_in, 48)
            link(nc.vector.tensor_tensor(lam_p[:, :, :], lam_sb[:, 0::2, :], lam_sb[:, 1::2, :], ALU.mult))
            nc.vector.tensor_reduce(lam_e[:, :], lam_p[:, :, :], AX, ALU.add).then_inc(lam_ok, 1)

            for n in range(N_MOD, N_A):
                dim = pieces[n][1]
                k = n - N_MOD
                dve.wait_ge(raw_hi, k + 1)
                nc.vector.scalar_tensor_tensor(out=wa(n, 1), in0=slot(n, dim),
                                               scalar=SCALE0 if k < 12 and k % 3 == 0 else 1.0,
                                               in1=wa(n, 0).bitcast(F32), op0=ALU.mult,
                                               op1=ALU.subtract).then_inc(raw_used, 1)

            def prep_stats(s, x):
                n = [0]

                def step_link(ins):
                    n[0] += 1
                    ins.then_inc(dcom, 1)
                    dve.wait_ge(dcom, s * 2 + n[0])

                nc.vector.tensor_copy(mod_now[:, :], mod[:, s, 0:4]).then_inc(mod_cp, 1)
                for t in range(TT):
                    last = nc.vector.bn_stats(stats[:, t, :], x[:, t, :])
                step_link(last)
                dve.sem_inc(carrier, 1)
                for t in range(TT):
                    last = nc.vector.bn_aggr(mv[:, t, :], stats[:, t, :])
                step_link(last)
                nc.vector.tensor_scalar(ve[:, :], mv[:, :, 1], EPS, None, ALU.add).then_inc(var_ok, 1)

            def prep_apply(s, x, xn=xn):
                if xn is x_out:
                    dve.wait_ge(x_store, at(x_store, s - 2, 15))
                    dve.sem_inc(carrier, 1)
                dve.wait_ge(rstd_ok, at(rstd_ok, s))
                for t in range(TT):
                    last = nc.vector.tensor_scalar(xn[:, t, :], x[:, t, :], mv[:, t, 0:1], rstd[:, t:t + 1],
                                                   ALU.subtract, ALU.mult)
                last.then_inc(xn_ok, 1)

            def prep(s, x):
                prep_stats(s, x)
                prep_apply(s, x)

            def prep_low(s):
                dve.wait_ge(h_hi, at(h_hi, s))
                nc.vector.tensor_copy(h[:, 0], h_f[:, :, :]).then_inc(h_high, 1)
                dve.wait_ge(h_high, at(h_high, s))
                nc.vector.tensor_tensor(h[:, 1], h_f[:, :, :], h[:, 0].bitcast(F32), ALU.subtract).then_inc(h_ok, 1)

            def gate(s):
                dve.wait_ge(y_ev, at(y_ev, s - 1))
                nc.vector.tensor_copy(gate_now[:, :], mod[:, s, 4:6]).then_inc(gate_ok, 1)

            def finish(s, late=False):
                dve.wait_ge(yt_full, at(yt_full, s))
                if late:
                    dve.wait_ge(x_load, at(x_load, s - 1, 15))
                    dve.sem_inc(carrier, 1)
                    dve.wait_ge(x_store, at(x_store, s - 1, 15))
                    dve.sem_inc(carrier, 1)
                nc.vector.tensor_tensor(x_out[:, :, :], x_cur[:, :, :],
                                        tr_ps[:, :].rearrange("p (t n) -> p t n", t=TT), ALU.add).then_inc(dcom2, 1)
                dve.wait_ge(dcom2, at(dcom2, s))
                nc.vector.tensor_copy(x_cur[:, :, :], x_next[:, :, :]).then_inc(x_moved, 1)

            prep(0, x_cur)
            prep_low(0)
            dve.wait_ge(lam_exp, 1)
            link(nc.vector.tensor_tensor(nlam[:, :], lam_e[:, 1:2], lam_e[:, 0:1], ALU.subtract))
            link(nc.vector.tensor_scalar(nlam[:, :], nlam[:, :], -LAMBDA_INIT, None, ALU.add))

            def head_step(b, i, cur=True, prev=True):
                if cur:
                    dve.wait_ge(qk_hi, at(qk_hi, b, i))
                    nc.vector.tensor_tensor(qk[:, i % 2, 1].rearrange("p m n -> p (m n)"), bank[i % 2][:, :],
                                            qk[:, i % 2, 0].rearrange("p m n -> p (m n)").bitcast(F32),
                                            ALU.subtract).then_inc(qk_lo, 1)
                if cur and i == H0 - 1:
                    prep_low(b + 1)
                n = i - 1
                if n >= 0 and cur or n < 0 and prev:
                    dve.wait_ge(s_full, at(s_full, b, n))
                    nc.vector.tensor_reduce(nmax[:, n % 2, :], bank[2][:, :].rearrange("p (t n) -> p t n", t=TT),
                                            AX, ALU.max, negate=True).then_inc(s_max, 1)
                n = i - 3
                if n >= 0 and cur or n < 0 and prev:
                    dve.wait_ge(o_hi, at(o_hi, b, n))
                    nc.vector.tensor_tensor(ot[:, n % 4, 1, :], bank[4][:, 0:T], ot[:, n % 4, 0, :].bitcast(F32),
                                            ALU.subtract).then_inc(o_lo, 1)
                if cur and 2 <= i < 2 + LUT // 2:
                    if i == 2:
                        dve.wait_ge(idx_in, b * 16 + 16)
                        dve.sem_inc(carrier, 1)
                        if prev:
                            dve.wait_ge(dec_out, b * 16)
                            dve.sem_inc(carrier, 1)
                    for j in (2 * i - 4, 2 * i - 3):
                        if j > 3:
                            dve.wait_ge(pchain, at(pchain, b, j - 4))
                            dve.sem_inc(carrier, 1)
                        nc.vector.tensor_scalar(entries(j), idx, float(j), lut_sb[:, j:j + 1], ALU.is_equal, ALU.mult
                                                ).then_inc(entry, 1)
                if cur and i % 2 == 0:
                    dve.wait_ge(v_hi, at(v_hi, b, i // 2))
                    nc.vector.tensor_tensor(v[:, i // 4 % 2, 1, i // 2 % 2, :], bank[5][:, :],
                                            v[:, i // 4 % 2, 0, i // 2 % 2, :].bitcast(F32), ALU.subtract
                                            ).then_inc(v_lo, 1)
                n = i - 1
                if n >= 0 and cur or n < 0 and prev:
                    dve.wait_ge(s_exp, at(s_exp, b, n))
                    nc.vector.reciprocal(rden[:, n % 2, :], den[:, n % 2, :]).then_inc(s_rden, 1)
                    dve.wait_ge(s_rden, at(s_rden, b, n))
                    for t in range(TT):
                        last = nc.vector.tensor_scalar(probs[:, n % 2, t, :], probs[:, n % 2, t, :],
                                                       rden[:, n % 2, t:t + 1], None, ALU.mult)
                    last.then_inc(s_norm, 1)
                n = i - 2
                if n >= 0 and cur or n < 0 and prev:
                    dve.wait_ge(pt_hi, at(pt_hi, b, n))
                    nc.vector.tensor_tensor(pt[:, n % 2, 1].rearrange("p t n -> p (t n)"), bank[3][:, :],
                                            pt[:, n % 2, 0].rearrange("p t n -> p (t n)").bitcast(F32),
                                            ALU.subtract).then_inc(pt_lo, 1)
                if i == 1 and prev:
                    gate(b - 1)
                if i == 5 and prev:
                    finish(b - 1)
                if cur and i == 12:
                    dve.wait_ge(x_load, at(x_load, b - 1, 15))
                    prep_stats(b + 1, x_next)
                if cur and i == 13:
                    prep_apply(b + 1, x_next)

            for i in range(H0):
                head_step(0, i, prev=False)
            with dve.Fori(1, B) as b:
                for i in range(H0):
                    head_step(b, i)
            for i in range(6):
                head_step(B, i, cur=False)

            if phases > 1:
                for n in range(NB):
                    lo, width = n * PIECE, min(PIECE, FLAT_B - n * PIECE)
                    dve.wait_ge(bc_hi, n + 1)
                    nc.vector.tensor_tensor(WB[:, 1, lo:lo + width], raw[:, n % RING, 0:width],
                                            WB[:, 0, lo:lo + width].bitcast(F32), ALU.subtract).then_inc(raw2_used, 1)
                with dve.Fori(0, B) as b:
                    gate(b + B)
                    for k in range(FK + 1):
                        if k < FK:
                            dve.wait_ge(gu_lo, at(gu_lo, b, k - 2))
                            dve.wait_ge(gu_silu, at(gu_silu, b, k))
                            nc.vector.tensor_tensor(guf[:, k % 2, :], sg[:, k % 2, :], bank[k % 4][:, T:2 * T], ALU.mult
                                                    ).then_inc(gu_mul, 1)
                        if k >= 1:
                            dve.wait_ge(gu_hi, at(gu_hi, b, k - 1))
                            nc.vector.tensor_tensor(gu_slot(k - 1, 1), guf[:, (k - 1) % 2, :],
                                                    gu_slot(k - 1, 0).bitcast(F32), ALU.subtract).then_inc(gu_lo, 1)
                        if k == 2:
                            dve.wait_ge(x_load, at(x_load, b + B - 1, 15))
                            prep(b + B + 1, x_next)
                        if k == FK - 1:
                            pass
                    prep_low(b + B + 1)
                    finish(b + B)

            if phases > 2:
                def narrow(b, g, m):
                    dve.wait_ge(c_hi, at(c_hi, b, 2 * g + m))
                    for x in range(2):
                        last = nc.vector.scalar_tensor_tensor(
                            out=v[:, g % 2, m, x, 0:T], in0=qk[:, m, 0, x, :].bitcast(F32),
                            scalar=(low_q, low_k)[x][:, 0:1], in1=narrow_ps(g, m)[:, x * T:(x + 1) * T],
                            op0=ALU.mult, op1=ALU.add)
                    last.then_inc(c_ok, 1)

                def output(b, stage):
                    if stage == 0:
                        dve.wait_ge(av_done, at(av_done, b, H1 - 1))
                        r1 = repeat(rall_old[:, :, :].rearrange("p h t -> p t h"), 3, 16)
                        nc.vector.tensor_tensor(y_t[:, :, :].rearrange("p t (h d) -> p t h d", h=H1),
                                                y_ps[:, :].rearrange("p (t h d) -> p t h d", t=TT, h=H1),
                                                r1, ALU.mult).then_inc(d_read, 1)
                    else:
                        dve.wait_ge(d_square, at(d_square, b))
                        nc.vector.tensor_reduce(ssum[:, :], square[:, :, :].rearrange("p t (h d) -> p (t h) d", h=H1),
                                                AX, ALU.add).then_inc(d_chain, 1)
                        dve.wait_ge(d_chain, at(d_chain, b))
                        dve.sem_inc(carrier, 1)
                        cc = (1.0 - LAMBDA_INIT) ** 2
                        nc.vector.tensor_scalar(ssum[:, :], ssum[:, :], 1.0 / (16 * cc), EPS / cc, ALU.mult, ALU.add
                                                ).then_inc(rms_in, 1)

                def head_step(b, i, cur=True, prev=True, following=True):
                    if cur:
                        dve.wait_ge(e_full, at(e_full, b, i))
                        for t in range(TT):
                            keys = (t + 1) * P
                            ps = bank[(1, 3)[i % 2] if t else (2, 5)[i % 2]]
                            last = nc.vector.tensor_reduce(nmax1[:, i % 2, t, :],
                                                           ps[:, 0:2 * keys].rearrange("p (m n) -> p m n", m=2),
                                                           AX, ALU.max, negate=True)
                        last.then_inc(e_max, 1)
                    if i == DIFF_AT + 1 and prev:
                        dve.wait_ge(dr_hi, at(dr_hi, b - 1))
                        nc.vector.tensor_tensor(dr[:, 1].rearrange("p c n -> p (c n)"), tr_ps[:, :],
                                                dr[:, 0].rearrange("p c n -> p (c n)").bitcast(F32), ALU.subtract
                                                ).then_inc(dr_lo, 1)
                    if i == DIFF_AT + 4 and prev:
                        finish(b + 2 * B - 1, late=True)
                    if i == 14 and following:
                        narrow(b + 1, 0, 0)
                    if i == 1 and prev:
                        nc.vector.tensor_copy(rall_old[:, :, :], rall[:, :, :, 0]).then_inc(r_moved, 1)
                        dve.wait_ge(r_moved, at(r_moved, b - 1))
                    n = i - 1
                    if n >= 0 and cur or n < 0 and prev:
                        dve.wait_ge(e_exp, at(e_exp, b, n))
                        nc.vector.reciprocal(rall[:, n % H1, :, :], den1[:, n % 2, :, :]).then_inc(e_rec, 1)
                        dve.wait_ge(e_rec, at(e_rec, b, n))
                        nc.vector.scalar_tensor_tensor(out=ratio[:, n % 2, :], in0=den1[:, n % 2, :, 0],
                                                       scalar=nlam[:, 0:1], in1=rall[:, n % H1, :, 1], op0=ALU.mult,
                                                       op1=ALU.mult).then_inc(e_rat, 1)
                        dve.wait_ge(e_rat, at(e_rat, b, n))
                        for t in range(TT):
                            lo, hi = t * P, t * P + (t + 1) * P
                            last = nc.vector.scalar_tensor_tensor(
                                out=pc[:, n % 2, 0, lo:hi], in0=pc[:, n % 2, 1, lo:hi],
                                scalar=ratio[:, n % 2, t:t + 1], in1=pc[:, n % 2, 0, lo:hi], op0=ALU.mult, op1=ALU.add)
                        last.then_inc(e_diff, 1)
                    if cur and i in NARROW_AT:
                        narrow(b, *NARROW_AT[i])
                    if i == 2 and prev:
                        output(b - 1, 0)
                        gate(b + 2 * B - 1)
                    if i == 4 and prev:
                        output(b - 1, 1)
                    if i == PREP_AT - 1 and cur:
                        dve.wait_ge(early_in, at(early_in, b, 15))
                        dve.sem_inc(carrier, 1)
                        prep_stats(b + 2 * B + 1, x_early)
                    if i == PREP_AT and cur:
                        prep_apply(b + 2 * B + 1, x_early, xn_early)
                    if i == PREP_AT + 2 and cur:
                        prep_low(b + 2 * B + 1)
                    if i == 15 and following:
                        narrow(b + 1, 0, 1)

                narrow(0, 0, 0)
                narrow(0, 0, 1)
                for i in range(H1):
                    head_step(0, i, prev=False)
                with dve.Fori(1, B - 1) as b:
                    for i in range(H1):
                        head_step(b, i)
                for i in range(H1):
                    head_step(B - 1, i, following=False)
                for i in range(DIFF_AT + 5):
                    head_step(B, i, cur=False, following=False)

            if phases > 3:
                link(nc.vector.memset(comb[:, :, :], 0.0))
                with dve.Fori(0, B) as b:
                    gate(b + 3 * B)
                    n = [0]

                    def step_link(ins):
                        ins.then_inc(dr_chain, 1)
                        dve.wait_ge(dr_chain, at(dr_chain, b, n[0]))
                        n[0] += 1

                    dve.wait_ge(lg_full, at(lg_full, b))
                    nc.vector.tensor_reduce(r_max[:, :], bank[3][:, 0:TT * E1].rearrange("p (t e) -> p t e", t=TT), AX,
                                            ALU.max, negate=True).then_inc(lg_max, 1)
                    dve.wait_ge(lg_exp, at(lg_exp, b))
                    ej = repeat(r_e[:, :, :], 2, E1)
                    ee = repeat(r_e[:, :, :], 3, E1)
                    tr = repeat(tri[:, :, :], 1, TT)
                    nc.vector.tensor_tensor(r_gt, ej, ee, ALU.is_gt)
                    step_link(nc.vector.tensor_tensor(r_eq, ej, ee, ALU.is_equal))
                    step_link(nc.vector.tensor_tensor(r_eq, r_eq, tr, ALU.mult))
                    step_link(nc.vector.tensor_tensor(r_gt, r_gt, r_eq, ALU.add))
                    step_link(nc.vector.tensor_reduce(r_rank[:, :, :], r_gt, AX, ALU.add))
                    step_link(nc.vector.scalar_tensor_tensor(out=r_w[:, :, :], in0=r_rank[:, :, :], scalar=2.0,
                                                             in1=r_e[:, :, :], op0=ALU.is_lt, op1=ALU.mult))
                    step_link(nc.vector.tensor_reduce(r_sum[:, :], r_w[:, :, :], AX, ALU.add))
                    step_link(nc.vector.reciprocal(r_sum[:, :], r_sum[:, :]))
                    for t in range(TT):
                        last = nc.vector.tensor_scalar(comb[:, t, 0:E1], r_w[:, t, :], r_sum[:, t:t + 1], None, ALU.mult)
                    last.then_inc(cb_ok, 1)
                    dve.wait_ge(cb_hi, at(cb_hi, b))
                    nc.vector.tensor_tensor(comb_r[:, 1], bank[3][0:E1, 0:T], comb_r[:, 0].bitcast(F32), ALU.subtract
                                            ).then_inc(cb_lo, 1)
                    for k in range(EK + 1):
                        if k < EK:
                            dve.wait_ge(eg_lo, at(eg_lo, b, k - 2))
                            dve.wait_ge(eg_silu, at(eg_silu, b, k))
                            nc.vector.tensor_tensor(guf[:, k % 2, :], sg[:, k % 2, :], bank[k % 3][:, T:2 * T], ALU.mult
                                                    ).then_inc(eg_up, 1)
                            dve.wait_ge(bc_full, at(bc_full, b, k))
                            dve.sem_inc(carrier, 1)
                            dve.wait_ge(eg_up, at(eg_up, b, k))
                            nc.vector.tensor_tensor(guf[:, k % 2, :], guf[:, k % 2, :], bank[4 + k % 2][:, 0:T], ALU.mult
                                                    ).then_inc(eg_mul, 1)
                        if k >= 1:
                            dve.wait_ge(eg_hi, at(eg_hi, b, k - 1))
                            nc.vector.tensor_tensor(gu_slot(k - 1, 1), guf[:, (k - 1) % 2, :],
                                                    gu_slot(k - 1, 0).bitcast(F32), ALU.subtract).then_inc(eg_lo, 1)
                        if k == 5:
                            dve.wait_ge(x_load, at(x_load, b + 3 * B - 1, 15))
                            prep(b + 3 * B + 1, x_next)
                    prep_low(b + 3 * B + 1)
                    finish(b + 3 * B)

        @block.tensor
        def _(pe):
            for s_ in (proj_done, av_done):
                pe.sem_inc(s_, OFF)
            pe.wait_ge(c_silu, 1)
            for n in range(N_MOD):
                pe.wait_ge(raw_in[n % RING], 16 * (n // RING + 1))
                for j in range(4):
                    k = 4 * (n % 3) + j
                    for c in range(CC):
                        last = nc.tensor.matmul(bank[n // 3][:, 8 * k:8 * k + 8], slot(n, CC)[:, c, P * j:P * (j + 1)],
                                                cs[:, n // 3, c, :], start=(c == 0), stop=(c == CC - 1))
                last.then_inc(mod_ps, 1)

            def three(ps, w, m, n, first=True, last=True, **kw):
                parts = [(0, 0), (0, 1), (1, 0)]
                for j in range(n):
                    for a, (wp, mp) in enumerate(parts):
                        ins = nc.tensor.matmul(ps, w(j, wp), m(j, mp), start=(first and j == 0 and a == 0),
                                               stop=(last and j == n - 1 and a == 2), **kw)
                return ins

            def prep(s, xn=xn):
                pe.wait_ge(xn_ok, at(xn_ok, s))
                pe.wait_ge(x_moved, at(x_moved, s - 2))
                for c in range(CC):
                    for t in range(TT):
                        last = nc.tensor.transpose(tr_ps[:, c * T + t * P:c * T + (t + 1) * P],
                                                   xn[:, t, c * P:(c + 1) * P], ident[:, :])
                last.then_inc(xnt_full, 1)

            def finish(s):
                pe.wait_ge(y_ev, at(y_ev, s))
                pe.wait_ge(h_hi, at(h_hi, s + 1))
                for t in range(TT):
                    for c in range(CC):
                        last = nc.tensor.transpose(tr_ps[:, t * C + c * P:t * C + (c + 1) * P],
                                                   y_t[:, c, t * P:(t + 1) * P], ident[:, :])
                last.then_inc(yt_full, 1)

            pe.wait_ge(s_const, 1)
            prep(0)
            pe.wait_ge(raw_used, N_A - N_MOD)

            def head_step(b, i, cur=True, prev=True):
                if cur:
                    if i == 0:
                        pe.wait_ge(h_ok, at(h_ok, b))
                    pe.wait_ge(qk_lo, at(qk_lo, b, i - 2))
                    for m in range(2):
                        last = three(bank[i % 2][:, m * T:(m + 1) * T],
                                     lambda j, a: WQK[:, a, j, m, i * P:(i + 1) * P],
                                     lambda j, a: h[:, a, j, :], CC)
                    last.then_inc(qk_full, 1)
                n = i - 1
                if n >= 0 and cur or n < 0 and prev:
                    pe.wait_ge(qk_lo, at(qk_lo, b, n))
                    pe.wait_ge(s_exp, at(s_exp, b, n - 1))
                    for q in range(TT):
                        last = three(bank[2][:, q * T:(q + 1) * T],
                                     lambda j, a: qk[:, n % 2, a, 0, q * P:(q + 1) * P],
                                     lambda j, a: qk[:, n % 2, a, 1, :], 1)
                    last.then_inc(s_full, 1)
                n = i - 3
                if n >= 0 and cur or n < 0 and prev:
                    pe.wait_ge(pt_lo, at(pt_lo, b, n))
                    pe.wait_ge(o_lo, at(o_lo, b, n - 1))
                    if n % 4 == 0:
                        pe.wait_ge(v_lo, at(v_lo, b, 2 * (n // 4) + 1))
                    three(bank[4][:, 0:T],
                          lambda j, a: v[:, n // 4 % 2, a, j, (n % 4) * P:(n % 4 + 1) * P],
                          lambda j, a: pt[:, n % 2, a, j, :], TT).then_inc(o_full, 1)
                if cur and i % 2 == 0:
                    g, t = i // 4, i // 2 % 2
                    pe.wait_ge(v_lo, at(v_lo, b, i // 2 - 1))
                    three(bank[5][:, :], lambda j, a: h[:, a, j, t * P:(t + 1) * P],
                          lambda j, a: WV[:, a, j, 512 * g:512 * (g + 1)], CC).then_inc(v_full, 1)
                n = i - 2
                if n >= 0 and cur or n < 0 and prev:
                    pe.wait_ge(s_norm, at(s_norm, b, n))
                    pe.wait_ge(pt_lo, at(pt_lo, b, n - 1))
                    for k in range(TT):
                        for q in range(TT):
                            last = nc.tensor.transpose(bank[3][:, k * T + q * P:k * T + (q + 1) * P],
                                                       probs[:, n % 2, q, k * P:(k + 1) * P], ident[:, :])
                    last.then_inc(pt_full, 1)
                n = i - 4
                if n >= 0 and cur or n < 0 and prev:
                    pe.wait_ge(o_lo, at(o_lo, b, n))
                    if n == 0:
                        pe.wait_ge(y_ev, at(y_ev, b - 1))
                    for c in range(CC):
                        last = three(y_ps[:, c * T:(c + 1) * T],
                                     lambda j, a: WO[:, a, n % H0, c * P:(c + 1) * P],
                                     lambda j, a: ot[:, n % 4, a, :], 1, first=(n == 0 and c == 0),
                                     last=(n == -1), skip_group_check=True)
                    last.then_inc(proj_done, 1)
                if i == 4 and prev:
                    finish(b - 1)
                if i == 14 and cur:
                    prep(b + 1)

            for i in range(H0):
                head_step(0, i, prev=False)
            with pe.Fori(1, B) as b:
                for i in range(H0):
                    head_step(b, i)
            for i in range(5):
                head_step(B, i, cur=False)

            if phases > 1:
                pe.wait_ge(raw2_used, NB)
                with pe.Fori(0, B) as b:
                    pe.wait_ge(h_ok, at(h_ok, b + B))
                    for k in range(FK + 2):
                        if k < FK:
                            pe.wait_ge(gu_mul, at(gu_mul, b, k - 4))
                            for x, w in enumerate((WG, WU)):
                                last = three(bank[k % 4][:, x * T:(x + 1) * T],
                                             lambda j, a: w[:, a, j, k * P:(k + 1) * P], lambda j, a: h[:, a, j, :], CC)
                            last.then_inc(gu_full, 1)
                        if k == FK - 1:
                            prep(b + B + 1)
                        if k >= 2:
                            n = k - 2
                            pe.wait_ge(gu_lo, at(gu_lo, b, n))
                            for c in range(CC):
                                last = three(y_ps[:, c * T:(c + 1) * T], lambda j, a: WD[:, a, n, c * P:(c + 1) * P],
                                             lambda j, a: gu_slot(n, a), 1, first=(n == 0 and c == 0),
                                             last=(n == FK - 1), skip_group_check=True)
                            last.then_inc(y_full if n == FK - 1 else down_done, 1)
                    finish(b + B)

            if phases > 2:
                pe.wait_ge(wc_ok, 3)
                def narrow(b, g, m, x):
                    if g == 0:
                        pe.wait_ge(h_ok, at(h_ok, b + 2 * B))
                    if x == 0:
                        pe.wait_ge(c_ok, at(c_ok, b, 2 * g + m - 1 - ((g, m) in ((0, 1), (1, 0)))))
                    last = three(narrow_ps(g, m)[:, x * T:(x + 1) * T],
                                 lambda j, a: WC[:, a, 2 * m + x, j, g * P:(g + 1) * P],
                                 lambda j, a: h[:, a, j, :], CC)
                    if x:
                        last.then_inc(c_full, 1)

                def narrow_first(b):
                    for m in range(2):
                        for x in range(2):
                            narrow(b, 0, m, x)
                    narrow(b, 1, 0, 0)

                def head_step(b, i, cur=True, prev=True, following=True):
                    if cur:
                        g, lo = i // 4, 32 * (i % 4)
                        if i % 4 == 0:
                            pe.wait_ge(c_ok, at(c_ok, b, 2 * g + 1))
                        pe.wait_ge(e_exp, at(e_exp, b, i - 2))
                        for t in range(TT):
                            keys = (t + 1) * P
                            ps = bank[(1, 3)[i % 2] if t else (2, 5)[i % 2]]
                            for m in range(2):
                                nc.tensor.matmul(ps[:, m * keys:(m + 1) * keys],
                                                 v[lo:lo + 32, g % 2, m, 0, t * P:(t + 1) * P],
                                                 v[lo:lo + 32, g % 2, m, 1, 0:keys], start=(m == 0), stop=False,
                                                 skip_group_check=True)
                        for t in range(TT):
                            keys = (t + 1) * P
                            ps = bank[(1, 3)[i % 2] if t else (2, 5)[i % 2]]
                            masked = ps[:, 0:2 * keys].rearrange("p (m n) -> p m n", m=2)[:, :, keys - P:]
                            last = nc.tensor.matmul(masked, ident_r[:, :], repeat(mask_r[:, :], 1, 2),
                                                    start=False, stop=True, skip_group_check=True)
                        last.then_inc(e_full, 1)
                    if cur and i in NARROW_AT:
                        narrow(b, *NARROW_AT[i], 1)
                    if cur and i + 1 in NARROW_AT:
                        narrow(b, *NARROW_AT[i + 1], 0)
                    n = i - 2
                    if n >= 0 and cur or n < 0 and prev:
                        pe.wait_ge(e_diff, at(e_diff, b, n))
                        pe.wait_ge(t_ok, at(t_ok, b, n - 1))
                        for k, lo in enumerate((0, P, 2 * P)):
                            last = nc.tensor.transpose(bank[4][:, k * P:(k + 1) * P], pc[:, n % 2, 0, lo:lo + P],
                                                       ident[:, :])
                        last.then_inc(t_full, 1)
                    n = i - 3
                    if n >= 0 and cur or n < 0 and prev:
                        pe.wait_ge(t_ok, at(t_ok, b, n))
                        if n == 0:
                            pe.wait_ge(v1_ok, at(v1_ok, b))
                            pe.wait_ge(y_ev, at(y_ev, 2 * B - 1))
                            pe.wait_ge(d_read, at(d_read, b - 1))
                        o = n % H1 * 16
                        e = min(o + P, C)
                        nc.tensor.matmul(y_ps[:, o:e], ptf[:, n % 2, 0:P], v1[:, 0, o:e], start=True, stop=True)
                        nc.tensor.matmul(y_ps[:, T + o:T + e], ptf[:, n % 2, P:2 * P], v1[:, 0, o:e],
                                         start=True, stop=False)
                        nc.tensor.matmul(y_ps[:, T + o:T + e], ptf[:, n % 2, 2 * P:3 * P], v1[:, 1, o:e],
                                         start=False, stop=True).then_inc(av_done, 1)
                    if i == 0 and cur:
                        pe.wait_ge(c_ok, at(c_ok, b, 1))
                        for t in range(TT):
                            last = three(tr_ps[:, t * C:(t + 1) * C], lambda j, a: h[:, a, j, t * P:(t + 1) * P],
                                         lambda j, a: WV1[:, a, j, :], CC)
                        last.then_inc(v1_full, 1)
                    if i == PREP_AT + 1 and cur:
                        prep(b + 2 * B + 1, xn_early)
                    if following and 13 <= i <= 14:
                        narrow(b + 1, 0, i - 13, 0)
                        narrow(b + 1, 0, i - 13, 1)
                    if following and i == 15:
                        narrow(b + 1, 1, 0, 0)
                    if i == DIFF_AT and prev:
                        pe.wait_ge(d_ok, at(d_ok, b - 1))
                        if cur:
                            pe.wait_ge(v1_ok, at(v1_ok, b))
                        for c in range(CC):
                            for t in range(TT):
                                last = nc.tensor.transpose(tr_ps[:, c * T + t * P:c * T + (t + 1) * P],
                                                           y_t[:, t, c * P:(c + 1) * P], ident[:, :])
                        last.then_inc(dt_full, 1)
                    if i == DIFF_AT + 1 and prev:
                        pe.wait_ge(dr_lo, at(dr_lo, b - 1))
                        for c in range(CC):
                            last = three(tr_ps[:, c * T:(c + 1) * T], lambda j, a: WP1[:, a, j, c * P:(c + 1) * P],
                                         lambda j, a: dr[:, a, j, :], CC)
                        last.then_inc(y_full, 1)
                    if i == DIFF_AT + 3 and prev:
                        finish(b + 2 * B - 1)

                pe.wait_ge(x_moved, at(x_moved, 2 * B - 1))
                narrow_first(0)
                for i in range(H1):
                    head_step(0, i, prev=False)
                with pe.Fori(1, B - 1) as b:
                    for i in range(H1):
                        head_step(b, i)
                for i in range(H1):
                    head_step(B - 1, i, following=False)
                for i in range(DIFF_AT + 4):
                    head_step(B, i, cur=False, following=False)

            if phases > 3:
                pe.wait_ge(wd_ok, NGU + 3)
                with pe.Fori(0, B) as b:
                    pe.wait_ge(h_ok, at(h_ok, b + 3 * B))
                    pe.wait_ge(cb_lo, at(cb_lo, b - 1))
                    for t in range(TT):
                        for c in range(CC):
                            last = nc.tensor.matmul(bank[3][:, t * E1:(t + 1) * E1], h_f[:, c, t * P:(t + 1) * P],
                                                    gw_sb[:, c, :], start=(c == 0), stop=(c == CC - 1))
                    last.then_inc(lg_full, 1)

                    def spread(k):
                        pe.wait_ge(eg_mul, at(eg_mul, b, k - 2))
                        for a in range(2):
                            last = nc.tensor.matmul(bank[4 + k % 2][:, 0:T], sel[:, k * P:(k + 1) * P], comb_r[:, a],
                                                    start=(a == 0), stop=(a == 1))
                        last.then_inc(bc_full, 1)

                    for k in range(EK + 2):
                        if k < EK:
                            pe.wait_ge(eg_mul, at(eg_mul, b, k - 3))
                            for x, w in enumerate((WG1, WU1)):
                                last = three(bank[k % 3][:, x * T:(x + 1) * T],
                                             lambda j, a: w[:, a, j, k * P:(k + 1) * P], lambda j, a: h[:, a, j, :], CC)
                            last.then_inc(eg_full, 1)
                        if k == 1:
                            pe.wait_ge(cb_ok, at(cb_ok, b))
                            for t in range(TT):
                                last = nc.tensor.transpose(bank[3][:, t * P:(t + 1) * P], comb[:, t, :], ident[:, :])
                            last.then_inc(cbt_full, 1)
                        if k == 2:
                            pe.wait_ge(cb_lo, at(cb_lo, b))
                            spread(0)
                            spread(1)
                        if 2 <= k < EK:
                            spread(k)
                        if k == EK - 1:
                            prep(b + 3 * B + 1)
                        if k >= 2:
                            n = k - 2
                            pe.wait_ge(eg_lo, at(eg_lo, b, n))
                            for c in range(CC):
                                last = three(y_ps[:, c * T:(c + 1) * T], lambda j, a: WD1[:, a, n, c * P:(c + 1) * P],
                                             lambda j, a: gu_slot(n, a), 1, first=(n == 0 and c == 0),
                                             last=(n == EK - 1), skip_group_check=True)
                            last.then_inc(y_full if n == EK - 1 else edown, 1)
                    finish(b + 3 * B)


PHASES = 4


def kernel(**inputs):
    import numpy as np
    import concourse.bacc as bacc
    from concourse.bass_utils import run_bass_kernel_spmd

    i = {k: np.asarray(a) for k, a in inputs.items()}
    t = np.ascontiguousarray
    pad = lambda a, n, ax, val: np.concatenate([a, np.full([n - a.shape[d] if d == ax else a.shape[d]
                                                            for d in range(a.ndim)], val, a.dtype)], ax)
    w1 = i["L1_ffn_w1"]
    chunks = lambda a: a.reshape(-1, P, a.shape[1]).transpose(1, 0, 2).reshape(P, -1)
    arrays = {
        "x_in": t(i["L0_attn_x"].reshape(B * T, C)),
        "c_t0": t(i["L0_c"].T), "c_t1": t(i["L1_c"].T),
        "wmod0": t(i["L0_wmod"]), "wmod1": t(i["L1_wmod"]),
        "wqkv0": t(i["L0_attn_w_qkv"]), "wout0": t(i["L0_attn_w_out"]),
        "lut_b": t(np.broadcast_to(i["L0_ffn_lut"][None, :], (P, LUT))),
        "ffn_idx": t(np.concatenate([chunks(pad(i["L0_ffn_gate_idx"], FP, 0, LUT).T),
                                     chunks(pad(i["L0_ffn_up_idx"], FP, 0, LUT).T),
                                     chunks(pad(i["L0_ffn_down_idx"], FP, 1, LUT).T),
                                     np.zeros((P, SIX), i["L0_ffn_gate_idx"].dtype)], 1)),
        "w_c": t(i["L1_attn_Wqkv"][:, :4 * P].reshape(CC, P, 4, P).transpose(1, 2, 0, 3).reshape(P, -1)),
        "w_vp": t(np.concatenate([chunks(i["L1_attn_Wqkv"][:, 4 * P:]), chunks(i["L1_attn_Wproj"])], 1)),
        "lam_v": t(np.broadcast_to(np.concatenate([i["L1_attn_lambda_" + k] for k in ("q1", "k1", "q2", "k2")])[None],
                                   (P, 4 * D1))),
        "gatew": t(chunks(i["L1_ffn_gate_w"].T)),
        "w_gu": t(np.concatenate([chunks(w1[:, :I1].reshape(EI, C).T), chunks(w1[:, I1:].reshape(EI, C).T)], 1)),
        "w_d": t(chunks(i["L1_ffn_w2"].transpose(0, 2, 1).reshape(EI, C))),
    }
    nc = bacc.Bacc("TRN2", target_bir_lowering=False, num_devices=1)
    args = [nc.dram_tensor(k, a.shape, mybir.dt.from_np(a.dtype), kind="ExternalInput").ap() for k, a in arrays.items()]
    args.append(nc.dram_tensor("out", *[(B * T, C), F32], kind="ExternalOutput").ap())
    program(nc, *args, phases=PHASES)
    r = run_bass_kernel_spmd(nc, [arrays], core_ids=[0])
    return r.results[0]["out"].reshape(B, T, C)
```

```python
from contextlib import ExitStack

import concourse.bass as bass
from concourse import mybir

F32 = mybir.dt.float32
F32R = mybir.dt.float32r
I32 = mybir.dt.int32
ALU = mybir.AluOpType
ACT = mybir.ActivationFunctionType
AX = mybir.AxisListType.X

P = 128
B, T, C = 8, 256, 256
CC = C // P
TT = T // P
H0, D0 = 16, 128
SCALE0 = D0 ** -0.5
LUT, INTER = 16, 688
FK = -(-INTER // P)
FP = FK * P
H1, D1 = 16, 8
SCALE1 = D1 ** -0.5
LAMBDA_INIT = 0.8 - 0.6 * 2.718281828459045 ** (-0.3)
EPS = 1e-5
E1, I1 = 8, 176
EI = E1 * I1
EK = EI // P
NARROW_AT = {0: (1, 0), 2: (1, 1), 4: (2, 0), 6: (2, 1), 8: (3, 0), 10: (3, 1)}
DIFF_AT = 7
PREP_AT = 10
STEPS = 4 * B
OFF = 8
PIECE = 1024
RING = 3
NEG = -(2.0 ** 100)
FLAT_B = 2 * CC * FP + FK * C
PART = -(-FLAT_B // (B - 1) // 4) * 4
NB = -(-FLAT_B // PIECE)
NGU = -(-2 * CC * EI // PIECE)




def repeat(ap, axis, n):
    ap = ap.unsqueeze(axis)
    shape = list(ap.shape)
    shape[axis] = n
    return ap.broadcast_to(shape)


def last_user(k, slots, chunks):
    return k - slots if k >= slots else max(j for j in range(chunks) if j % slots == k % slots) - chunks


def program(nc, x_in, c_t0, c_t1, wmod0, wmod1, wqkv0, wout0, lut_b, ffn_idx, w_c, w_vp, lam_v, gatew, w_gu, w_d, out,
            phases=4):
    ctx = ExitStack()
    with ctx:
        def sb(name, shape, dt=F32):
            return ctx.enter_context(nc.sbuf_tensor(name, shape, dt))

        per, ahead = {}, {}

        def sem(name, events=1, head=0):
            made = ctx.enter_context(nc.semaphore(name))
            per[name], ahead[name] = events, head
            names[id(made)] = name
            return made

        def at(s, step, n=0):
            name = names[id(s)]
            return step * per[name] + (n + 1 + ahead[name])

        names = {}

        bank = [ctx.enter_context(nc.psum_tensor(f"bank{i}", [P, 512], F32)) for i in range(8)]
        tr_ps, y_ps = bank[6], bank[7]
        x_dram = nc.dram_tensor("x_steps", ((STEPS + 2) * T, C), F32).ap()
        out_steps = out.rearrange("(s t p) c -> s p t c", t=TT, p=P)
        x_steps = x_dram.rearrange("(s t p) c -> s p t c", t=TT, p=P)

        ident = sb("ident", [P, P])
        raw = sb("raw", [P, RING, PIECE])
        mod = sb("mod", [P, STEPS + 2, 6])
        mod_now = sb("mod_now", [P, 4])
        gate_now = sb("gate_now", [P, 2])
        c_sb = sb("c_sb", [P, 2, CC, B])
        cs = sb("cs", [P, 2, CC, B])
        x_cur = sb("x_cur", [P, TT, C])
        x_next = sb("x_next", [P, TT, C])
        xn = sb("xn", [P, TT, C])
        x_out = xn
        h_f = sb("h_f", [P, CC, T])
        y_t = sb("y_t", [P, CC, T])
        stats = sb("stats", [P, TT, 6])
        mv = sb("mv", [P, TT, 2])
        ve = sb("ve", [P, TT])
        rstd = sb("rstd", [P, TT])
        mhalf = sb("mhalf", [P, 32])
        work = sb("work", [P, 2048])
        probs = work[:, 0:1024].rearrange("p (s t n) -> p s t n", s=2, t=TT)
        nmax = sb("nmax", [P, 2, TT])
        den = sb("den", [P, 2, TT])
        rden = sb("rden", [P, 2, TT])
        warm = sb("warm", [P, 1])
        lut_sb = sb("lut_sb", [P, LUT])
        mask_f = sb("mask_f", [P, P])
        lanes = sb("lanes", [P, 1], I32)
        lane_bit = sb("lane_bit", [P, 2], I32)
        low_q = sb("low_q", [P, 1])
        low_k = sb("low_k", [P, 1])
        lam_sb = sb("lam_sb", [P, 4, D1])
        lam_p = sb("lam_p", [P, 2, D1])
        lam_e = sb("lam_e", [P, 2])
        nlam = sb("nlam", [P, 1])
        nmax1 = sb("nmax1", [P, 2, TT, 2])
        den1 = sb("den1", [P, 2, TT, 2])
        rall = sb("rall", [P, H1, TT, 2])
        rall_old = sb("rall_old", [P, H1, TT])
        ratio = sb("ratio", [P, 2, TT])
        ssum = sb("ssum", [P, 32])
        tri = sb("tri", [P, E1, E1])
        gw_sb = sb("gw_sb", [P, CC, E1])
        r_max = sb("r_max", [P, TT])
        euler = sb("euler", [P, TT, E1])
        r_l = sb("r_l", [P, TT, E1])
        r_e = sb("r_e", [P, TT, E1])
        r_w = sb("r_w", [P, TT, E1])
        r_rank = sb("r_rank", [P, TT, E1])
        r_sum = sb("r_sum", [P, TT])

        W = sb("W", [P, 32768], F32R)
        h = sb("h", [P, 2, CC, T], F32R)
        qk = sb("qk", [P, 2, 2, 2, T], F32R)
        v = sb("v", [P, 2, 2, TT, 512], F32R)
        pt = sb("pt", [P, 2, 2, TT, T], F32R)
        mask_r = sb("mask_r", [P, P], F32R)
        ident_r = sb("ident_r", [P, P], F32R)
        with nc.sbuf_tensor("ot", [P, 4, 2, T], F32R) as ot:
            pass
        spare = sb("spare", [P, 2048])

        WQK = W[:, 0:16384].rearrange("p (l c m n) -> p l c m n", l=2, c=CC, m=2)
        WV = W[:, 16384:24576].rearrange("p (l c n) -> p l c n", l=2, c=CC)
        WO = W[:, 24576:32768].rearrange("p (l h n) -> p l h n", l=2, h=H0)

        WB = W[:, 0:2 * FLAT_B].rearrange("p (l n) -> p l n", l=2)
        WG = WB[:, :, 0:CC * FP].rearrange("p l (c n) -> p l c n", c=CC)
        WU = WB[:, :, CC * FP:2 * CC * FP].rearrange("p l (c n) -> p l c n", c=CC)
        WD = WB[:, :, 2 * CC * FP:FLAT_B].rearrange("p l (k n) -> p l k n", k=FK)
        C0 = 2 * FLAT_B
        WC = W[:, C0:C0 + 8192].rearrange("p (l m c n) -> p l m c n", l=2, m=4, c=CC)
        WVP = W[:, C0 + 8192:C0 + 10240].rearrange("p (l n) -> p l n", l=2)
        WV1 = WVP[:, :, 0:512].rearrange("p l (c n) -> p l c n", c=CC)
        WP1 = WVP[:, :, 512:1024].rearrange("p l (c n) -> p l c n", c=CC)
        G0 = C0 + 10240
        WGU = W[:, G0:G0 + 4 * CC * EI].rearrange("p (l n) -> p l n", l=2)
        WG1 = WGU[:, :, 0:CC * EI].rearrange("p l (c n) -> p l c n", c=CC)
        WU1 = WGU[:, :, CC * EI:2 * CC * EI].rearrange("p l (c n) -> p l c n", c=CC)
        WDD = W[:, 0:2 * EK * C].rearrange("p (l n) -> p l n", l=2)
        WD1 = WDD.rearrange("p l (k n) -> p l k n", k=EK)
        sel = W[0:E1, G0 + 4 * CC * EI:G0 + 4 * CC * EI + EI]
        gur = pt
        def gu_slot(k, part):
            return pt[:, k % 2, part, k // 2 % 2, :]
        sg = work[:, 0:512].rearrange("p (s n) -> p s n", s=2)
        guf = work[:, 512:1024].rearrange("p (s n) -> p s n", s=2)

        def gated(k):
            return work[:, (512, 768, 1536, 1792)[k % 4]:][:, 0:T]

        pc = work[:, 0:1536].rearrange("p (s m n) -> p s m n", s=2, m=2)
        v1 = work[:, 1536:2048].rearrange("p (t n) -> p t n", t=TT)
        ptf = raw[:, 2, 0:768].rearrange("p (s n) -> p s n", s=2)
        x_early = spare[:, 0:512].rearrange("p (t n) -> p t n", t=TT)
        xn_early = spare[:, 512:1024].rearrange("p (t n) -> p t n", t=TT)
        square = spare[:, 1024:1536].rearrange("p (t n) -> p t n", t=TT)
        dr = pt[:, 0]
        comb = work[:, 1024:1280].rearrange("p (t n) -> p t n", t=TT)
        r_gt = work[:, 1280:1408].rearrange("p (t e j) -> p t e j", t=TT, e=E1)
        r_eq = work[:, 1408:1536].rearrange("p (t e j) -> p t e j", t=TT, e=E1)
        comb_r = qk[0:E1, 0, :, 0, :]

        s_const = sem("s_const")
        s_pool = sem("s_pool")
        raw_in = [sem(f"raw_in{i}") for i in range(RING)]
        raw_used = sem("raw_used")
        raw_hi = sem("raw_hi")
        c_in = sem("c_in")
        c_silu = sem("c_silu")
        mod_ps = sem("mod_ps")
        mod_set = sem("mod_set")
        x_first = sem("x_first")
        x_copy = sem("x_copy")
        x_load = sem("x_load", 16, 16)
        x_store = sem("x_store", 16, 16)
        dchain = sem("dchain")
        mod_cp = sem("mod_cp")
        var_ok = sem("var_ok")
        rstd_ok = sem("rstd_ok")
        xn_ok = sem("xn_ok")
        xnt_full = sem("xnt_full")
        h_hi = sem("h_hi")
        h_high = sem("h_high")
        h_ok = sem("h_ok")
        y_full = sem("y_full", 1, -2 * B)
        y_ev = sem("y_ev", 1, OFF)
        yt_full = sem("yt_full")
        x_moved = sem("x_moved", 1, OFF)
        gate_ok = sem("gate_ok")
        p_carrier = sem("p_carrier")
        carrier = sem("carrier")
        sp_carrier = sem("sp_carrier")
        dcom2 = sem("dcom2")
        dcom = sem("dcom")

        block = ctx.enter_context(nc.Block())

        def cols(w, lo, n):
            return w.rearrange("(c p) n -> p c n", p=P)[:, :, lo:lo + n]

        def piece(kind, g):
            if kind in "01":
                return cols((wmod0, wmod1)[int(kind)], 512 * g, 512)
            if kind == "o":
                return wout0[512 * g:512 * (g + 1), :].rearrange("(h p) n -> p h n", p=P)
            return cols(wqkv0, "qkv".index(kind) * H0 * D0 + 512 * g, 512)

        first_pieces = [("0", 0), ("0", 1), ("0", 2), ("q", 0), ("k", 0), ("v", 0)]
        late_pieces = {0: [("q", 1)], 1: [("k", 1)], 2: [("v", 1)], 3: [("o", 0)], 4: [("q", 2)], 5: [("k", 2), ("1", 0)],
                       6: [("v", 2)], 7: [("o", 1), ("1", 1)], 8: [("q", 3)], 9: [("k", 3), ("1", 2)], 10: [("v", 3)],
                       11: [("o", 2)], 12: [("o", 3)]}
        pieces = first_pieces + [x for i in sorted(late_pieces) for x in late_pieces[i]]
        splits = [x for x in pieces if x[0] not in "01"]
        mods = [x for x in pieces if x[0] in "01"]

        def slot(n):
            return raw[:, n % RING, :].rearrange("p (c n) -> p c n", c=4 if pieces[n][0] == "o" else CC)

        flat = raw[:, :, :].rearrange("p s n -> p (s n)")
        idx = flat[:, 0:PART].bitcast(I32)
        decoded = flat[:, PART:2 * PART]

        def entries(j):
            return decoded if j == 0 else flat[:, (2 + j % 2) * PART:(3 + j % 2) * PART]

        def wa(x, part):
            kind, g = x
            if kind == "o":
                return WO[:, part, 4 * g:4 * (g + 1), :]
            if kind == "v":
                return WV[:, part, :, 512 * g:512 * (g + 1)]
            return WQK[:, part, :, "qk".index(kind), 512 * g:512 * (g + 1)]

        qk_full, qk_hi, qk_lo = sem("qk_full", H0), sem("qk_hi", H0), sem("qk_lo", H0, OFF)
        s_full, s_max, s_exp = sem("s_full", H0), sem("s_max", H0), sem("s_exp", H0, OFF)
        s_rden, s_norm = sem("s_rden", H0), sem("s_norm", H0)
        pt_full, pt_hi, pt_lo = sem("pt_full", H0), sem("pt_hi", H0), sem("pt_lo", H0, OFF)
        o_full, o_hi, o_lo = sem("o_full", H0), sem("o_hi", H0), sem("o_lo", H0, OFF)
        v_full, v_hi, v_lo = sem("v_full", 8), sem("v_hi", 8), sem("v_lo", 8, OFF)
        proj_done = sem("proj_done", H0, OFF)

        ffn_w = nc.dram_tensor("ffn_w", (P, (B - 1) * PART), F32).ap()
        raw2_in = [sem(f"raw2_in{i}") for i in range(RING)]
        raw2_used = sem("raw2_used")
        small_in = sem("small_in")
        idx_in, dec_out = sem("idx_in"), sem("dec_out")
        entry = sem("entry", LUT, OFF)
        pchain = sem("pchain", LUT - 1, OFF)
        pchain2 = sem("pchain2")
        dec_out_1 = sem("dec_out_1")
        bc_hi = sem("bc_hi")
        wc_ok, wd_ok, lam_ok, lam_exp, lane_ok = (sem(n) for n in ("wc_ok", "wd_ok", "lam_ok", "lam_exp", "lane_ok"))
        gu_full, gu_silu, gu_mul = sem("gu_full", FK), sem("gu_silu", FK), sem("gu_mul", FK, OFF)
        gu_hi, gu_lo, down_done = sem("gu_hi", FK), sem("gu_lo", FK, OFF), sem("down_done", FK, OFF)
        eg_full, eg_silu, eg_up, eg_mul = (
            sem("eg_full", EK), sem("eg_silu", EK), sem("eg_up", EK, OFF), sem("eg_mul", EK, OFF))
        eg_hi, eg_lo, edown = sem("eg_hi", EK), sem("eg_lo", EK, OFF), sem("edown", EK, OFF)
        bc_full = sem("bc_full", EK, OFF)
        lg_full, lg_max, lg_sub, lg_exp, cb_ok, cbt_full, cb_hi, cb_lo = (
            sem("lg_full"), sem("lg_max"), sem("lg_sub"), sem("lg_exp"), sem("cb_ok"), sem("cbt_full"), sem("cb_hi"), sem("cb_lo", 1, OFF))
        dr_chain, r_rec = sem("dr_chain", 6), sem("r_rec")
        v1_full, v1_ok = sem("v1_full"), sem("v1_ok", 1, OFF)
        c_full, c_hi, c_ok = sem("c_full", 8), sem("c_hi", 8), sem("c_ok", 8, OFF)
        e_full, e_max, e_exp, e_diff = sem("e_full", H1), sem("e_max", H1), sem("e_exp", H1, OFF), sem("e_diff", H1)
        e_rec, e_rat = sem("e_rec", H1), sem("e_rat", H1)
        t_full, t_ok, av_done = sem("t_full", H1), sem("t_ok", H1, OFF), sem("av_done", H1, OFF)
        rms_in, rms_ok, d_ok, dt_full, dr_hi, dr_lo = (sem(n) for n in ("rms_in", "rms_ok", "d_ok", "dt_full", "dr_hi", "dr_lo"))
        early_in = sem("early_in", 16)
        d_chain, d_square, r_moved, d_read = sem("d_chain"), sem("d_square"), sem("r_moved"), sem("d_read", 1, OFF)

        def narrow_ps(g, m):
            return tr_ps if (g, m) == (0, 1) else bank[0]

        @block.sync
        def _(sp):
            sp.sem_inc(x_store, 16)
            sp.sem_inc(x_load, 16)
            x9 = x_in.rearrange("(s t p) c -> s p t c", t=TT, p=P)
            sp.dma_start(x_cur[:, :, :], x9[0]).then_inc(x_first, 16)
            for n, (kind, g) in enumerate(pieces):
                if n >= RING:
                    old = pieces[n - RING]
                    if old in mods:
                        sp.wait_ge(mod_ps, mods.index(old) + 1)
                    else:
                        sp.wait_ge(raw_used, splits.index(old) + 1)
                sp.dma_start(slot(n), piece(kind, g)).then_inc(raw_in[n % RING], 16)
                if n == RING:
                    sp.dma_start(x_next[:, :, :], x9[1]).then_inc(x_first, 16)
            sp.wait_ge(x_copy, 32)
            for first, last in ((0, min(3, phases) * B), (3 * B, phases * B)):
                if first == last or phases < 4 and first:
                    continue
                to = x_steps if first == 0 else None
                with sp.Fori(first, last) as s:
                    sp.wait_ge(x_moved, at(x_moved, s))
                    sp.sem_inc(sp_carrier, 1)
                    dst = x_steps[s + B] if first == 0 else out_steps[s - 3 * B]
                    sp.dma_start(dst, x_out[:, :, :]).then_inc(x_store, 16)
                    sp.dma_start(x_next[:, :, :], x_steps[s + 2]).then_inc(x_load, 16)
                    sp.wait_ge(x_store, at(x_store, s, 15))
                    sp.sem_inc(sp_carrier, 1)
            if phases < 4:
                sp.dma_start(out, x_dram[8 * phases * T:8 * (phases + 1) * T, :]).then_inc(x_first, 16)
                sp.wait_ge(x_first, 48)
            sp.wait_ge(x_load, 16 * 8 * phases + 16)

        @block.gpsimd
        def _(pool):
            pool.dma_start(x_dram[0:B * T, :], x_in[0:B * T, :]).then_inc(x_copy, 16)
            pool.dma_start(x_dram[STEPS * T:(STEPS + 2) * T, :], x_in[0:2 * T, :]).then_inc(x_copy, 16)
            nc.gpsimd.memset(ident[:, :], 0.0).then_inc(s_pool, 1)
            nc.gpsimd.memset(mhalf[:, :], -0.5).then_inc(s_pool, 1)
            nc.gpsimd.memset(euler[:, :, :], 2.718281828459045)
            pool.wait_ge(s_pool, 2)
            nc.gpsimd.affine_select(out=ident[:, :], in_=ident[:, :], compare_op=ALU.not_equal, fill=1.0, base=0,
                                    pattern=[[-1, P]], channel_multiplier=1).then_inc(s_const, 1)

            pool.sem_inc(pchain, OFF)

            def rstd_stage(s):
                pool.wait_ge(var_ok, at(var_ok, s))
                nc.gpsimd.tensor_tensor(rstd[:, :], ve[:, :], mhalf[:, 0:TT], ALU.pow).then_inc(rstd_ok, 1)

            nc.gpsimd.memset(mask_f[:, :], 0.0).then_inc(s_pool, 1)
            nc.gpsimd.memset(tri[:, :, :], 0.0).then_inc(s_pool, 1)
            nc.gpsimd.iota(lanes[:, :], [[0, 1]], base=0, channel_multiplier=1).then_inc(lane_ok, 1)
            pool.wait_ge(s_pool, 4)
            nc.gpsimd.affine_select(out=mask_f[:, :], in_=mask_f[:, :], compare_op=ALU.is_ge, fill=NEG, base=0,
                                    pattern=[[-1, P]], channel_multiplier=1).then_inc(lane_ok, 1)
            nc.gpsimd.affine_select(out=tri[:, :, :], in_=tri[:, :, :], compare_op=ALU.is_ge, fill=1.0, base=0,
                                    pattern=[[-1, E1], [1, E1]], channel_multiplier=0).then_inc(lane_ok, 1)
            pool.dma_start(lut_sb[:, :], lut_b).then_inc(small_in, 16)
            pool.dma_start(lam_sb[:, :, :].rearrange("p a b -> p (a b)"), lam_v).then_inc(small_in, 16)
            pool.dma_start(gw_sb[:, :, :].rearrange("p a b -> p (a b)"), gatew).then_inc(small_in, 16)
            pool.wait_ge(small_in, 48)
            rstd_stage(0)
            rstd_stage(1)
            pool.wait_ge(raw_used, len(splits))
            pool.wait_ge(mod_ps, len(mods))
            pool.sem_inc(dec_out_1, 1)
            ffn_parts = ffn_idx.rearrange("p (b n) -> b p n", b=B)
            pool.dma_start(idx, ffn_parts[0]).then_inc(idx_in, 16)
            with pool.Fori(1, B) as b:
                for j in range(1, LUT):
                    pool.wait_ge(entry, at(entry, b - 1, j))
                    if j > 1:
                        pool.sem_inc(p_carrier, 1)
                        pool.wait_ge(pchain, at(pchain, b - 1, j - 2))
                    nc.gpsimd.tensor_tensor(decoded, decoded, entries(j), ALU.add).then_inc(pchain, 1)
                pool.wait_ge(pchain, at(pchain, b - 1, LUT - 2))
                pool.sem_inc(p_carrier, 1)
                pool.dma_start(ffn_w.rearrange("p (b n) -> b p n", b=B - 1)[b - 1], decoded).then_inc(dec_out, 16)
                pool.dma_start(idx, ffn_parts[b]).then_inc(idx_in, 16)
                pool.wait_ge(dec_out, b * 16)
                pool.sem_inc(dec_out_1, 1)
                rstd_stage(b + 1)

            if phases > 1:
                def load2(n, src, width):
                    pool.dma_start(raw[:, n % RING, 0:width], src).then_inc(raw2_in[n % RING], 16)

                pool.wait_ge(idx_in, 16 * B)
                for n in range(NB):
                    if n >= RING:
                        pool.wait_ge(raw2_used, n - RING + 1)
                    load2(n, ffn_w[:, n * PIECE:min((n + 1) * PIECE, FLAT_B)], min(PIECE, FLAT_B - n * PIECE))
                chain = [0]

                def link(ins):
                    chain[0] += 1
                    ins.then_inc(pchain2, 1)
                    pool.wait_ge(pchain2, chain[0])

                def split_flat(n, dst, lo, width, done):
                    link(nc.gpsimd.tensor_copy(dst[:, 0, lo:lo + width], raw[:, n % RING, 0:width]))
                    link(nc.gpsimd.tensor_tensor(dst[:, 1, lo:lo + width], raw[:, n % RING, 0:width],
                                                 dst[:, 0, lo:lo + width].bitcast(F32), ALU.subtract))
                    pool.sem_inc(done, 1)

                pool.wait_ge(raw2_used, NB)
                pool.wait_ge(proj_done, at(proj_done, B - 1, H0 - 1))
                load2(NB, w_c, 1024)
                load2(NB + 1, w_vp, 1024)
                later = [(w_gu, n * PIECE, min(PIECE, 2 * CC * EI - n * PIECE)) for n in range(NGU)]
                for b in range(B):
                    pool.wait_ge(xn_ok, at(xn_ok, B + b))
                    pool.wait_ge(x_store, at(x_store, b + 1, 15))
                    pool.dma_start(x_early, x_steps[B + b + 1]).then_inc(early_in, 16)
                    rstd_stage(B + b + 1)
                    if b == 0:
                        n = NB
                        pool.wait_ge(raw2_in[n % RING], 16 * (n // RING + 1))
                        q = raw[:, n % RING, :].rearrange("p (m c n) -> p m c n", m=4, c=CC)
                        for m in (0, 2):
                            link(nc.gpsimd.tensor_scalar(q[:, m], q[:, m], SCALE1, None, ALU.mult))
                    if b in (0, 1):
                        for m in (2 * b, 2 * b + 1):
                            for c in range(CC):
                                src = repeat(q[:, m, c].rearrange("p (h d) -> p h d", d=D1), 2, 4)
                                hi = WC[:, 0, m, c].rearrange("p (h r d) -> p h r d", r=4, d=D1)
                                lo = WC[:, 1, m, c].rearrange("p (h r d) -> p h r d", r=4, d=D1)
                                link(nc.gpsimd.tensor_copy(hi, src))
                                link(nc.gpsimd.tensor_tensor(lo, src, hi.bitcast(F32), ALU.subtract))
                        pool.sem_inc(wc_ok, 1)
                    if b == 2:
                        n = NB + 1
                        load2(NB + 2, *[w_gu[:, 0:PIECE], PIECE])
                        pool.wait_ge(raw2_in[n % RING], 16 * (n // RING + 1))
                        split_flat(n, WVP, 0, 1024, wc_ok)
                    if b >= 2:
                        k = b - 2
                        n = NB + 2 + k
                        if k + 1 < NGU:
                            load2(n + 1, w_gu[:, (k + 1) * PIECE:min((k + 2) * PIECE, 2 * CC * EI)],
                                  min(PIECE, 2 * CC * EI - (k + 1) * PIECE))
                        pool.wait_ge(raw2_in[n % RING], 16 * (n // RING + 1))
                        split_flat(n, WGU, k * PIECE, later[k][2], wd_ok)
            if phases > 2:
                pool.wait_ge(down_done, at(down_done, B - 1, FK - 1))
                for b in range(B + 1):
                    if b < B:
                        pool.wait_ge(xn_ok, at(xn_ok, 2 * B + b))
                        pool.wait_ge(x_store, at(x_store, B + b + 1, 15))
                        pool.dma_start(x_early, x_steps[2 * B + b + 1]).then_inc(early_in, 16)
                    if b:
                        pool.wait_ge(d_read, at(d_read, b - 1))
                        nc.gpsimd.tensor_tensor(square[:, :, :], y_t[:, :, :], y_t[:, :, :], ALU.mult
                                                ).then_inc(d_square, 1)
                        pool.wait_ge(rms_in, at(rms_in, b - 1))
                        nc.gpsimd.tensor_tensor(ssum[:, :], ssum[:, :], mhalf[:, :], ALU.pow).then_inc(rms_ok, 1)
                        pool.wait_ge(rms_ok, at(rms_ok, b - 1))
                        yv = y_t[:, :, :].rearrange("p t (h d) -> p t h d", h=H1)
                        rr = repeat(ssum[:, :].rearrange("p (t h) -> p t h", t=TT), 3, 16)
                        nc.gpsimd.tensor_tensor(yv, yv, rr, ALU.mult).then_inc(d_ok, 1)
                    if b == 0:
                        link(nc.gpsimd.memset(flat[0:E1, 0:EI], 1.0))
                        for cmp, base, sign in ((ALU.is_ge, 0, 1), (ALU.is_ge, I1 - 1, -1)):
                            link(nc.gpsimd.affine_select(out=flat[0:E1, 0:EI], in_=flat[0:E1, 0:EI], compare_op=cmp,
                                                         fill=0.0, base=base, pattern=[[sign, EI]],
                                                         channel_multiplier=-sign * I1))
                        link(nc.gpsimd.tensor_copy(sel, flat[0:E1, 0:EI]))
                    if 1 <= b <= 3:
                        lo = (b - 1) * PIECE
                        width = min(PIECE, EK * C - lo)
                        pool.dma_start(raw[:, b % 2, 0:width], w_d[:, lo:lo + width]).then_inc(idx_in, 16)
                        pool.wait_ge(idx_in, 16 * (B + b))
                        link(nc.gpsimd.tensor_copy(WDD[:, 0, lo:lo + width], raw[:, b % 2, 0:width]))
                        link(nc.gpsimd.tensor_tensor(WDD[:, 1, lo:lo + width], raw[:, b % 2, 0:width],
                                                     WDD[:, 0, lo:lo + width].bitcast(F32), ALU.subtract))
                        pool.sem_inc(wd_ok, 1)
                    if b < B:
                        rstd_stage(2 * B + b + 1)
            if phases > 3:
                def router(b):
                    pool.wait_ge(lg_sub, at(lg_sub, b))
                    nc.gpsimd.tensor_tensor(r_e[:, :, :], euler[:, :, :], r_l[:, :, :], ALU.pow).then_inc(lg_exp, 1)

                router(0)
                pool.wait_ge(x_copy, 32)
                with pool.Fori(0, B) as b:
                    pool.wait_ge(xn_ok, at(xn_ok, 3 * B + b))
                    pool.sem_inc(p_carrier, 1)
                    pool.wait_ge(x_store, at(x_store, 2 * B + b + 1, 15))
                    pool.sem_inc(p_carrier, 1)
                    pool.dma_start(x_early, x_steps[3 * B + b + 1]).then_inc(early_in, 16)
                    rstd_stage(b + 3 * B + 1)
                    router(b + 1)

        @block.scalar
        def _(act):
            act.sem_inc(s_exp, OFF)
            act.sem_inc(e_exp, OFF)
            act.sem_inc(t_ok, OFF)
            act.sem_inc(v1_ok, OFF)
            act.sem_inc(y_ev, OFF)
            act.dma_start(c_sb[:, 0], c_t0.rearrange("(c p) b -> p c b", p=P)).then_inc(c_in, 16)
            act.dma_start(c_sb[:, 1], c_t1.rearrange("(c p) b -> p c b", p=P)).then_inc(c_in, 16)
            act.wait_ge(c_in, 32)
            nc.scalar.activation(cs[:, :, :, :], c_sb[:, :, :, :], ACT.Silu).then_inc(c_silu, 1)

            def split(x):
                n = pieces.index(x)
                act.wait_ge(raw_in[n % RING], 16 * (n // RING + 1))
                act.activation(wa(x, 0), slot(n), ACT.Copy, scale=SCALE0 if x[0] == "q" else 1.0).then_inc(raw_hi, 1)

            def prep(s, tr_ps=tr_ps):
                act.wait_ge(xnt_full, at(xnt_full, s))
                act.wait_ge(mod_cp, at(mod_cp, s))
                for c in range(CC):
                    last = nc.scalar.activation(h_f[:, c, :], tr_ps[:, c * T:(c + 1) * T], ACT.Identity,
                                                bias=mod_now[:, c:c + 1], scale=mod_now[:, 2 + c:3 + c])
                last.then_inc(h_hi, 1)

            def finish(s, y_ps=y_ps, ready=None):
                if ready:
                    done, batch, last_one = ready
                    act.wait_ge(done, at(done, batch, last_one))
                else:
                    act.wait_ge(y_full, at(y_full, s))
                act.wait_ge(gate_ok, at(gate_ok, s))
                for c in range(CC):
                    last = nc.scalar.activation(y_t[:, c, :], y_ps[:, c * T:(c + 1) * T], ACT.Copy,
                                                scale=gate_now[:, c:c + 1])
                last.then_inc(y_ev, 1)

            split(("q", 0))
            prep(0)
            split(("k", 0))
            split(("v", 0))
            act.wait_ge(lam_ok, 1)
            nc.scalar.activation(lam_e[:, :], lam_e[:, :], ACT.Exp).then_inc(lam_exp, 1)

            def head_step(b, i, cur=True, prev=True):
                if cur:
                    act.wait_ge(qk_full, at(qk_full, b, i))
                    nc.scalar.activation(qk[:, i % 2, 0].rearrange("p m n -> p (m n)"), bank[i % 2][:, :], ACT.Copy
                                         ).then_inc(qk_hi, 1)
                if cur and i == H0 - 1:
                    prep(b + 1)
                n = i - 3
                if n >= 0 and cur or n < 0 and prev:
                    act.wait_ge(o_full, at(o_full, b, n))
                    act.wait_ge(proj_done, at(proj_done, b, n - 4))
                    nc.scalar.activation(ot[:, n % 4, 0, :], bank[4][:, 0:T], ACT.Copy).then_inc(o_hi, 1)
                n = i - 1
                if n >= 0 and cur or n < 0 and prev:
                    act.wait_ge(s_max, at(s_max, b, n))
                    for t in range(TT):
                        last = nc.scalar.activation(probs[:, n % 2, t, :], bank[2][:, t * T:(t + 1) * T], ACT.Exp,
                                                    bias=nmax[:, n % 2, t:t + 1], accum_out=den[:, n % 2, t:t + 1])
                    last.then_inc(s_exp, 1)
                if cur and i % 2 == 0:
                    act.wait_ge(v_full, at(v_full, b, i // 2))
                    nc.scalar.activation(v[:, i // 4 % 2, 0, i // 2 % 2, :], bank[5][:, :], ACT.Copy).then_inc(v_hi, 1)
                n = i - 2
                if n >= 0 and cur or n < 0 and prev:
                    act.wait_ge(pt_full, at(pt_full, b, n))
                    nc.scalar.activation(pt[:, n % 2, 0].rearrange("p t n -> p (t n)"), bank[3][:, :], ACT.Copy
                                         ).then_inc(pt_hi, 1)
                if i == 3 and prev:
                    finish(b - 1, ready=(proj_done, b - 1, H0 - 1))

            nc.scalar.activation(warm[:, :], mhalf[:, 0:1], ACT.Exp)
            for i in range(H0):
                head_step(0, i, prev=False)
                for x in late_pieces.get(i, []):
                    if x not in mods:
                        split(x)
            with act.Fori(1, B) as b:
                for i in range(H0):
                    head_step(b, i)
            for i in range(4):
                head_step(B, i, cur=False)

            if phases > 1:
                for n in range(NB):
                    lo, width = n * PIECE, min(PIECE, FLAT_B - n * PIECE)
                    act.wait_ge(raw2_in[n % RING], 16 * (n // RING + 1))
                    nc.scalar.activation(WB[:, 0, lo:lo + width], raw[:, n % RING, 0:width], ACT.Copy).then_inc(bc_hi, 1)
                def chunk(b, k, cur=True, prev=True):
                    if k == 2 and prev:
                        finish(b + B - 1, ready=(down_done, b - 1, FK - 1))
                    if k == 4 and cur:
                        prep(b + B + 1, bank[4])
                    if cur:
                        act.wait_ge(gu_full, at(gu_full, b, k))
                        act.wait_ge(gu_mul, at(gu_mul, b, k - 2))
                        nc.scalar.activation(sg[:, k % 2, :], bank[k % 4][:, 0:T], ACT.Silu).then_inc(gu_silu, 1)
                    n = k - 1
                    if n >= 0 and cur or n < 0 and prev:
                        act.wait_ge(gu_mul, at(gu_mul, b, n))
                        act.wait_ge(down_done, at(down_done, b, last_user(n % FK, 4, FK) - (n < 0) * FK))
                        nc.scalar.activation(gu_slot(n % FK, 0), guf[:, n % 2, :], ACT.Copy).then_inc(gu_hi, 1)

                for k in range(FK):
                    chunk(0, k, prev=False)
                with act.Fori(1, B) as b:
                    for k in range(FK):
                        chunk(b, k)
                for k in range(3):
                    chunk(B, k, cur=False)

            if phases > 2:
                nc.scalar.activation(warm[:, :], mhalf[:, 0:1], ACT.Exp)
                def narrow(b, g, m):
                    act.wait_ge(c_full, at(c_full, b, 2 * g + m))
                    nc.scalar.activation(qk[:, m, 0].rearrange("p x n -> p (x n)"), narrow_ps(g, m)[:, :], ACT.Copy
                                         ).then_inc(c_hi, 1)

                def head_step(b, i, cur=True, prev=True, following=True):
                    n = i - 2
                    if n >= 0 and cur or n < 0 and prev:
                        act.wait_ge(t_full, at(t_full, b, n))
                        act.wait_ge(av_done, at(av_done, b, n - 2))
                        nc.scalar.activation(ptf[:, n % 2, :], bank[4][:, 0:384], ACT.Copy).then_inc(t_ok, 1)
                    if i == 2 and cur:
                        act.wait_ge(v1_full, at(v1_full, b))
                        act.wait_ge(av_done, at(av_done, b - 1, H1 - 1))
                        nc.scalar.activation(v1[:, :, :].rearrange("p t n -> p (t n)"), tr_ps[:, :], ACT.Copy
                                             ).then_inc(v1_ok, 1)
                    if cur and i in NARROW_AT:
                        narrow(b, *NARROW_AT[i])
                    if i == 15 and following:
                        narrow(b + 1, 0, 1)
                    if i == PREP_AT + 2 and cur:
                        prep(b + 2 * B + 1)
                    if cur:
                        act.wait_ge(e_max, at(e_max, b, i))
                        for t in range(TT):
                            keys = (t + 1) * P
                            ps = bank[(1, 3)[i % 2] if t else (2, 5)[i % 2]]
                            for m in range(2):
                                last = nc.scalar.activation(pc[:, i % 2, m, t * P:t * P + keys],
                                                            ps[:, m * keys:(m + 1) * keys], ACT.Exp,
                                                            bias=nmax1[:, i % 2, t, m:m + 1],
                                                            accum_out=den1[:, i % 2, t, m:m + 1])
                        last.then_inc(e_exp, 1)
                    if i == DIFF_AT + 2 and prev:
                        finish(b + 2 * B - 1, tr_ps)
                    if i == 13 and following:
                        narrow(b + 1, 0, 0)
                    if i == DIFF_AT and prev:
                        act.wait_ge(dt_full, at(dt_full, b - 1))
                        nc.scalar.activation(dr[:, 0].rearrange("p c n -> p (c n)"), tr_ps[:, :], ACT.Copy
                                             ).then_inc(dr_hi, 1)

                narrow(0, 0, 0)
                narrow(0, 0, 1)
                for i in range(H1):
                    head_step(0, i, prev=False)
                with act.Fori(1, B - 1) as b:
                    for i in range(H1):
                        head_step(b, i)
                for i in range(H1):
                    head_step(B - 1, i, following=False)
                for i in range(DIFF_AT + 4):
                    head_step(B, i, cur=False, following=False)

            if phases > 3:
                def chunk(b, k, cur=True, prev=True):
                    if k == 1 and cur:
                        act.wait_ge(cbt_full, at(cbt_full, b))
                        act.wait_ge(bc_full, at(bc_full, b - 1, EK - 1))
                        nc.scalar.activation(comb_r[:, 0], bank[3][0:E1, 0:T], ACT.Copy).then_inc(cb_hi, 1)
                    if k == 3 and prev:
                        finish(b + 3 * B - 1, ready=(edown, b - 1, EK - 1))
                    if k == 6 and cur:
                        prep(b + 3 * B + 1)
                    if cur:
                        act.wait_ge(eg_full, at(eg_full, b, k))
                        act.wait_ge(eg_up, at(eg_up, b, k - 2 + (k == 0)))
                        nc.scalar.activation(sg[:, k % 2, :], bank[k % 3][:, 0:T], ACT.Silu).then_inc(eg_silu, 1)
                    n = k - 2
                    if n >= 0 and cur or n < 0 and prev:
                        act.wait_ge(eg_mul, at(eg_mul, b, n))
                        act.wait_ge(edown, at(edown, b, last_user(n % EK, 4, EK) - (n < 0) * EK))
                        nc.scalar.activation(gu_slot(n % EK, 0), gated(n % EK), ACT.Copy).then_inc(eg_hi, 1)

                for k in range(EK):
                    chunk(0, k, prev=False)
                with act.Fori(1, B) as b:
                    for k in range(EK):
                        chunk(b, k)
                for k in range(4):
                    chunk(B, k, cur=False)

        @block.vector
        def _(dve):
            seq = [0]

            def link(ins):
                seq[0] += 1
                ins.then_inc(dchain, 1)
                dve.wait_ge(dchain, seq[0])

            for s_ in (qk_lo, pt_lo, o_lo, v_lo, x_moved, d_read, entry, gu_lo, eg_lo, gu_mul, eg_mul, eg_up, c_ok, cb_lo):
                dve.sem_inc(s_, OFF)
            link(nc.vector.memset(mod[:, STEPS:, :], 0.0))
            def table(l):
                dve.wait_ge(mod_ps, 3 * (l + 1))
                part = mod[:, 2 * B * l:2 * B * (l + 1), :]
                src = (bank[0], tr_ps)[l][:, 0:96].rearrange("p (u k b) -> p u b k", u=2, k=6)
                for u in range(2):
                    last = nc.vector.tensor_copy(part[:, B * u:B * (u + 1), :], src[:, u])
                link(last)
                link(nc.vector.tensor_scalar(part[:, :, 2:4], part[:, :, 2:4], 1.0, None, ALU.add))
                gt = work[:, 1024:1024 + 4 * B].rearrange("p (s k) -> p s k", k=2)
                ga = part[:, :, 4:6]
                link(nc.vector.tensor_scalar(gt, ga, 0.0, 2.0, ALU.is_ge, ALU.mult))
                link(nc.vector.tensor_scalar(gt, gt, -1.0, None, ALU.add))
                link(nc.vector.tensor_tensor(ga, ga, gt, ALU.mult))
                link(nc.vector.tensor_scalar(ga, ga, 0.25, None, ALU.max))
                link(nc.vector.tensor_tensor(ga, ga, gt, ALU.mult))

            table(0)
            def prep_stats(s, x):
                n = [0]

                def step_link(ins):
                    n[0] += 1
                    ins.then_inc(dcom, 1)
                    dve.wait_ge(dcom, s * 2 + n[0])

                nc.vector.tensor_copy(mod_now[:, :], mod[:, s, 0:4]).then_inc(mod_cp, 1)
                for t in range(TT):
                    last = nc.vector.bn_stats(stats[:, t, :], x[:, t, :])
                step_link(last)
                dve.sem_inc(carrier, 1)
                for t in range(TT):
                    last = nc.vector.bn_aggr(mv[:, t, :], stats[:, t, :])
                step_link(last)
                nc.vector.tensor_scalar(ve[:, :], mv[:, :, 1], EPS, None, ALU.add).then_inc(var_ok, 1)

            def prep_apply(s, x, xn=xn):
                if xn is x_out:
                    dve.wait_ge(x_store, at(x_store, s - 2, 15))
                    dve.sem_inc(carrier, 1)
                dve.wait_ge(rstd_ok, at(rstd_ok, s))
                for t in range(TT):
                    last = nc.vector.tensor_scalar(xn[:, t, :], x[:, t, :], mv[:, t, 0:1], rstd[:, t:t + 1],
                                                   ALU.subtract, ALU.mult)
                last.then_inc(xn_ok, 1)

            def prep(s, x):
                prep_stats(s, x)
                prep_apply(s, x)

            def prep_low(s, free=None):
                dve.wait_ge(h_hi, at(h_hi, s))
                if free:
                    dve.wait_ge(free[0], at(*free))
                    dve.sem_inc(carrier, 1)
                nc.vector.tensor_copy(h[:, 0], h_f[:, :, :]).then_inc(h_high, 1)
                dve.wait_ge(h_high, at(h_high, s))
                nc.vector.tensor_tensor(h[:, 1], h_f[:, :, :], h[:, 0].bitcast(F32), ALU.subtract).then_inc(h_ok, 1)

            def gate(s):
                dve.wait_ge(y_ev, at(y_ev, s - 1))
                nc.vector.tensor_copy(gate_now[:, :], mod[:, s, 4:6]).then_inc(gate_ok, 1)

            def finish(s, late=False):
                dve.wait_ge(yt_full, at(yt_full, s))
                if late:
                    dve.wait_ge(x_load, at(x_load, s - 1, 15))
                    dve.sem_inc(carrier, 1)
                    dve.wait_ge(x_store, at(x_store, s - 1, 15))
                    dve.sem_inc(carrier, 1)
                nc.vector.tensor_tensor(x_out[:, :, :], x_cur[:, :, :],
                                        tr_ps[:, :].rearrange("p (t n) -> p t n", t=TT), ALU.add).then_inc(dcom2, 1)
                dve.wait_ge(dcom2, at(dcom2, s))
                nc.vector.tensor_copy(x_cur[:, :, :], x_next[:, :, :]).then_inc(x_moved, 1)

            def split(x):
                n = splits.index(x)
                dve.wait_ge(raw_hi, n + 1)
                nc.vector.scalar_tensor_tensor(out=wa(x, 1), in0=slot(pieces.index(x)),
                                               scalar=SCALE0 if x[0] == "q" else 1.0, in1=wa(x, 0).bitcast(F32),
                                               op0=ALU.mult, op1=ALU.subtract).then_inc(raw_used, 1)

            dve.wait_ge(x_first, 32)
            prep(0, x_cur)
            split(("q", 0))
            prep_low(0)
            split(("k", 0))
            split(("v", 0))
            dve.wait_ge(lane_ok, 3)
            for x in range(2):
                last = nc.vector.tensor_scalar(lane_bit[:, x:x + 1], lanes[:, :], (16, 8)[x], None, ALU.bitwise_and)
            link(last)
            nc.vector.tensor_scalar(low_q[:, :], lane_bit[:, 0:1], -1.0 / 16, None, ALU.mult)
            nc.vector.tensor_scalar(low_k[:, :], lane_bit[:, 1:2], -1.0 / 8, None, ALU.mult)
            nc.vector.tensor_copy(mask_r[:, :], mask_f[:, :])
            dve.wait_ge(s_const, 1)
            link(nc.vector.tensor_copy(ident_r[:, :], ident[:, :]))
            dve.wait_ge(small_in, 48)
            link(nc.vector.tensor_tensor(lam_p[:, :, :], lam_sb[:, 0::2, :], lam_sb[:, 1::2, :], ALU.mult))
            nc.vector.tensor_reduce(lam_e[:, :], lam_p[:, :, :], AX, ALU.add).then_inc(lam_ok, 1)
            dve.wait_ge(lam_exp, 1)
            link(nc.vector.tensor_tensor(nlam[:, :], lam_e[:, 1:2], lam_e[:, 0:1], ALU.subtract))
            link(nc.vector.tensor_scalar(nlam[:, :], nlam[:, :], -LAMBDA_INIT, None, ALU.add))

            def head_step(b, i, cur=True, prev=True):
                if cur:
                    dve.wait_ge(qk_hi, at(qk_hi, b, i))
                    nc.vector.tensor_tensor(qk[:, i % 2, 1].rearrange("p m n -> p (m n)"), bank[i % 2][:, :],
                                            qk[:, i % 2, 0].rearrange("p m n -> p (m n)").bitcast(F32),
                                            ALU.subtract).then_inc(qk_lo, 1)
                if cur and i == H0 - 1:
                    prep_low(b + 1)
                n = i - 1
                if n >= 0 and cur or n < 0 and prev:
                    dve.wait_ge(s_full, at(s_full, b, n))
                    nc.vector.tensor_reduce(nmax[:, n % 2, :], bank[2][:, :].rearrange("p (t n) -> p t n", t=TT),
                                            AX, ALU.max, negate=True).then_inc(s_max, 1)
                n = i - 3
                if n >= 0 and cur or n < 0 and prev:
                    dve.wait_ge(o_hi, at(o_hi, b, n))
                    nc.vector.tensor_tensor(ot[:, n % 4, 1, :], bank[4][:, 0:T], ot[:, n % 4, 0, :].bitcast(F32),
                                            ALU.subtract).then_inc(o_lo, 1)
                if cur and prev and 2 <= i < 2 + LUT // 2:
                    if i == 2:
                        dve.wait_ge(idx_in, b * 16)
                        dve.sem_inc(carrier, 1)
                    for j in (2 * i - 4, 2 * i - 3):
                        if j == 0:
                            dve.wait_ge(dec_out_1, b)
                            dve.sem_inc(carrier, 1)
                        if j > 2:
                            dve.wait_ge(pchain, at(pchain, b - 1, j - 3))
                            dve.sem_inc(carrier, 1)
                        nc.vector.tensor_scalar(entries(j), idx, float(j), lut_sb[:, j:j + 1], ALU.is_equal, ALU.mult
                                                ).then_inc(entry, 1)
                if cur and i % 2 == 0:
                    dve.wait_ge(v_hi, at(v_hi, b, i // 2))
                    nc.vector.tensor_tensor(v[:, i // 4 % 2, 1, i // 2 % 2, :], bank[5][:, :],
                                            v[:, i // 4 % 2, 0, i // 2 % 2, :].bitcast(F32), ALU.subtract
                                            ).then_inc(v_lo, 1)
                n = i - 1
                if n >= 0 and cur or n < 0 and prev:
                    dve.wait_ge(s_exp, at(s_exp, b, n))
                    nc.vector.reciprocal(rden[:, n % 2, :], den[:, n % 2, :]).then_inc(s_rden, 1)
                    dve.wait_ge(s_rden, at(s_rden, b, n))
                    for t in range(TT):
                        last = nc.vector.tensor_scalar(probs[:, n % 2, t, :], probs[:, n % 2, t, :],
                                                       rden[:, n % 2, t:t + 1], None, ALU.mult)
                    last.then_inc(s_norm, 1)
                n = i - 2
                if n >= 0 and cur or n < 0 and prev:
                    dve.wait_ge(pt_hi, at(pt_hi, b, n))
                    nc.vector.tensor_tensor(pt[:, n % 2, 1].rearrange("p t n -> p (t n)"), bank[3][:, :],
                                            pt[:, n % 2, 0].rearrange("p t n -> p (t n)").bitcast(F32),
                                            ALU.subtract).then_inc(pt_lo, 1)
                if i == 1 and prev:
                    gate(b - 1)
                if i == 5 and prev:
                    finish(b - 1)
                if cur and i == 12:
                    dve.wait_ge(x_load, at(x_load, b - 1, 15))
                    prep_stats(b + 1, x_next)
                if cur and i == 13:
                    prep_apply(b + 1, x_next)

            for i in range(H0):
                head_step(0, i, prev=False)
                for x in late_pieces.get(i, []):
                    if x not in mods:
                        split(x)
                if i == 10:
                    table(1)
            with dve.Fori(1, B) as b:
                for i in range(H0):
                    head_step(b, i)
            for i in range(6):
                head_step(B, i, cur=False)

            if phases > 1:
                for n in range(NB):
                    lo, width = n * PIECE, min(PIECE, FLAT_B - n * PIECE)
                    dve.wait_ge(bc_hi, n + 1)
                    nc.vector.tensor_tensor(WB[:, 1, lo:lo + width], raw[:, n % RING, 0:width],
                                            WB[:, 0, lo:lo + width].bitcast(F32), ALU.subtract).then_inc(raw2_used, 1)
                def chunk(b, k, cur=True, prev=True):
                    if k == FK - 1 and cur:
                        prep_low(b + B + 1, free=(gu_full, b, FK - 1))
                    if cur:
                        dve.wait_ge(gu_lo, at(gu_lo, b, k - 2))
                        dve.wait_ge(gu_silu, at(gu_silu, b, k))
                        nc.vector.tensor_tensor(guf[:, k % 2, :], sg[:, k % 2, :], bank[k % 4][:, T:2 * T], ALU.mult
                                                ).then_inc(gu_mul, 1)
                    n = k - 1
                    if n >= 0 and cur or n < 0 and prev:
                        dve.wait_ge(gu_hi, at(gu_hi, b, n))
                        nc.vector.tensor_tensor(gu_slot(n % FK, 1), guf[:, n % 2, :],
                                                gu_slot(n % FK, 0).bitcast(F32), ALU.subtract).then_inc(gu_lo, 1)
                    if k == 0 and prev:
                        gate(b + B - 1)
                    if k == 3 and prev:
                        finish(b + B - 1, late=True)
                    if k == 1 and cur:
                        dve.wait_ge(early_in, at(early_in, b, 15))
                        dve.sem_inc(carrier, 1)
                        prep_stats(b + B + 1, x_early)
                    if k == 2 and cur:
                        prep_apply(b + B + 1, x_early, xn_early)

                for k in range(FK):
                    chunk(0, k, prev=False)
                with dve.Fori(1, B) as b:
                    for k in range(FK):
                        chunk(b, k)
                for k in range(4):
                    chunk(B, k, cur=False)

            if phases > 2:
                def narrow(b, g, m):
                    dve.wait_ge(c_hi, at(c_hi, b, 2 * g + m))
                    for x in range(2):
                        last = nc.vector.scalar_tensor_tensor(
                            out=v[:, g % 2, m, x, 0:T], in0=qk[:, m, 0, x, :].bitcast(F32),
                            scalar=(low_q, low_k)[x][:, 0:1], in1=narrow_ps(g, m)[:, x * T:(x + 1) * T],
                            op0=ALU.mult, op1=ALU.add)
                    last.then_inc(c_ok, 1)

                def output(b, stage):
                    if stage == 0:
                        dve.wait_ge(av_done, at(av_done, b, H1 - 1))
                        r1 = repeat(rall_old[:, :, :].rearrange("p h t -> p t h"), 3, 16)
                        nc.vector.tensor_tensor(y_t[:, :, :].rearrange("p t (h d) -> p t h d", h=H1),
                                                y_ps[:, :].rearrange("p (t h d) -> p t h d", t=TT, h=H1),
                                                r1, ALU.mult).then_inc(d_read, 1)
                    else:
                        dve.wait_ge(d_square, at(d_square, b))
                        nc.vector.tensor_reduce(ssum[:, :], square[:, :, :].rearrange("p t (h d) -> p (t h) d", h=H1),
                                                AX, ALU.add).then_inc(d_chain, 1)
                        dve.wait_ge(d_chain, at(d_chain, b))
                        dve.sem_inc(carrier, 1)
                        cc = (1.0 - LAMBDA_INIT) ** 2
                        nc.vector.tensor_scalar(ssum[:, :], ssum[:, :], 1.0 / (16 * cc), EPS / cc, ALU.mult, ALU.add
                                                ).then_inc(rms_in, 1)

                def head_step(b, i, cur=True, prev=True, following=True):
                    if cur:
                        dve.wait_ge(e_full, at(e_full, b, i))
                        for t in range(TT):
                            keys = (t + 1) * P
                            ps = bank[(1, 3)[i % 2] if t else (2, 5)[i % 2]]
                            last = nc.vector.tensor_reduce(nmax1[:, i % 2, t, :],
                                                           ps[:, 0:2 * keys].rearrange("p (m n) -> p m n", m=2),
                                                           AX, ALU.max, negate=True)
                        last.then_inc(e_max, 1)
                    if i == DIFF_AT + 1 and prev:
                        dve.wait_ge(dr_hi, at(dr_hi, b - 1))
                        nc.vector.tensor_tensor(dr[:, 1].rearrange("p c n -> p (c n)"), tr_ps[:, :],
                                                dr[:, 0].rearrange("p c n -> p (c n)").bitcast(F32), ALU.subtract
                                                ).then_inc(dr_lo, 1)
                    if i == DIFF_AT + 4 and prev:
                        finish(b + 2 * B - 1, late=True)
                    if i == 14 and following:
                        narrow(b + 1, 0, 0)
                    if i == 1 and prev:
                        nc.vector.tensor_copy(rall_old[:, :, :], rall[:, :, :, 0]).then_inc(r_moved, 1)
                        dve.wait_ge(r_moved, at(r_moved, b - 1))
                    n = i - 1
                    if n >= 0 and cur or n < 0 and prev:
                        dve.wait_ge(e_exp, at(e_exp, b, n))
                        nc.vector.reciprocal(rall[:, n % H1, :, :], den1[:, n % 2, :, :]).then_inc(e_rec, 1)
                        dve.wait_ge(e_rec, at(e_rec, b, n))
                        nc.vector.scalar_tensor_tensor(out=ratio[:, n % 2, :], in0=den1[:, n % 2, :, 0],
                                                       scalar=nlam[:, 0:1], in1=rall[:, n % H1, :, 1], op0=ALU.mult,
                                                       op1=ALU.mult).then_inc(e_rat, 1)
                        dve.wait_ge(e_rat, at(e_rat, b, n))
                        for t in range(TT):
                            lo, hi = t * P, t * P + (t + 1) * P
                            last = nc.vector.scalar_tensor_tensor(
                                out=pc[:, n % 2, 0, lo:hi], in0=pc[:, n % 2, 1, lo:hi],
                                scalar=ratio[:, n % 2, t:t + 1], in1=pc[:, n % 2, 0, lo:hi], op0=ALU.mult, op1=ALU.add)
                        last.then_inc(e_diff, 1)
                    if cur and i in NARROW_AT:
                        narrow(b, *NARROW_AT[i])
                    if i == 2 and prev:
                        output(b - 1, 0)
                        gate(b + 2 * B - 1)
                    if i == 4 and prev:
                        output(b - 1, 1)
                    if i == PREP_AT - 1 and cur:
                        dve.wait_ge(early_in, at(early_in, b + B, 15))
                        dve.sem_inc(carrier, 1)
                        prep_stats(b + 2 * B + 1, x_early)
                    if i == PREP_AT and cur:
                        prep_apply(b + 2 * B + 1, x_early, xn_early)
                    if i == PREP_AT + 2 and cur:
                        prep_low(b + 2 * B + 1)
                    if i == 15 and following:
                        narrow(b + 1, 0, 1)

                narrow(0, 0, 0)
                narrow(0, 0, 1)
                for i in range(H1):
                    head_step(0, i, prev=False)
                with dve.Fori(1, B - 1) as b:
                    for i in range(H1):
                        head_step(b, i)
                for i in range(H1):
                    head_step(B - 1, i, following=False)
                for i in range(DIFF_AT + 5):
                    head_step(B, i, cur=False, following=False)

            if phases > 3:
                link(nc.vector.memset(comb[:, :, :], 0.0))

                def router_logits(b):
                    dve.wait_ge(lg_full, at(lg_full, b))
                    nc.vector.tensor_reduce(r_max[:, :], bank[3][:, 0:TT * E1].rearrange("p (t e) -> p t e", t=TT), AX,
                                            ALU.max).then_inc(lg_max, 1)
                    dve.wait_ge(lg_max, at(lg_max, b))
                    nc.vector.tensor_tensor(r_l[:, :, :], bank[3][:, 0:TT * E1].rearrange("p (t e) -> p t e", t=TT),
                                            repeat(r_max[:, :], 2, E1), ALU.subtract).then_inc(lg_sub, 1)

                def router_weights(b):
                    dve.wait_ge(lg_exp, at(lg_exp, b))
                    n = [0]

                    def step_link(ins):
                        ins.then_inc(dr_chain, 1)
                        dve.wait_ge(dr_chain, at(dr_chain, b, n[0]))
                        n[0] += 1

                    ej = repeat(r_e[:, :, :], 2, E1)
                    ee = repeat(r_e[:, :, :], 3, E1)
                    tr = repeat(tri[:, :, :], 1, TT)
                    nc.vector.tensor_tensor(r_gt, ej, ee, ALU.is_gt)
                    step_link(nc.vector.tensor_tensor(r_eq, ej, ee, ALU.is_equal))
                    step_link(nc.vector.tensor_tensor(r_eq, r_eq, tr, ALU.mult))
                    step_link(nc.vector.tensor_tensor(r_gt, r_gt, r_eq, ALU.add))
                    step_link(nc.vector.tensor_reduce(r_rank[:, :, :], r_gt, AX, ALU.add))
                    step_link(nc.vector.scalar_tensor_tensor(out=r_w[:, :, :], in0=r_rank[:, :, :], scalar=2.0,
                                                             in1=r_e[:, :, :], op0=ALU.is_lt, op1=ALU.mult))
                    step_link(nc.vector.tensor_reduce(r_sum[:, :], r_w[:, :, :], AX, ALU.add))
                    nc.vector.reciprocal(r_sum[:, :], r_sum[:, :]).then_inc(r_rec, 1)
                    dve.wait_ge(r_rec, at(r_rec, b))
                    for t in range(TT):
                        last = nc.vector.tensor_scalar(comb[:, t, 0:E1], r_w[:, t, :], r_sum[:, t:t + 1], None, ALU.mult)
                    last.then_inc(cb_ok, 1)

                def chunk(b, k, cur=True, prev=True):
                    if k == 1 and cur:
                        dve.wait_ge(cb_hi, at(cb_hi, b))
                        nc.vector.tensor_tensor(comb_r[:, 1], bank[3][0:E1, 0:T], comb_r[:, 0].bitcast(F32), ALU.subtract
                                                ).then_inc(cb_lo, 1)
                    if k == EK - 1 and cur:
                        prep_low(b + 3 * B + 1, free=(eg_full, b, EK - 1))
                    if cur:
                        dve.wait_ge(eg_silu, at(eg_silu, b, k))
                        dve.wait_ge(eg_lo, at(eg_lo, b, last_user(k, 4, EK)))
                        nc.vector.tensor_tensor(gated(k), sg[:, k % 2, :], bank[k % 3][:, T:2 * T], ALU.mult
                                                ).then_inc(eg_up, 1)
                    n = k - 1
                    if n >= 0 and cur or n < 0 and prev:
                        dve.wait_ge(bc_full, at(bc_full, b, n))
                        dve.sem_inc(carrier, 1)
                        dve.wait_ge(eg_up, at(eg_up, b, n))
                        nc.vector.tensor_tensor(gated(n % EK), gated(n % EK), bank[4 + n % EK % 2][:, 0:T], ALU.mult
                                                ).then_inc(eg_mul, 1)
                    n = k - 2
                    if n >= 0 and cur or n < 0 and prev:
                        dve.wait_ge(eg_hi, at(eg_hi, b, n))
                        nc.vector.tensor_tensor(gu_slot(n % EK, 1), gated(n % EK),
                                                gu_slot(n % EK, 0).bitcast(F32), ALU.subtract).then_inc(eg_lo, 1)
                    if k == 1 and prev:
                        gate(b + 3 * B - 1)
                    if k == 4 and prev:
                        finish(b + 3 * B - 1, late=True)
                    if k == 3 and cur:
                        dve.wait_ge(early_in, at(early_in, b + 2 * B, 15))
                        dve.sem_inc(carrier, 1)
                        prep_stats(b + 3 * B + 1, x_early)
                    if k == 4 and cur:
                        prep_apply(b + 3 * B + 1, x_early, xn_early)
                    if k == 7 and cur:
                        router_logits(b + 1)
                    if k == 9 and cur:
                        router_weights(b + 1)

                router_logits(0)
                router_weights(0)
                for k in range(EK):
                    chunk(0, k, prev=False)
                with dve.Fori(1, B) as b:
                    for k in range(EK):
                        chunk(b, k)
                for k in range(5):
                    chunk(B, k, cur=False)

        @block.tensor
        def _(pe):
            for s_ in (proj_done, av_done, down_done, edown, bc_full):
                pe.sem_inc(s_, OFF)
            pe.wait_ge(c_silu, 1)

            def modulation(x):
                n = pieces.index(x)
                l, ps = int(x[0]), (bank[0], tr_ps)[int(x[0])]
                pe.wait_ge(raw_in[n % RING], 16 * (n // RING + 1))
                for j in range(4):
                    k = 4 * x[1] + j
                    for c in range(CC):
                        last = nc.tensor.matmul(ps[:, 8 * k:8 * k + 8], slot(n)[:, c, P * j:P * (j + 1)],
                                                cs[:, l, c, :], start=(c == 0), stop=(c == CC - 1))
                last.then_inc(mod_ps, 1)

            for x in first_pieces[0:3]:
                modulation(x)

            def three(ps, w, m, n, first=True, last=True, **kw):
                parts = [(0, 0), (0, 1), (1, 0)]
                for j in range(n):
                    for a, (wp, mp) in enumerate(parts):
                        ins = nc.tensor.matmul(ps, w(j, wp), m(j, mp), start=(first and j == 0 and a == 0),
                                               stop=(last and j == n - 1 and a == 2), **kw)
                return ins

            def prep(s, xn=xn, tr_ps=tr_ps):
                pe.wait_ge(xn_ok, at(xn_ok, s))
                if tr_ps is bank[6]:
                    pe.wait_ge(x_moved, at(x_moved, s - 2))
                else:
                    pe.wait_ge(h_hi, at(h_hi, s - 1))
                for c in range(CC):
                    for t in range(TT):
                        last = nc.tensor.transpose(tr_ps[:, c * T + t * P:c * T + (t + 1) * P],
                                                   xn[:, t, c * P:(c + 1) * P], ident[:, :])
                last.then_inc(xnt_full, 1)

            def finish(s):
                pe.wait_ge(y_ev, at(y_ev, s))
                pe.wait_ge(h_hi, at(h_hi, s + 1))
                for t in range(TT):
                    for c in range(CC):
                        last = nc.tensor.transpose(tr_ps[:, t * C + c * P:t * C + (c + 1) * P],
                                                   y_t[:, c, t * P:(t + 1) * P], ident[:, :])
                last.then_inc(yt_full, 1)

            pe.wait_ge(s_const, 1)
            prep(0)

            def head_step(b, i, cur=True, prev=True):
                if cur:
                    if i == 0:
                        pe.wait_ge(h_ok, at(h_ok, b))
                    if not prev and i % 4 == 0:
                        pe.wait_ge(raw_used, splits.index(("v", i // 4)) + 1)
                    pe.wait_ge(qk_lo, at(qk_lo, b, i - 2))
                    for m in range(2):
                        last = three(bank[i % 2][:, m * T:(m + 1) * T],
                                     lambda j, a: WQK[:, a, j, m, i * P:(i + 1) * P],
                                     lambda j, a: h[:, a, j, :], CC)
                    last.then_inc(qk_full, 1)
                n = i - 1
                if n >= 0 and cur or n < 0 and prev:
                    pe.wait_ge(qk_lo, at(qk_lo, b, n))
                    pe.wait_ge(s_exp, at(s_exp, b, n - 1))
                    for q in range(TT):
                        last = three(bank[2][:, q * T:(q + 1) * T],
                                     lambda j, a: qk[:, n % 2, a, 0, q * P:(q + 1) * P],
                                     lambda j, a: qk[:, n % 2, a, 1, :], 1)
                    last.then_inc(s_full, 1)
                n = i - 3
                if n >= 0 and cur or n < 0 and prev:
                    pe.wait_ge(pt_lo, at(pt_lo, b, n))
                    pe.wait_ge(o_lo, at(o_lo, b, n - 1))
                    if n % 4 == 0:
                        pe.wait_ge(v_lo, at(v_lo, b, 2 * (n // 4) + 1))
                    three(bank[4][:, 0:T],
                          lambda j, a: v[:, n // 4 % 2, a, j, (n % 4) * P:(n % 4 + 1) * P],
                          lambda j, a: pt[:, n % 2, a, j, :], TT).then_inc(o_full, 1)
                if cur and i % 2 == 0:
                    g, t = i // 4, i // 2 % 2
                    pe.wait_ge(v_lo, at(v_lo, b, i // 2 - 1))
                    three(bank[5][:, :], lambda j, a: h[:, a, j, t * P:(t + 1) * P],
                          lambda j, a: WV[:, a, j, 512 * g:512 * (g + 1)], CC).then_inc(v_full, 1)
                n = i - 2
                if n >= 0 and cur or n < 0 and prev:
                    pe.wait_ge(s_norm, at(s_norm, b, n))
                    pe.wait_ge(pt_lo, at(pt_lo, b, n - 1))
                    for k in range(TT):
                        for q in range(TT):
                            last = nc.tensor.transpose(bank[3][:, k * T + q * P:k * T + (q + 1) * P],
                                                       probs[:, n % 2, q, k * P:(k + 1) * P], ident[:, :])
                    last.then_inc(pt_full, 1)
                n = i - 4
                if n >= 0 and cur or n < 0 and prev:
                    pe.wait_ge(o_lo, at(o_lo, b, n))
                    if not prev and n % 4 == 0:
                        pe.wait_ge(raw_used, splits.index(("o", n // 4)) + 1)
                    if n == 0:
                        pe.wait_ge(y_ev, at(y_ev, b - 1))
                    for c in range(CC):
                        last = three(y_ps[:, c * T:(c + 1) * T],
                                     lambda j, a: WO[:, a, n % H0, c * P:(c + 1) * P],
                                     lambda j, a: ot[:, n % 4, a, :], 1, first=(n == 0 and c == 0),
                                     last=(n == -1), skip_group_check=True)
                    last.then_inc(proj_done, 1)
                if i == 4 and prev:
                    finish(b - 1)
                if i == 14 and cur:
                    prep(b + 1)

            for i in range(H0):
                head_step(0, i, prev=False)
                for x in late_pieces.get(i, []):
                    if x in mods:
                        if x == ("1", 0):
                            pe.wait_ge(h_hi, at(h_hi, 0))
                        modulation(x)
            with pe.Fori(1, B) as b:
                for i in range(H0):
                    head_step(b, i)
            for i in range(5):
                head_step(B, i, cur=False)

            if phases > 1:
                pe.wait_ge(raw2_used, NB)
                def down(b, n):
                    pe.wait_ge(gu_lo, at(gu_lo, b, n))
                    if n == 0:
                        pe.wait_ge(y_ev, at(y_ev, b + B - 1))
                    for c in range(CC):
                        last = three(y_ps[:, c * T:(c + 1) * T], lambda j, a: WD[:, a, n % FK, c * P:(c + 1) * P],
                                     lambda j, a: gu_slot(n % FK, a), 1, first=(n == 0 and c == 0),
                                     last=(n % FK == FK - 1), skip_group_check=True)
                    last.then_inc(down_done, 1)

                def chunk(b, k, cur=True, prev=True):
                    if cur:
                        if k == 0:
                            pe.wait_ge(h_ok, at(h_ok, b + B))
                        pe.wait_ge(gu_mul, at(gu_mul, b, last_user(k, 4, FK)))
                        for x, w in enumerate((WG, WU)):
                            last = three(bank[k % 4][:, x * T:(x + 1) * T],
                                         lambda j, a: w[:, a, j, k * P:(k + 1) * P], lambda j, a: h[:, a, j, :], CC)
                        last.then_inc(gu_full, 1)
                    if k < 2 and prev:
                        down(b, k - 2)
                    if k == 3 and prev:
                        finish(b + B - 1)
                    if k == 3 and cur:
                        prep(b + B + 1, xn_early, bank[4])
                    if k == 3 and cur:
                        down(b, 0)
                    if k >= 3 and cur:
                        down(b, k - 2)

                for k in range(FK):
                    chunk(0, k, prev=False)
                with pe.Fori(1, B) as b:
                    for k in range(FK):
                        chunk(b, k)
                for k in range(4):
                    chunk(B, k, cur=False)

            if phases > 2:
                pe.wait_ge(wc_ok, 3)
                def narrow(b, g, m, x):
                    if g == 0:
                        pe.wait_ge(h_ok, at(h_ok, b + 2 * B))
                    if x == 0:
                        pe.wait_ge(c_ok, at(c_ok, b, 2 * g + m - 1 - ((g, m) in ((0, 1), (1, 0)))))
                    last = three(narrow_ps(g, m)[:, x * T:(x + 1) * T],
                                 lambda j, a: WC[:, a, 2 * m + x, j, g * P:(g + 1) * P],
                                 lambda j, a: h[:, a, j, :], CC)
                    if x:
                        last.then_inc(c_full, 1)

                def narrow_first(b):
                    for m in range(2):
                        for x in range(2):
                            narrow(b, 0, m, x)
                    narrow(b, 1, 0, 0)

                def head_step(b, i, cur=True, prev=True, following=True):
                    if cur:
                        g, lo = i // 4, 32 * (i % 4)
                        if i % 4 == 0:
                            pe.wait_ge(c_ok, at(c_ok, b, 2 * g + 1))
                        pe.wait_ge(e_exp, at(e_exp, b, i - 2))
                        for t in range(TT):
                            keys = (t + 1) * P
                            ps = bank[(1, 3)[i % 2] if t else (2, 5)[i % 2]]
                            for m in range(2):
                                nc.tensor.matmul(ps[:, m * keys:(m + 1) * keys],
                                                 v[lo:lo + 32, g % 2, m, 0, t * P:(t + 1) * P],
                                                 v[lo:lo + 32, g % 2, m, 1, 0:keys], start=(m == 0), stop=False,
                                                 skip_group_check=True)
                        for t in range(TT):
                            keys = (t + 1) * P
                            ps = bank[(1, 3)[i % 2] if t else (2, 5)[i % 2]]
                            masked = ps[:, 0:2 * keys].rearrange("p (m n) -> p m n", m=2)[:, :, keys - P:]
                            last = nc.tensor.matmul(masked, ident_r[:, :], repeat(mask_r[:, :], 1, 2),
                                                    start=False, stop=True, skip_group_check=True)
                        last.then_inc(e_full, 1)
                    if cur and i in NARROW_AT:
                        narrow(b, *NARROW_AT[i], 1)
                    if cur and i + 1 in NARROW_AT:
                        narrow(b, *NARROW_AT[i + 1], 0)
                    n = i - 2
                    if n >= 0 and cur or n < 0 and prev:
                        pe.wait_ge(e_diff, at(e_diff, b, n))
                        pe.wait_ge(t_ok, at(t_ok, b, n - 1))
                        for k, lo in enumerate((0, P, 2 * P)):
                            last = nc.tensor.transpose(bank[4][:, k * P:(k + 1) * P], pc[:, n % 2, 0, lo:lo + P],
                                                       ident[:, :])
                        last.then_inc(t_full, 1)
                    n = i - 3
                    if n >= 0 and cur or n < 0 and prev:
                        pe.wait_ge(t_ok, at(t_ok, b, n))
                        if n == 0:
                            pe.wait_ge(v1_ok, at(v1_ok, b))
                            pe.wait_ge(y_ev, at(y_ev, 2 * B - 1))
                            pe.wait_ge(d_read, at(d_read, b - 1))
                        o = n % H1 * 16
                        e = min(o + P, C)
                        nc.tensor.matmul(y_ps[:, o:e], ptf[:, n % 2, 0:P], v1[:, 0, o:e], start=True, stop=True)
                        nc.tensor.matmul(y_ps[:, T + o:T + e], ptf[:, n % 2, P:2 * P], v1[:, 0, o:e],
                                         start=True, stop=False)
                        nc.tensor.matmul(y_ps[:, T + o:T + e], ptf[:, n % 2, 2 * P:3 * P], v1[:, 1, o:e],
                                         start=False, stop=True).then_inc(av_done, 1)
                    if i == 0 and cur:
                        pe.wait_ge(c_ok, at(c_ok, b, 1))
                        for t in range(TT):
                            last = three(tr_ps[:, t * C:(t + 1) * C], lambda j, a: h[:, a, j, t * P:(t + 1) * P],
                                         lambda j, a: WV1[:, a, j, :], CC)
                        last.then_inc(v1_full, 1)
                    if i == PREP_AT + 1 and cur:
                        prep(b + 2 * B + 1, xn_early)
                    if following and 13 <= i <= 14:
                        narrow(b + 1, 0, i - 13, 0)
                        narrow(b + 1, 0, i - 13, 1)
                    if following and i == 15:
                        narrow(b + 1, 1, 0, 0)
                    if i == DIFF_AT and prev:
                        pe.wait_ge(d_ok, at(d_ok, b - 1))
                        if cur:
                            pe.wait_ge(v1_ok, at(v1_ok, b))
                        for c in range(CC):
                            for t in range(TT):
                                last = nc.tensor.transpose(tr_ps[:, c * T + t * P:c * T + (t + 1) * P],
                                                           y_t[:, t, c * P:(c + 1) * P], ident[:, :])
                        last.then_inc(dt_full, 1)
                    if i == DIFF_AT + 1 and prev:
                        pe.wait_ge(dr_lo, at(dr_lo, b - 1))
                        for c in range(CC):
                            last = three(tr_ps[:, c * T:(c + 1) * T], lambda j, a: WP1[:, a, j, c * P:(c + 1) * P],
                                         lambda j, a: dr[:, a, j, :], CC)
                        last.then_inc(y_full, 1)
                    if i == DIFF_AT + 3 and prev:
                        finish(b + 2 * B - 1)

                pe.wait_ge(x_moved, at(x_moved, 2 * B - 1))
                narrow_first(0)
                for i in range(H1):
                    head_step(0, i, prev=False)
                with pe.Fori(1, B - 1) as b:
                    for i in range(H1):
                        head_step(b, i)
                for i in range(H1):
                    head_step(B - 1, i, following=False)
                for i in range(DIFF_AT + 4):
                    head_step(B, i, cur=False, following=False)

            if phases > 3:
                pe.wait_ge(wd_ok, NGU + 3)
                def router(b):
                    pe.wait_ge(h_hi, at(h_hi, b + 3 * B))
                    pe.wait_ge(cb_lo, at(cb_lo, b - 1))
                    for t in range(TT):
                        for c in range(CC):
                            last = nc.tensor.matmul(bank[3][:, t * E1:(t + 1) * E1], h_f[:, c, t * P:(t + 1) * P],
                                                    gw_sb[:, c, :], start=(c == 0), stop=(c == CC - 1))
                    last.then_inc(lg_full, 1)

                def weights_transposed(b):
                    pe.wait_ge(cb_ok, at(cb_ok, b))
                    for t in range(TT):
                        last = nc.tensor.transpose(bank[3][:, t * P:(t + 1) * P], comb[:, t, :], ident[:, :])
                    last.then_inc(cbt_full, 1)

                def spread(b, k):
                    k %= EK
                    pe.wait_ge(eg_mul, at(eg_mul, b, last_user(k, 2, EK)))
                    for a in range(2):
                        last = nc.tensor.matmul(bank[4 + k % 2][:, 0:T], sel[:, k * P:(k + 1) * P], comb_r[:, a],
                                                start=(a == 0), stop=(a == 1))
                    last.then_inc(bc_full, 1)

                def down(b, n):
                    pe.wait_ge(eg_lo, at(eg_lo, b, n))
                    if n == 0:
                        pe.wait_ge(y_ev, at(y_ev, b + 3 * B - 1))
                    for c in range(CC):
                        last = three(y_ps[:, c * T:(c + 1) * T], lambda j, a: WD1[:, a, n % EK, c * P:(c + 1) * P],
                                     lambda j, a: gu_slot(n % EK, a), 1, first=(n == 0 and c == 0),
                                     last=(n % EK == EK - 1), skip_group_check=True)
                    last.then_inc(edown, 1)

                def chunk(b, k, cur=True, prev=True):
                    if cur:
                        if k == 0:
                            pe.wait_ge(h_ok, at(h_ok, b + 3 * B))
                        pe.wait_ge(eg_up, at(eg_up, b, last_user(k, 3, EK)))
                        for x, w in enumerate((WG1, WU1)):
                            last = three(bank[k % 3][:, x * T:(x + 1) * T],
                                         lambda j, a: w[:, a, j, k * P:(k + 1) * P], lambda j, a: h[:, a, j, :], CC)
                        last.then_inc(eg_full, 1)
                    if k == 0 and prev:
                        spread(b - 1, EK - 1)
                    if k >= 1 and cur:
                        if k == 1:
                            pe.wait_ge(cb_lo, at(cb_lo, b))
                        spread(b, k - 1)
                    n = k - 3
                    if n >= 0 and cur or n < 0 and prev:
                        down(b, n)
                    if k == 4 and prev:
                        finish(b + 3 * B - 1)
                    if k == 5 and cur:
                        prep(b + 3 * B + 1, xn_early)
                    if k == 6 and cur:
                        router(b + 1)
                    if k == EK - 1 and cur:
                        weights_transposed(b + 1)

                router(0)
                weights_transposed(0)
                for k in range(EK):
                    chunk(0, k, prev=False)
                with pe.Fori(1, B) as b:
                    for k in range(EK):
                        chunk(b, k)
                for k in range(5):
                    chunk(B, k, cur=False)


PHASES = 4


def kernel(**inputs):
    import numpy as np
    import concourse.bacc as bacc
    from concourse.bass_utils import run_bass_kernel_spmd

    i = {k: np.asarray(a) for k, a in inputs.items()}
    t = np.ascontiguousarray
    pad = lambda a, n, ax, val: np.concatenate([a, np.full([n - a.shape[d] if d == ax else a.shape[d]
                                                            for d in range(a.ndim)], val, a.dtype)], ax)
    w1 = i["L1_ffn_w1"]
    chunks = lambda a: a.reshape(-1, P, a.shape[1]).transpose(1, 0, 2).reshape(P, -1)
    arrays = {
        "x_in": t(i["L0_attn_x"].reshape(B * T, C)),
        "c_t0": t(i["L0_c"].T), "c_t1": t(i["L1_c"].T),
        "wmod0": t(i["L0_wmod"]), "wmod1": t(i["L1_wmod"]),
        "wqkv0": t(i["L0_attn_w_qkv"]), "wout0": t(i["L0_attn_w_out"]),
        "lut_b": t(np.broadcast_to(i["L0_ffn_lut"][None, :], (P, LUT))),
        "ffn_idx": t(np.concatenate([chunks(pad(i["L0_ffn_gate_idx"], FP, 0, LUT).T),
                                     chunks(pad(i["L0_ffn_up_idx"], FP, 0, LUT).T),
                                     chunks(pad(i["L0_ffn_down_idx"], FP, 1, LUT).T),
                                     np.zeros((P, B * PART - FLAT_B), i["L0_ffn_gate_idx"].dtype)], 1)),
        "w_c": t(i["L1_attn_Wqkv"][:, :4 * P].reshape(CC, P, 4, P).transpose(1, 2, 0, 3).reshape(P, -1)),
        "w_vp": t(np.concatenate([chunks(i["L1_attn_Wqkv"][:, 4 * P:]), chunks(i["L1_attn_Wproj"])], 1)),
        "lam_v": t(np.broadcast_to(np.concatenate([i["L1_attn_lambda_" + k] for k in ("q1", "k1", "q2", "k2")])[None],
                                   (P, 4 * D1))),
        "gatew": t(chunks(i["L1_ffn_gate_w"].T)),
        "w_gu": t(np.concatenate([chunks(w1[:, :I1].reshape(EI, C).T), chunks(w1[:, I1:].reshape(EI, C).T)], 1)),
        "w_d": t(chunks(i["L1_ffn_w2"].transpose(0, 2, 1).reshape(EI, C))),
    }
    nc = bacc.Bacc("TRN2", target_bir_lowering=False, num_devices=1)
    args = [nc.dram_tensor(k, a.shape, mybir.dt.from_np(a.dtype), kind="ExternalInput").ap() for k, a in arrays.items()]
    args.append(nc.dram_tensor("out", *[(B * T, C), F32], kind="ExternalOutput").ap())
    program(nc, *args, phases=PHASES)
    r = run_bass_kernel_spmd(nc, [arrays], core_ids=[0])
    return r.results[0]["out"].reshape(B, T, C)
```

```python
from contextlib import ExitStack

import concourse.bass as bass
from concourse import mybir

F32 = mybir.dt.float32
F32R = mybir.dt.float32r
I32 = mybir.dt.int32
ALU = mybir.AluOpType
ACT = mybir.ActivationFunctionType
AX = mybir.AxisListType.X

P = 128
B, T, C = 8, 256, 256
CC = C // P
TT = T // P
H0, D0 = 16, 128
SCALE0 = D0 ** -0.5
LUT, INTER = 16, 688
FK = -(-INTER // P)
FP = FK * P
H1, D1 = 16, 8
SCALE1 = D1 ** -0.5
LAMBDA_INIT = 0.8 - 0.6 * 2.718281828459045 ** (-0.3)
EPS = 1e-5
E1, I1 = 8, 176
EI = E1 * I1
EK = EI // P
NARROW_AT = {0: (1, 0), 2: (1, 1), 4: (2, 0), 6: (2, 1), 8: (3, 0), 10: (3, 1)}
DIFF_AT = 7
PREP_AT = 10
STEPS = 4 * B
OFF = 8
PIECE = 1024
RING = 3
NEG = -(2.0 ** 100)
FLAT_B = 2 * CC * FP + FK * C
PART = -(-FLAT_B // (B - 1) // 4) * 4
NB = -(-FLAT_B // PIECE)
NGU = -(-2 * CC * EI // PIECE)


def repeat(ap, axis, n):
    ap = ap.unsqueeze(axis)
    shape = list(ap.shape)
    shape[axis] = n
    return ap.broadcast_to(shape)


def last_user(k, slots, chunks):
    return k - slots if k >= slots else max(j for j in range(chunks) if j % slots == k % slots) - chunks


def program(nc, x_in, c_t, wmod0, wmod1, wqkv0, wout0, lut_b, ffn_idx, w_c, w_vp, lam_v, gatew, w_gu, w_d, out):
    ctx = ExitStack()
    with ctx:
        def sb(name, shape, dt=F32):
            return ctx.enter_context(nc.sbuf_tensor(name, shape, dt))

        per, ahead = {}, {}

        def sem(name, events=1, head=0):
            made = ctx.enter_context(nc.semaphore(name))
            per[name], ahead[name] = events, head
            names[id(made)] = name
            return made

        def at(s, step, n=0):
            name = names[id(s)]
            return step * per[name] + (n + 1 + ahead[name])

        names = {}

        bank = [ctx.enter_context(nc.psum_tensor(f"bank{i}", [P, 512], F32)) for i in range(8)]
        tr_ps, y_ps = bank[6], bank[7]
        x_dram = nc.dram_tensor("x_steps", ((STEPS + 2) * T, C), F32).ap()
        out_steps = out.rearrange("(s t p) c -> s p t c", t=TT, p=P)
        x_steps = x_dram.rearrange("(s t p) c -> s p t c", t=TT, p=P)

        ident = sb("ident", [P, P])
        raw = sb("raw", [P, RING, PIECE])
        mod = sb("mod", [P, STEPS + 2, 6])
        mod_now = sb("mod_now", [P, 4])
        gate_now = sb("gate_now", [P, 2])
        c_sb = sb("c_sb", [P, 2, CC, B])
        cs = sb("cs", [P, 2, CC, B])
        x_cur = sb("x_cur", [P, TT, C])
        x_next = sb("x_next", [P, TT, C])
        xn = sb("xn", [P, TT, C])
        x_out = xn
        h_f = sb("h_f", [P, CC, T])
        y_t = sb("y_t", [P, CC, T])
        stats = sb("stats", [P, TT, 6])
        mv = sb("mv", [P, TT, 2])
        ve = sb("ve", [P, TT])
        rstd = sb("rstd", [P, TT])
        mhalf = sb("mhalf", [P, 32])
        work = sb("work", [P, 2048])
        probs = work[:, 0:1024].rearrange("p (s t n) -> p s t n", s=2, t=TT)
        nmax = sb("nmax", [P, 2, TT])
        den = sb("den", [P, 2, TT])
        rden = sb("rden", [P, 2, TT])
        warm = sb("warm", [P, 1])
        lut_sb = sb("lut_sb", [P, LUT])
        mask_f = sb("mask_f", [P, P])
        lanes = sb("lanes", [P, 1], I32)
        lane_bit = sb("lane_bit", [P, 2], I32)
        low_q = sb("low_q", [P, 1])
        low_k = sb("low_k", [P, 1])
        lam_sb = sb("lam_sb", [P, 4, D1])
        lam_p = sb("lam_p", [P, 2, D1])
        lam_e = sb("lam_e", [P, 2])
        nlam = sb("nlam", [P, 1])
        nmax1 = sb("nmax1", [P, 2, TT, 2])
        den1 = sb("den1", [P, 2, TT, 2])
        rall = sb("rall", [P, H1, TT, 2])
        rall_old = sb("rall_old", [P, H1, TT])
        ratio = sb("ratio", [P, 2, TT])
        ssum = sb("ssum", [P, 32])
        tri = sb("tri", [P, E1, E1])
        gw_sb = sb("gw_sb", [P, CC, E1])
        r_max = sb("r_max", [P, TT])
        euler = sb("euler", [P, TT, E1])
        r_l = sb("r_l", [P, TT, E1])
        r_e = sb("r_e", [P, TT, E1])
        r_w = sb("r_w", [P, TT, E1])
        r_rank = sb("r_rank", [P, TT, E1])
        r_sum = sb("r_sum", [P, TT])

        W = sb("W", [P, 32768], F32R)
        h = sb("h", [P, 2, CC, T], F32R)
        qk = sb("qk", [P, 2, 2, 2, T], F32R)
        v = sb("v", [P, 2, 2, TT, 512], F32R)
        pt = sb("pt", [P, 2, 2, TT, T], F32R)
        mask_r = sb("mask_r", [P, P], F32R)
        ident_r = sb("ident_r", [P, P], F32R)
        with nc.sbuf_tensor("ot", [P, 4, 2, T], F32R) as ot:
            pass
        spare = sb("spare", [P, 2048])

        WQK = W[:, 0:16384].rearrange("p (l c m n) -> p l c m n", l=2, c=CC, m=2)
        WV = W[:, 16384:24576].rearrange("p (l c n) -> p l c n", l=2, c=CC)
        WO = W[:, 24576:32768].rearrange("p (l h n) -> p l h n", l=2, h=H0)

        WB = W[:, 0:2 * FLAT_B].rearrange("p (l n) -> p l n", l=2)
        WG = WB[:, :, 0:CC * FP].rearrange("p l (c n) -> p l c n", c=CC)
        WU = WB[:, :, CC * FP:2 * CC * FP].rearrange("p l (c n) -> p l c n", c=CC)
        WD = WB[:, :, 2 * CC * FP:FLAT_B].rearrange("p l (k n) -> p l k n", k=FK)
        C0 = 2 * FLAT_B
        WC = W[:, C0:C0 + 8192].rearrange("p (l m c n) -> p l m c n", l=2, m=4, c=CC)
        WVP = W[:, C0 + 8192:C0 + 10240].rearrange("p (l n) -> p l n", l=2)
        WV1 = WVP[:, :, 0:512].rearrange("p l (c n) -> p l c n", c=CC)
        WP1 = WVP[:, :, 512:1024].rearrange("p l (c n) -> p l c n", c=CC)
        G0 = C0 + 10240
        WGU = W[:, G0:G0 + 4 * CC * EI].rearrange("p (l n) -> p l n", l=2)
        WG1 = WGU[:, :, 0:CC * EI].rearrange("p l (c n) -> p l c n", c=CC)
        WU1 = WGU[:, :, CC * EI:2 * CC * EI].rearrange("p l (c n) -> p l c n", c=CC)
        WDD = W[:, 0:2 * EK * C].rearrange("p (l n) -> p l n", l=2)
        WD1 = WDD.rearrange("p l (k n) -> p l k n", k=EK)
        sel = W[0:E1, G0 + 4 * CC * EI:G0 + 4 * CC * EI + EI]
        def gu_slot(k, part):
            return pt[:, k % 2, part, k // 2 % 2, :]
        sg = work[:, 0:512].rearrange("p (s n) -> p s n", s=2)
        guf = work[:, 512:1024].rearrange("p (s n) -> p s n", s=2)

        def gated(k):
            return work[:, (512, 768, 1536, 1792)[k % 4]:][:, 0:T]

        pc = work[:, 0:1536].rearrange("p (s m n) -> p s m n", s=2, m=2)
        v1 = work[:, 1536:2048].rearrange("p (t n) -> p t n", t=TT)
        ptf = raw[:, 2, 0:768].rearrange("p (s n) -> p s n", s=2)
        x_early = spare[:, 0:512].rearrange("p (t n) -> p t n", t=TT)
        xn_early = spare[:, 512:1024].rearrange("p (t n) -> p t n", t=TT)
        square = spare[:, 1024:1536].rearrange("p (t n) -> p t n", t=TT)
        dr = v[:, 0, :, :, T:2 * T]
        comb = work[:, 1024:1280].rearrange("p (t n) -> p t n", t=TT)
        r_gt = work[:, 1280:1408].rearrange("p (t e j) -> p t e j", t=TT, e=E1)
        r_eq = work[:, 1408:1536].rearrange("p (t e j) -> p t e j", t=TT, e=E1)
        comb_r = qk[0:E1, 0, :, 0, :]

        s_const = sem("s_const")
        s_pool = sem("s_pool")
        raw_in = [sem(f"raw_in{i}") for i in range(RING)]
        raw_used = sem("raw_used")
        raw_hi = sem("raw_hi")
        c_in = sem("c_in")
        c_silu = sem("c_silu")
        mod_ps = sem("mod_ps")
        x_first = sem("x_first")
        x_second = sem("x_second")
        x_copy = sem("x_copy")
        x_load = sem("x_load", 16, 16)
        x_store = sem("x_store", 16, 16)
        dchain = sem("dchain")
        mod_cp = sem("mod_cp")
        var_ok = sem("var_ok")
        rstd_ok = sem("rstd_ok")
        xn_ok = sem("xn_ok")
        xnt_full = sem("xnt_full")
        h_hi = sem("h_hi")
        h_high = sem("h_high")
        h_ok = sem("h_ok")
        y_full = sem("y_full", 1, -2 * B)
        y_ev = sem("y_ev", 1, OFF)
        yt_full = sem("yt_full")
        x_moved = sem("x_moved", 1, OFF)
        gate_ok = sem("gate_ok")
        p_carrier = sem("p_carrier")
        carrier = sem("carrier")
        sp_carrier = sem("sp_carrier")
        dcom2 = sem("dcom2")
        dcom = sem("dcom")

        block = ctx.enter_context(nc.Block())

        def cols(w, lo, n):
            return w.rearrange("(c p) n -> p c n", p=P)[:, :, lo:lo + n]

        def piece(kind, g):
            if kind in "01":
                return cols((wmod0, wmod1)[int(kind)], 512 * g, 512)
            if kind == "o":
                return wout0[512 * g:512 * (g + 1), :].rearrange("(h p) n -> p h n", p=P)
            return cols(wqkv0, "qkv".index(kind) * H0 * D0 + 512 * g, 512)

        first_pieces = [("0", 0), ("q", 0), ("k", 0), ("v", 0)]
        late_pieces = {0: [("q", 1)], 1: [("k", 1)], 2: [("v", 1)], 3: [("o", 0), ("0", 1)], 4: [("q", 2)],
                       5: [("k", 2), ("0", 2)], 6: [("v", 2), ("1", 0)], 7: [("o", 1), ("1", 1)], 8: [("q", 3)],
                       9: [("k", 3), ("1", 2)], 10: [("v", 3)],
                       11: [("o", 2)], 12: [("o", 3)]}
        pieces = first_pieces + [x for i in sorted(late_pieces) for x in late_pieces[i]]
        splits = [x for x in pieces if x[0] not in "01"]
        mods = [x for x in pieces if x[0] in "01"]

        def slot(n):
            return raw[:, n % RING, :].rearrange("p (c n) -> p c n", c=4 if pieces[n][0] == "o" else CC)

        flat = raw[:, :, :].rearrange("p s n -> p (s n)")
        idx = flat[:, 0:PART].bitcast(I32)
        decoded = flat[:, PART:2 * PART]

        def entries(j):
            return decoded if j == 0 else flat[:, (2 + j % 2) * PART:(3 + j % 2) * PART]

        def raw_b(n):
            return work[:, 1024:2048] if n == 3 else raw[:, n % 4, :]

        def wa(x, part):
            kind, g = x
            if kind == "o":
                return WO[:, part, 4 * g:4 * (g + 1), :]
            if kind == "v":
                return WV[:, part, :, 512 * g:512 * (g + 1)]
            return WQK[:, part, :, "qk".index(kind), 512 * g:512 * (g + 1)]

        qk_full, qk_hi, qk_lo = sem("qk_full", H0), sem("qk_hi", H0), sem("qk_lo", H0, OFF)
        s_full, s_max, s_exp = sem("s_full", H0), sem("s_max", H0), sem("s_exp", H0, OFF)
        s_rden, s_norm = sem("s_rden", H0), sem("s_norm", H0)
        pt_full, pt_hi, pt_lo = sem("pt_full", H0), sem("pt_hi", H0), sem("pt_lo", H0, OFF)
        o_full, o_hi, o_lo = sem("o_full", H0), sem("o_hi", H0), sem("o_lo", H0, OFF)
        v_full, v_hi, v_lo = sem("v_full", 8), sem("v_hi", 8), sem("v_lo", 8, OFF)
        proj_done = sem("proj_done", H0, OFF)

        ffn_w = nc.dram_tensor("ffn_w", (P, (B - 1) * PART), F32).ap()
        raw2_in = [sem(f"raw2_in{i}") for i in range(NB)]
        raw2_used = sem("raw2_used")
        small_in = sem("small_in")
        idx_in, dec_out = sem("idx_in"), sem("dec_out")
        entry = sem("entry", LUT, OFF)
        pchain = sem("pchain", LUT - 1, OFF)
        pchain2 = sem("pchain2")
        dec_out_1 = sem("dec_out_1")
        bc_hi = sem("bc_hi")
        wc_ok, wd_ok, lam_ok, lam_exp, lane_ok = (sem(n) for n in ("wc_ok", "wd_ok", "lam_ok", "lam_exp", "lane_ok"))
        gu_full, gu_silu, gu_mul = sem("gu_full", FK), sem("gu_silu", FK), sem("gu_mul", FK, OFF)
        gu_hi, gu_lo, down_done = sem("gu_hi", FK), sem("gu_lo", FK, OFF), sem("down_done", FK, OFF)
        eg_full, eg_silu, eg_up, eg_mul = (
            sem("eg_full", EK), sem("eg_silu", EK), sem("eg_up", EK, OFF), sem("eg_mul", EK, OFF))
        eg_hi, eg_lo, edown = sem("eg_hi", EK), sem("eg_lo", EK, OFF), sem("edown", EK, OFF)
        bc_full = sem("bc_full", EK, OFF)
        lg_full, lg_max, lg_sub, lg_exp, cb_ok, cbt_full, cb_hi, cb_lo = (
            sem("lg_full"), sem("lg_max"), sem("lg_sub"), sem("lg_exp"), sem("cb_ok"), sem("cbt_full"), sem("cb_hi"), sem("cb_lo", 1, OFF))
        comb_clear = sem("comb_clear")
        dr_chain, r_rec = sem("dr_chain", 6), sem("r_rec")
        v1_full, v1_ok = sem("v1_full"), sem("v1_ok", 1, OFF)
        c_full, c_hi, c_ok = sem("c_full", 8), sem("c_hi", 8), sem("c_ok", 8, OFF)
        e_full, e_max, e_exp, e_diff = sem("e_full", H1), sem("e_max", H1), sem("e_exp", H1, OFF), sem("e_diff", H1)
        e_rec, e_rat = sem("e_rec", H1), sem("e_rat", H1)
        t_full, t_ok, av_done = sem("t_full", H1), sem("t_ok", H1, OFF), sem("av_done", H1, OFF)
        rms_in, rms_ok, d_ok, dt_full, dr_hi, dr_lo = (sem(n) for n in ("rms_in", "rms_ok", "d_ok", "dt_full", "dr_hi", "dr_lo"))
        early_in = sem("early_in", 16)
        d_chain, d_square, r_moved, d_read = sem("d_chain"), sem("d_square"), sem("r_moved"), sem("d_read", 1, OFF)

        def narrow_ps(g, m):
            return tr_ps if (g, m) == (0, 1) else bank[0]

        @block.sync
        def _(sp):
            sp.sem_inc(x_store, 16)
            sp.sem_inc(x_load, 16)
            x9 = x_in.rearrange("(s t p) c -> s p t c", t=TT, p=P)
            sp.dma_start(x_cur[:, :, :], x9[0]).then_inc(x_first, 16)
            for n, (kind, g) in enumerate(pieces):
                if n >= RING:
                    old = pieces[n - RING]
                    if old in mods:
                        sp.wait_ge(mod_ps, mods.index(old) + 1)
                    else:
                        sp.wait_ge(raw_used, splits.index(old) + 1)
                sp.dma_start(slot(n), piece(kind, g)).then_inc(raw_in[n % RING], 16)
                if n == len(first_pieces) - 1:
                    sp.dma_start(x_next[:, :, :], x9[1]).then_inc(x_second, 16)
            sp.wait_ge(x_copy, 32)
            for first, last in ((0, 3 * B), (3 * B, 4 * B)):
                with sp.Fori(first, last) as s:
                    sp.wait_ge(x_moved, at(x_moved, s))
                    sp.sem_inc(sp_carrier, 1)
                    dst = x_steps[s + B] if first == 0 else out_steps[s - 3 * B]
                    sp.dma_start(dst, x_out[:, :, :]).then_inc(x_store, 16)
                    sp.dma_start(x_next[:, :, :], x_steps[s + 2]).then_inc(x_load, 16)
                    sp.wait_ge(x_store, at(x_store, s, 15))
                    sp.sem_inc(sp_carrier, 1)
            sp.wait_ge(x_load, 16 * B * 4 + 16)

        @block.gpsimd
        def _(pool):
            nc.gpsimd.memset(ident[:, :], 0.0).then_inc(s_pool, 1)
            nc.gpsimd.memset(mhalf[:, :], -0.5).then_inc(s_pool, 1)
            nc.gpsimd.memset(euler[:, :, :], 2.718281828459045)
            pool.wait_ge(s_pool, 2)
            nc.gpsimd.affine_select(out=ident[:, :], in_=ident[:, :], compare_op=ALU.not_equal, fill=1.0, base=0,
                                    pattern=[[-1, P]], channel_multiplier=1).then_inc(s_const, 1)

            pool.sem_inc(pchain, OFF)

            def rstd_stage(s):
                pool.wait_ge(var_ok, at(var_ok, s))
                nc.gpsimd.tensor_tensor(rstd[:, :], ve[:, :], mhalf[:, 0:TT], ALU.pow).then_inc(rstd_ok, 1)

            nc.gpsimd.memset(mask_f[:, :], 0.0).then_inc(s_pool, 1)
            nc.gpsimd.memset(tri[:, :, :], 0.0).then_inc(s_pool, 1)
            nc.gpsimd.iota(lanes[:, :], [[0, 1]], base=0, channel_multiplier=1).then_inc(lane_ok, 1)
            pool.wait_ge(s_pool, 4)
            nc.gpsimd.affine_select(out=mask_f[:, :], in_=mask_f[:, :], compare_op=ALU.is_ge, fill=NEG, base=0,
                                    pattern=[[-1, P]], channel_multiplier=1).then_inc(lane_ok, 1)
            nc.gpsimd.affine_select(out=tri[:, :, :], in_=tri[:, :, :], compare_op=ALU.is_ge, fill=1.0, base=0,
                                    pattern=[[-1, E1], [1, E1]], channel_multiplier=0).then_inc(lane_ok, 1)
            pool.dma_start(lut_sb[:, :], lut_b).then_inc(small_in, 16)
            pool.dma_start(lam_sb[:, :, :].rearrange("p a b -> p (a b)"), lam_v).then_inc(small_in, 16)
            pool.dma_start(gw_sb[:, :, :].rearrange("p a b -> p (a b)"), gatew).then_inc(small_in, 16)
            rstd_stage(0)
            pool.wait_ge(x_second, 16)
            pool.dma_start(x_dram[0:B * T, :], x_in[0:B * T, :]).then_inc(x_copy, 16)
            pool.dma_start(x_dram[STEPS * T:(STEPS + 2) * T, :], x_in[0:2 * T, :]).then_inc(x_copy, 16)
            pool.wait_ge(small_in, 48)
            rstd_stage(1)
            pool.wait_ge(raw_used, len(splits))
            pool.wait_ge(mod_ps, len(mods))
            pool.sem_inc(dec_out_1, 1)
            ffn_parts = ffn_idx.rearrange("p (b n) -> b p n", b=B)
            pool.dma_start(idx, ffn_parts[0]).then_inc(idx_in, 16)
            with pool.Fori(1, B) as b:
                for j in range(1, LUT):
                    pool.wait_ge(entry, at(entry, b - 1, j))
                    if j > 1:
                        pool.sem_inc(p_carrier, 1)
                        pool.wait_ge(pchain, at(pchain, b - 1, j - 2))
                    nc.gpsimd.tensor_tensor(decoded, decoded, entries(j), ALU.add).then_inc(pchain, 1)
                pool.wait_ge(pchain, at(pchain, b - 1, LUT - 2))
                pool.sem_inc(p_carrier, 1)
                pool.dma_start(ffn_w.rearrange("p (b n) -> b p n", b=B - 1)[b - 1], decoded).then_inc(dec_out, 16)
                pool.dma_start(idx, ffn_parts[b]).then_inc(idx_in, 16)
                pool.wait_ge(dec_out, b * 16)
                pool.sem_inc(dec_out_1, 1)
                rstd_stage(b + 1)

            pool.wait_ge(idx_in, 16 * B)
            for n in range(NB):
                lo, width = n * PIECE, min(PIECE, FLAT_B - n * PIECE)
                if n == 4:
                    pool.wait_ge(raw2_used, 1)
                pool.dma_start(raw_b(n)[:, 0:width], ffn_w[:, lo:lo + width]).then_inc(raw2_in[n], 16)
            count = {"chain": 0, "load": B}

            def link(ins):
                count["chain"] += 1
                ins.then_inc(pchain2, 1)
                pool.wait_ge(pchain2, count["chain"])

            def load(place, src):
                pool.dma_start(place, src).then_inc(idx_in, 16)
                count["load"] += 1
                pool.wait_ge(idx_in, 16 * count["load"])

            def load_split(place, src, dst, lo, width, done):
                place = place[:, 0:width]
                load(place, src)
                link(nc.gpsimd.tensor_copy(dst[:, 0, lo:lo + width], place))
                link(nc.gpsimd.tensor_tensor(dst[:, 1, lo:lo + width], place,
                                             dst[:, 0, lo:lo + width].bitcast(F32), ALU.subtract))
                pool.sem_inc(done, 1)

            def split_c(m):
                for c in range(CC):
                    src = repeat(q[:, m, c].rearrange("p (h d) -> p h d", d=D1), 2, 4)
                    hi = WC[:, 0, m, c].rearrange("p (h r d) -> p h r d", r=4, d=D1)
                    lo = WC[:, 1, m, c].rearrange("p (h r d) -> p h r d", r=4, d=D1)
                    link(nc.gpsimd.tensor_copy(hi, src))
                    link(nc.gpsimd.tensor_tensor(lo, src, hi.bitcast(F32), ALU.subtract))
                pool.sem_inc(wc_ok, 1)

            pool.wait_ge(raw2_used, 3)
            q = raw[:, 2, :].rearrange("p (m c n) -> p m c n", m=4, c=CC)
            load(raw[:, 2, :], w_c)
            pool.wait_ge(qk_full, at(qk_full, B - 1, H0 - 1))
            for m in (0, 2):
                link(nc.gpsimd.tensor_scalar(q[:, m], q[:, m], SCALE1, None, ALU.mult))
            for b in range(B):
                pool.wait_ge(xn_ok, at(xn_ok, B + b))
                if b == 0:
                    pool.wait_ge(proj_done, at(proj_done, B - 1, H0 - 1))
                pool.wait_ge(x_store, at(x_store, b + 1, 15))
                pool.dma_start(x_early, x_steps[B + b + 1]).then_inc(early_in, 16)
                rstd_stage(B + b + 1)
                if b < 4:
                    split_c(b)
                if b == 4:
                    load_split(raw[:, 0], w_vp, WVP, 0, PIECE, wc_ok)
            pool.wait_ge(down_done, at(down_done, B - 1, FK - 1))
            def router(b):
                pool.wait_ge(lg_sub, at(lg_sub, b))
                nc.gpsimd.tensor_tensor(r_e[:, :, :], euler[:, :, :], r_l[:, :, :], ALU.pow).then_inc(lg_exp, 1)

            def load_early(s):
                pool.wait_ge(xn_ok, at(xn_ok, s))
                pool.sem_inc(p_carrier, 1)
                pool.wait_ge(x_store, at(x_store, s + 1 - B, 15))
                pool.sem_inc(p_carrier, 1)
                pool.dma_start(x_early, x_steps[s + 1]).then_inc(early_in, 16)

            for b in range(B + 1):
                if b == B:
                    load_early(3 * B)
                    router(0)
                if b < B:
                    pool.wait_ge(xn_ok, at(xn_ok, 2 * B + b))
                    pool.wait_ge(x_store, at(x_store, B + b + 1, 15))
                    pool.dma_start(x_early, x_steps[2 * B + b + 1]).then_inc(early_in, 16)
                if b:
                    pool.wait_ge(d_read, at(d_read, b - 1))
                    nc.gpsimd.tensor_tensor(square[:, :, :], y_t[:, :, :], y_t[:, :, :], ALU.mult
                                            ).then_inc(d_square, 1)
                    pool.wait_ge(rms_in, at(rms_in, b - 1))
                    nc.gpsimd.tensor_tensor(ssum[:, :], ssum[:, :], mhalf[:, :], ALU.pow).then_inc(rms_ok, 1)
                    pool.wait_ge(rms_ok, at(rms_ok, b - 1))
                    yv = y_t[:, :, :].rearrange("p t (h d) -> p t h d", h=H1)
                    rr = repeat(ssum[:, :].rearrange("p (t h) -> p t h", t=TT), 3, 16)
                    nc.gpsimd.tensor_tensor(yv, yv, rr, ALU.mult).then_inc(d_ok, 1)
                if b < B:
                    rstd_stage(2 * B + b + 1)
                if b < NGU // 2:
                    for k in (2 * b, 2 * b + 1):
                        lo, width = k * PIECE, min(PIECE, 2 * CC * EI - k * PIECE)
                        load_split(raw[:, k % 2], w_gu[:, lo:lo + width], WGU, lo, width, wd_ok)
                if b == NGU // 2:
                    link(nc.gpsimd.memset(flat[0:E1, 0:EI], 1.0))
                    for cmp, base, sign in ((ALU.is_ge, 0, 1), (ALU.is_ge, I1 - 1, -1)):
                        link(nc.gpsimd.affine_select(out=flat[0:E1, 0:EI], in_=flat[0:E1, 0:EI], compare_op=cmp,
                                                     fill=0.0, base=base, pattern=[[sign, EI]],
                                                     channel_multiplier=-sign * I1))
                    link(nc.gpsimd.tensor_copy(sel, flat[0:E1, 0:EI]))
                if NGU // 2 < b <= NGU // 2 + 3:
                    k = b - NGU // 2 - 1
                    lo, width = k * PIECE, min(PIECE, EK * C - k * PIECE)
                    load_split(raw[:, k % 2], w_d[:, lo:lo + width], WDD, lo, width, wd_ok)
            pool.wait_ge(x_copy, 32)
            with pool.Fori(0, B) as b:
                rstd_stage(b + 3 * B + 1)
                load_early(3 * B + b + 1)
                router(b + 1)

        @block.scalar
        def _(act):
            act.sem_inc(s_exp, OFF)
            act.sem_inc(e_exp, OFF)
            act.sem_inc(t_ok, OFF)
            act.sem_inc(v1_ok, OFF)
            act.sem_inc(y_ev, OFF)
            act.dma_start(c_sb[:, :, :, :].rearrange("p l c b -> p (l c b)"), c_t).then_inc(c_in, 16)
            act.wait_ge(c_in, 16)
            nc.scalar.activation(cs[:, :, :, :], c_sb[:, :, :, :], ACT.Silu).then_inc(c_silu, 1)

            def split(x):
                n = pieces.index(x)
                act.wait_ge(raw_in[n % RING], 16 * (n // RING + 1))
                act.activation(wa(x, 0), slot(n), ACT.Copy, scale=SCALE0 if x[0] == "q" else 1.0).then_inc(raw_hi, 1)

            def prep(s, tr_ps=tr_ps):
                act.wait_ge(xnt_full, at(xnt_full, s))
                act.wait_ge(mod_cp, at(mod_cp, s))
                for c in range(CC):
                    last = nc.scalar.activation(h_f[:, c, :], tr_ps[:, c * T:(c + 1) * T], ACT.Identity,
                                                bias=mod_now[:, c:c + 1], scale=mod_now[:, 2 + c:3 + c])
                last.then_inc(h_hi, 1)

            def finish(s, y_ps=y_ps, ready=None):
                if ready:
                    done, batch, last_one = ready
                    act.wait_ge(done, at(done, batch, last_one))
                else:
                    act.wait_ge(y_full, at(y_full, s))
                act.wait_ge(gate_ok, at(gate_ok, s))
                for c in range(CC):
                    last = nc.scalar.activation(y_t[:, c, :], y_ps[:, c * T:(c + 1) * T], ACT.Copy,
                                                scale=gate_now[:, c:c + 1])
                last.then_inc(y_ev, 1)

            split(("q", 0))
            prep(0)
            split(("k", 0))
            split(("v", 0))
            act.wait_ge(lam_ok, 1)
            nc.scalar.activation(lam_e[:, :], lam_e[:, :], ACT.Exp).then_inc(lam_exp, 1)

            def head_step(b, i, cur=True, prev=True):
                if cur:
                    act.wait_ge(qk_full, at(qk_full, b, i))
                    nc.scalar.activation(qk[:, i % 2, 0].rearrange("p m n -> p (m n)"), bank[i % 2][:, :], ACT.Copy
                                         ).then_inc(qk_hi, 1)
                if cur and i == H0 - 1:
                    prep(b + 1)
                n = i - 3
                if n >= 0 and cur or n < 0 and prev:
                    act.wait_ge(o_full, at(o_full, b, n))
                    act.wait_ge(proj_done, at(proj_done, b, n - 4))
                    nc.scalar.activation(ot[:, n % 4, 0, :], bank[4][:, 0:T], ACT.Copy).then_inc(o_hi, 1)
                n = i - 1
                if n >= 0 and cur or n < 0 and prev:
                    act.wait_ge(s_max, at(s_max, b, n))
                    for t in range(TT):
                        last = nc.scalar.activation(probs[:, n % 2, t, :], bank[2][:, t * T:(t + 1) * T], ACT.Exp,
                                                    bias=nmax[:, n % 2, t:t + 1], accum_out=den[:, n % 2, t:t + 1])
                    last.then_inc(s_exp, 1)
                if cur and i % 2 == 0:
                    act.wait_ge(v_full, at(v_full, b, i // 2))
                    nc.scalar.activation(v[:, i // 4 % 2, 0, i // 2 % 2, :], bank[5][:, :], ACT.Copy).then_inc(v_hi, 1)
                n = i - 2
                if n >= 0 and cur or n < 0 and prev:
                    act.wait_ge(pt_full, at(pt_full, b, n))
                    nc.scalar.activation(pt[:, n % 2, 0].rearrange("p t n -> p (t n)"), bank[3][:, :], ACT.Copy
                                         ).then_inc(pt_hi, 1)
                if i == 3 and prev:
                    finish(b - 1, ready=(proj_done, b - 1, H0 - 1))

            nc.scalar.activation(warm[:, :], mhalf[:, 0:1], ACT.Exp)
            for i in range(H0):
                head_step(0, i, prev=False)
                for x in late_pieces.get(i, []):
                    if x not in mods:
                        split(x)
            with act.Fori(1, B) as b:
                for i in range(H0):
                    head_step(b, i)
            for i in range(5):
                if i < 4:
                    head_step(B, i, cur=False)
                lo, width = i * PIECE, min(PIECE, FLAT_B - i * PIECE)
                act.wait_ge(raw2_in[i], 16)
                nc.scalar.activation(WB[:, 0, lo:lo + width], raw_b(i)[:, 0:width], ACT.Copy).then_inc(bc_hi, 1)

            def chunk(b, k, cur=True, prev=True):
                if k == 2 and prev:
                    finish(b + B - 1, ready=(down_done, b - 1, FK - 1))
                if k == 4 and cur:
                    prep(b + B + 1, bank[4])
                if cur:
                    act.wait_ge(gu_full, at(gu_full, b, k))
                    act.wait_ge(gu_mul, at(gu_mul, b, k - 2))
                    nc.scalar.activation(sg[:, k % 2, :], bank[k % 4][:, 0:T], ACT.Silu).then_inc(gu_silu, 1)
                n = k - 1
                if n >= 0 and cur or n < 0 and prev:
                    act.wait_ge(gu_mul, at(gu_mul, b, n))
                    act.wait_ge(down_done, at(down_done, b, last_user(n % FK, 4, FK) - (n < 0) * FK))
                    nc.scalar.activation(gu_slot(n % FK, 0), guf[:, n % 2, :], ACT.Copy).then_inc(gu_hi, 1)

            for k in range(FK):
                chunk(0, k, prev=False)
            with act.Fori(1, B) as b:
                for k in range(FK):
                    chunk(b, k)
            for k in range(3):
                chunk(B, k, cur=False)

            nc.scalar.activation(warm[:, :], mhalf[:, 0:1], ACT.Exp)
            def narrow(b, g, m):
                act.wait_ge(c_full, at(c_full, b, 2 * g + m))
                nc.scalar.activation(qk[:, m, 0].rearrange("p x n -> p (x n)"), narrow_ps(g, m)[:, :], ACT.Copy
                                     ).then_inc(c_hi, 1)

            def head_step(b, i, cur=True, prev=True, following=True):
                n = i - 2
                if n >= 0 and cur or n < 0 and prev:
                    act.wait_ge(t_full, at(t_full, b, n))
                    act.wait_ge(av_done, at(av_done, b, n - 2))
                    nc.scalar.activation(ptf[:, n % 2, :], bank[4][:, 0:384], ACT.Copy).then_inc(t_ok, 1)
                if i == 2 and cur:
                    act.wait_ge(v1_full, at(v1_full, b))
                    act.wait_ge(av_done, at(av_done, b - 1, H1 - 1))
                    nc.scalar.activation(v1[:, :, :].rearrange("p t n -> p (t n)"), tr_ps[:, :], ACT.Copy
                                         ).then_inc(v1_ok, 1)
                if cur and i in NARROW_AT:
                    narrow(b, *NARROW_AT[i])
                if i == 15 and following:
                    narrow(b + 1, 0, 1)
                if i == PREP_AT + 2 and cur:
                    prep(b + 2 * B + 1, bank[0])
                if cur:
                    act.wait_ge(e_max, at(e_max, b, i))
                    for t in range(TT):
                        keys = (t + 1) * P
                        ps = bank[(1, 3)[i % 2] if t else (2, 5)[i % 2]]
                        for m in range(2):
                            last = nc.scalar.activation(pc[:, i % 2, m, t * P:t * P + keys],
                                                        ps[:, m * keys:(m + 1) * keys], ACT.Exp,
                                                        bias=nmax1[:, i % 2, t, m:m + 1],
                                                        accum_out=den1[:, i % 2, t, m:m + 1])
                    last.then_inc(e_exp, 1)
                if i == DIFF_AT + 2 and prev:
                    finish(b + 2 * B - 1, tr_ps)
                if i == 13 and following:
                    narrow(b + 1, 0, 0)
                if i == DIFF_AT and prev:
                    act.wait_ge(dt_full, at(dt_full, b - 1))
                    nc.scalar.activation(dr[:, 0], tr_ps[:, :].rearrange("p (c n) -> p c n", c=CC), ACT.Copy
                                         ).then_inc(dr_hi, 1)

            narrow(0, 0, 0)
            narrow(0, 0, 1)
            for i in range(H1):
                head_step(0, i, prev=False)
            with act.Fori(1, B - 1) as b:
                for i in range(H1):
                    head_step(b, i)
            for i in range(H1):
                head_step(B - 1, i, following=False)

            def chunk(b, k, cur=True, prev=True):
                if k == 1 and cur:
                    act.wait_ge(cbt_full, at(cbt_full, b))
                    act.wait_ge(bc_full, at(bc_full, b - 1, EK - 1))
                    nc.scalar.activation(comb_r[:, 0], bank[3][0:E1, 0:T], ACT.Copy).then_inc(cb_hi, 1)
                if k == 3 and prev:
                    finish(b + 3 * B - 1, ready=(edown, b - 1, EK - 1))
                if k == 4 and cur:
                    prep(b + 3 * B + 1, bank[3])
                if cur:
                    act.wait_ge(eg_full, at(eg_full, b, k))
                    act.wait_ge(eg_up, at(eg_up, b, k - 2 + (k == 0)))
                    nc.scalar.activation(sg[:, k % 2, :], bank[k % 3][:, 0:T], ACT.Silu).then_inc(eg_silu, 1)
                n = k - 2
                if n >= 0 and cur or n < 0 and prev:
                    act.wait_ge(eg_mul, at(eg_mul, b, n))
                    act.wait_ge(edown, at(edown, b, last_user(n % EK, 4, EK) - (n < 0) * EK))
                    nc.scalar.activation(gu_slot(n % EK, 0), gated(n % EK), ACT.Copy).then_inc(eg_hi, 1)

            def tail(*steps):
                for i in steps:
                    head_step(B, i, cur=False, following=False)

            tail(0, 1, 2)
            for k in range(EK):
                if k == 3:
                    tail(*range(3, DIFF_AT + 3))
                chunk(0, k, prev=False)
            with act.Fori(1, B) as b:
                for k in range(EK):
                    chunk(b, k)
            for k in range(4):
                chunk(B, k, cur=False)

        @block.vector
        def _(dve):
            seq = [0]

            def link(ins):
                seq[0] += 1
                ins.then_inc(dchain, 1)
                dve.wait_ge(dchain, seq[0])

            for s_ in (qk_lo, pt_lo, o_lo, v_lo, x_moved, d_read, entry, gu_lo, eg_lo, gu_mul, eg_mul, eg_up, c_ok, cb_lo):
                dve.sem_inc(s_, OFF)
            link(nc.vector.memset(mod[:, STEPS:, :], 0.0))
            def shifts():
                dve.wait_ge(mod_ps, 1)
                link(nc.vector.tensor_copy(mod[:, 0:B, 0:4], bank[1][:, 0:32].rearrange("p (k b) -> p b k", k=4)))
                link(nc.vector.tensor_scalar(mod[:, 0:B, 2:4], mod[:, 0:B, 2:4], 1.0, None, ALU.add))

            def table():
                dve.wait_ge(mod_ps, len(mods))
                src = tr_ps[:, 0:192].rearrange("p (l k b) -> p l b k", l=2, k=12)
                nc.vector.tensor_copy(mod[:, 0:B, 4:6], src[:, 0, :, 4:6])
                nc.vector.tensor_copy(mod[:, B:2 * B, :], src[:, 0, :, 6:12])
                nc.vector.tensor_copy(mod[:, 2 * B:3 * B, :], src[:, 1, :, 0:6])
                link(nc.vector.tensor_copy(mod[:, 3 * B:4 * B, :], src[:, 1, :, 6:12]))
                scale = mod[:, B:STEPS, 2:4]
                link(nc.vector.tensor_scalar(scale, scale, 1.0, None, ALU.add))
                gt = work[:, 1024:1024 + 2 * STEPS].rearrange("p (s k) -> p s k", k=2)
                ga = mod[:, 0:STEPS, 4:6]
                link(nc.vector.tensor_scalar(gt, ga, 0.0, 2.0, ALU.is_ge, ALU.mult))
                link(nc.vector.tensor_scalar(gt, gt, -1.0, None, ALU.add))
                link(nc.vector.tensor_tensor(ga, ga, gt, ALU.mult))
                link(nc.vector.tensor_scalar(ga, ga, 0.25, None, ALU.max))
                link(nc.vector.tensor_tensor(ga, ga, gt, ALU.mult))

            def modulation(s):
                nc.vector.tensor_copy(mod_now[:, :], mod[:, s, 0:4]).then_inc(mod_cp, 1)

            def prep_stats(s, x):
                modulation(s)
                moments(s, x)

            def moments(s, x):
                n = [0]

                def step_link(ins):
                    n[0] += 1
                    ins.then_inc(dcom, 1)
                    dve.wait_ge(dcom, s * 2 + n[0])

                for t in range(TT):
                    last = nc.vector.bn_stats(stats[:, t, :], x[:, t, :])
                step_link(last)
                dve.sem_inc(carrier, 1)
                for t in range(TT):
                    last = nc.vector.bn_aggr(mv[:, t, :], stats[:, t, :])
                step_link(last)
                nc.vector.tensor_scalar(ve[:, :], mv[:, :, 1], EPS, None, ALU.add).then_inc(var_ok, 1)

            def prep_apply(s, x, xn=xn):
                if xn is x_out:
                    dve.wait_ge(x_store, at(x_store, s - 2, 15))
                    dve.sem_inc(carrier, 1)
                dve.wait_ge(rstd_ok, at(rstd_ok, s))
                for t in range(TT):
                    last = nc.vector.tensor_scalar(xn[:, t, :], x[:, t, :], mv[:, t, 0:1], rstd[:, t:t + 1],
                                                   ALU.subtract, ALU.mult)
                last.then_inc(xn_ok, 1)

            def prep(s, x):
                prep_stats(s, x)
                prep_apply(s, x)

            def prep_low(s, free=None):
                dve.wait_ge(h_hi, at(h_hi, s))
                if free:
                    dve.wait_ge(free[0], at(*free))
                    dve.sem_inc(carrier, 1)
                nc.vector.tensor_copy(h[:, 0], h_f[:, :, :]).then_inc(h_high, 1)
                dve.wait_ge(h_high, at(h_high, s))
                nc.vector.tensor_tensor(h[:, 1], h_f[:, :, :], h[:, 0].bitcast(F32), ALU.subtract).then_inc(h_ok, 1)

            def gate(s):
                dve.wait_ge(y_ev, at(y_ev, s - 1))
                nc.vector.tensor_copy(gate_now[:, :], mod[:, s, 4:6]).then_inc(gate_ok, 1)

            def finish(s, late=False):
                dve.wait_ge(yt_full, at(yt_full, s))
                if late:
                    dve.wait_ge(x_load, at(x_load, s - 1, 15))
                    dve.sem_inc(carrier, 1)
                    dve.wait_ge(x_store, at(x_store, s - 1, 15))
                    dve.sem_inc(carrier, 1)
                nc.vector.tensor_tensor(x_out[:, :, :], x_cur[:, :, :],
                                        tr_ps[:, :].rearrange("p (t n) -> p t n", t=TT), ALU.add).then_inc(dcom2, 1)
                dve.wait_ge(dcom2, at(dcom2, s))
                nc.vector.tensor_copy(x_cur[:, :, :], x_next[:, :, :]).then_inc(x_moved, 1)

            def split(x):
                n = splits.index(x)
                dve.wait_ge(raw_hi, n + 1)
                nc.vector.scalar_tensor_tensor(out=wa(x, 1), in0=slot(pieces.index(x)),
                                               scalar=SCALE0 if x[0] == "q" else 1.0, in1=wa(x, 0).bitcast(F32),
                                               op0=ALU.mult, op1=ALU.subtract).then_inc(raw_used, 1)

            dve.wait_ge(x_first, 16)
            moments(0, x_cur)
            prep_apply(0, x_cur)
            shifts()
            modulation(0)
            split(("q", 0))
            prep_low(0)
            split(("k", 0))
            split(("v", 0))
            dve.wait_ge(lane_ok, 3)
            for x in range(2):
                last = nc.vector.tensor_scalar(lane_bit[:, x:x + 1], lanes[:, :], (16, 8)[x], None, ALU.bitwise_and)
            link(last)
            nc.vector.tensor_scalar(low_q[:, :], lane_bit[:, 0:1], -1.0 / 16, None, ALU.mult)
            nc.vector.tensor_scalar(low_k[:, :], lane_bit[:, 1:2], -1.0 / 8, None, ALU.mult)
            nc.vector.tensor_copy(mask_r[:, :], mask_f[:, :])
            dve.wait_ge(s_const, 1)
            link(nc.vector.tensor_copy(ident_r[:, :], ident[:, :]))
            dve.wait_ge(small_in, 48)
            link(nc.vector.tensor_tensor(lam_p[:, :, :], lam_sb[:, 0::2, :], lam_sb[:, 1::2, :], ALU.mult))
            nc.vector.tensor_reduce(lam_e[:, :], lam_p[:, :, :], AX, ALU.add).then_inc(lam_ok, 1)
            dve.wait_ge(lam_exp, 1)
            link(nc.vector.tensor_tensor(nlam[:, :], lam_e[:, 1:2], lam_e[:, 0:1], ALU.subtract))
            link(nc.vector.tensor_scalar(nlam[:, :], nlam[:, :], -LAMBDA_INIT, None, ALU.add))

            def head_step(b, i, cur=True, prev=True):
                if cur:
                    dve.wait_ge(qk_hi, at(qk_hi, b, i))
                    nc.vector.tensor_tensor(qk[:, i % 2, 1].rearrange("p m n -> p (m n)"), bank[i % 2][:, :],
                                            qk[:, i % 2, 0].rearrange("p m n -> p (m n)").bitcast(F32),
                                            ALU.subtract).then_inc(qk_lo, 1)
                if cur and i == H0 - 1:
                    prep_low(b + 1)
                n = i - 1
                if n >= 0 and cur or n < 0 and prev:
                    dve.wait_ge(s_full, at(s_full, b, n))
                    nc.vector.tensor_reduce(nmax[:, n % 2, :], bank[2][:, :].rearrange("p (t n) -> p t n", t=TT),
                                            AX, ALU.max, negate=True).then_inc(s_max, 1)
                n = i - 3
                if n >= 0 and cur or n < 0 and prev:
                    dve.wait_ge(o_hi, at(o_hi, b, n))
                    nc.vector.tensor_tensor(ot[:, n % 4, 1, :], bank[4][:, 0:T], ot[:, n % 4, 0, :].bitcast(F32),
                                            ALU.subtract).then_inc(o_lo, 1)
                if cur and prev and 2 <= i < 2 + LUT // 2:
                    if i == 2:
                        dve.wait_ge(idx_in, b * 16)
                        dve.sem_inc(carrier, 1)
                    for j in (2 * i - 4, 2 * i - 3):
                        if j == 0:
                            dve.wait_ge(dec_out_1, b)
                            dve.sem_inc(carrier, 1)
                        if j > 2:
                            dve.wait_ge(pchain, at(pchain, b - 1, j - 3))
                            dve.sem_inc(carrier, 1)
                        nc.vector.tensor_scalar(entries(j), idx, float(j), lut_sb[:, j:j + 1], ALU.is_equal, ALU.mult
                                                ).then_inc(entry, 1)
                n = i - 1
                if n >= 0 and cur or n < 0 and prev:
                    dve.wait_ge(s_exp, at(s_exp, b, n))
                    nc.vector.reciprocal(rden[:, n % 2, :], den[:, n % 2, :]).then_inc(s_rden, 1)
                    dve.wait_ge(s_rden, at(s_rden, b, n))
                    for t in range(TT):
                        last = nc.vector.tensor_scalar(probs[:, n % 2, t, :], probs[:, n % 2, t, :],
                                                       rden[:, n % 2, t:t + 1], None, ALU.mult)
                    last.then_inc(s_norm, 1)
                if cur and i % 2 == 0:
                    dve.wait_ge(v_hi, at(v_hi, b, i // 2))
                    nc.vector.tensor_tensor(v[:, i // 4 % 2, 1, i // 2 % 2, :], bank[5][:, :],
                                            v[:, i // 4 % 2, 0, i // 2 % 2, :].bitcast(F32), ALU.subtract
                                            ).then_inc(v_lo, 1)
                n = i - 2
                if n >= 0 and cur or n < 0 and prev:
                    dve.wait_ge(pt_hi, at(pt_hi, b, n))
                    nc.vector.tensor_tensor(pt[:, n % 2, 1].rearrange("p t n -> p (t n)"), bank[3][:, :],
                                            pt[:, n % 2, 0].rearrange("p t n -> p (t n)").bitcast(F32),
                                            ALU.subtract).then_inc(pt_lo, 1)
                if i == 1 and prev:
                    gate(b - 1)
                if i == 5 and prev:
                    finish(b - 1)
                if cur and i == 12:
                    if prev:
                        dve.wait_ge(x_load, at(x_load, b - 1, 15))
                    else:
                        dve.wait_ge(x_second, 16)
                    prep_stats(b + 1, x_next)
                if cur and i == 13:
                    prep_apply(b + 1, x_next)

            for i in range(H0):
                head_step(0, i, prev=False)
                for x in late_pieces.get(i, []):
                    if x not in mods:
                        split(x)
                if i == 10:
                    table()
            with dve.Fori(1, B) as b:
                for i in range(H0):
                    head_step(b, i)
            for i in range(6):
                head_step(B, i, cur=False)
                if i < NB:
                    lo, width = i * PIECE, min(PIECE, FLAT_B - i * PIECE)
                    dve.wait_ge(bc_hi, i + 1)
                    nc.vector.tensor_tensor(WB[:, 1, lo:lo + width], raw_b(i)[:, 0:width],
                                            WB[:, 0, lo:lo + width].bitcast(F32), ALU.subtract).then_inc(raw2_used, 1)

            def chunk(b, k, cur=True, prev=True):
                if k == FK - 1 and cur:
                    prep_low(b + B + 1, free=(gu_full, b, FK - 1))
                if cur:
                    dve.wait_ge(gu_lo, at(gu_lo, b, k - 2))
                    dve.wait_ge(gu_silu, at(gu_silu, b, k))
                    nc.vector.tensor_tensor(guf[:, k % 2, :], sg[:, k % 2, :], bank[k % 4][:, T:2 * T], ALU.mult
                                            ).then_inc(gu_mul, 1)
                n = k - 1
                if n >= 0 and cur or n < 0 and prev:
                    dve.wait_ge(gu_hi, at(gu_hi, b, n))
                    nc.vector.tensor_tensor(gu_slot(n % FK, 1), guf[:, n % 2, :],
                                            gu_slot(n % FK, 0).bitcast(F32), ALU.subtract).then_inc(gu_lo, 1)
                if k == 0 and prev:
                    gate(b + B - 1)
                if k == 3 and prev:
                    finish(b + B - 1, late=True)
                if k == 1 and cur:
                    dve.wait_ge(early_in, at(early_in, b, 15))
                    dve.sem_inc(carrier, 1)
                    prep_stats(b + B + 1, x_early)
                if k == 2 and cur:
                    prep_apply(b + B + 1, x_early, xn_early)

            for k in range(FK):
                chunk(0, k, prev=False)
            with dve.Fori(1, B) as b:
                for k in range(FK):
                    chunk(b, k)
            for k in range(4):
                chunk(B, k, cur=False)

            def narrow(b, g, m):
                dve.wait_ge(c_hi, at(c_hi, b, 2 * g + m))
                for x in range(2):
                    last = nc.vector.scalar_tensor_tensor(
                        out=v[:, g % 2, m, x, 0:T], in0=qk[:, m, 0, x, :].bitcast(F32),
                        scalar=(low_q, low_k)[x][:, 0:1], in1=narrow_ps(g, m)[:, x * T:(x + 1) * T],
                        op0=ALU.mult, op1=ALU.add)
                last.then_inc(c_ok, 1)

            def output(b, stage):
                if stage == 0:
                    dve.wait_ge(av_done, at(av_done, b, H1 - 1))
                    r1 = repeat(rall_old[:, :, :].rearrange("p h t -> p t h"), 3, 16)
                    nc.vector.tensor_tensor(y_t[:, :, :].rearrange("p t (h d) -> p t h d", h=H1),
                                            y_ps[:, :].rearrange("p (t h d) -> p t h d", t=TT, h=H1),
                                            r1, ALU.mult).then_inc(d_read, 1)
                else:
                    dve.wait_ge(d_square, at(d_square, b))
                    nc.vector.tensor_reduce(ssum[:, :], square[:, :, :].rearrange("p t (h d) -> p (t h) d", h=H1),
                                            AX, ALU.add).then_inc(d_chain, 1)
                    dve.wait_ge(d_chain, at(d_chain, b))
                    dve.sem_inc(carrier, 1)
                    cc = (1.0 - LAMBDA_INIT) ** 2
                    nc.vector.tensor_scalar(ssum[:, :], ssum[:, :], 1.0 / (16 * cc), EPS / cc, ALU.mult, ALU.add
                                            ).then_inc(rms_in, 1)

            def head_step(b, i, cur=True, prev=True, following=True):
                if cur:
                    dve.wait_ge(e_full, at(e_full, b, i))
                    for t in range(TT):
                        keys = (t + 1) * P
                        ps = bank[(1, 3)[i % 2] if t else (2, 5)[i % 2]]
                        last = nc.vector.tensor_reduce(nmax1[:, i % 2, t, :],
                                                       ps[:, 0:2 * keys].rearrange("p (m n) -> p m n", m=2),
                                                       AX, ALU.max, negate=True)
                    last.then_inc(e_max, 1)
                if i == DIFF_AT + 1 and prev:
                    dve.wait_ge(dr_hi, at(dr_hi, b - 1))
                    nc.vector.tensor_tensor(dr[:, 1], tr_ps[:, :].rearrange("p (c n) -> p c n", c=CC),
                                            dr[:, 0].bitcast(F32), ALU.subtract
                                            ).then_inc(dr_lo, 1)
                if i == DIFF_AT + 4 and prev:
                    finish(b + 2 * B - 1, late=True)
                if i == 14 and following:
                    narrow(b + 1, 0, 0)
                if i == 1 and prev:
                    nc.vector.tensor_copy(rall_old[:, :, :], rall[:, :, :, 0]).then_inc(r_moved, 1)
                    dve.wait_ge(r_moved, at(r_moved, b - 1))
                n = i - 1
                if n >= 0 and cur or n < 0 and prev:
                    dve.wait_ge(e_exp, at(e_exp, b, n))
                    nc.vector.reciprocal(rall[:, n % H1, :, :], den1[:, n % 2, :, :]).then_inc(e_rec, 1)
                    dve.wait_ge(e_rec, at(e_rec, b, n))
                    nc.vector.scalar_tensor_tensor(out=ratio[:, n % 2, :], in0=den1[:, n % 2, :, 0],
                                                   scalar=nlam[:, 0:1], in1=rall[:, n % H1, :, 1], op0=ALU.mult,
                                                   op1=ALU.mult).then_inc(e_rat, 1)
                    dve.wait_ge(e_rat, at(e_rat, b, n))
                    for t in range(TT):
                        lo, hi = t * P, t * P + (t + 1) * P
                        last = nc.vector.scalar_tensor_tensor(
                            out=pc[:, n % 2, 0, lo:hi], in0=pc[:, n % 2, 1, lo:hi],
                            scalar=ratio[:, n % 2, t:t + 1], in1=pc[:, n % 2, 0, lo:hi], op0=ALU.mult, op1=ALU.add)
                    last.then_inc(e_diff, 1)
                if cur and i in NARROW_AT:
                    narrow(b, *NARROW_AT[i])
                if i == 2 and prev:
                    output(b - 1, 0)
                    gate(b + 2 * B - 1)
                if i == 4 and prev:
                    output(b - 1, 1)
                if i == PREP_AT - 1 and cur:
                    dve.wait_ge(early_in, at(early_in, b + B, 15))
                    dve.sem_inc(carrier, 1)
                    prep_stats(b + 2 * B + 1, x_early)
                if i == PREP_AT and cur:
                    prep_apply(b + 2 * B + 1, x_early, xn_early)
                if i == PREP_AT + 2 and cur:
                    prep_low(b + 2 * B + 1)
                if i == 15 and following:
                    narrow(b + 1, 0, 1)

            narrow(0, 0, 0)
            narrow(0, 0, 1)
            for i in range(H1):
                head_step(0, i, prev=False)
            with dve.Fori(1, B - 1) as b:
                for i in range(H1):
                    head_step(b, i)
            for i in range(H1):
                head_step(B - 1, i, following=False)


            def router_logits(b):
                dve.wait_ge(lg_full, at(lg_full, b))
                nc.vector.tensor_reduce(r_max[:, :], bank[3][:, 0:TT * E1].rearrange("p (t e) -> p t e", t=TT), AX,
                                        ALU.max).then_inc(lg_max, 1)
                dve.wait_ge(lg_max, at(lg_max, b))
                nc.vector.tensor_tensor(r_l[:, :, :], bank[3][:, 0:TT * E1].rearrange("p (t e) -> p t e", t=TT),
                                        repeat(r_max[:, :], 2, E1), ALU.subtract).then_inc(lg_sub, 1)

            def router_weights(b, half):
                n = [4 * half]

                def step_link(ins):
                    ins.then_inc(dr_chain, 1)
                    dve.wait_ge(dr_chain, at(dr_chain, b, n[0]))
                    n[0] += 1

                if half == 0:
                    rank(b, step_link)
                else:
                    weights(b, step_link)

            def rank(b, step_link):
                dve.wait_ge(lg_exp, at(lg_exp, b))

                ej = repeat(r_e[:, :, :], 2, E1)
                ee = repeat(r_e[:, :, :], 3, E1)
                tr = repeat(tri[:, :, :], 1, TT)
                nc.vector.tensor_tensor(r_gt, ej, ee, ALU.is_gt)
                step_link(nc.vector.tensor_tensor(r_eq, ej, ee, ALU.is_equal))
                step_link(nc.vector.tensor_tensor(r_eq, r_eq, tr, ALU.mult))
                step_link(nc.vector.tensor_tensor(r_gt, r_gt, r_eq, ALU.add))
                step_link(nc.vector.tensor_reduce(r_rank[:, :, :], r_gt, AX, ALU.add))

            def weights(b, step_link):
                step_link(nc.vector.scalar_tensor_tensor(out=r_w[:, :, :], in0=r_rank[:, :, :], scalar=2.0,
                                                         in1=r_e[:, :, :], op0=ALU.is_lt, op1=ALU.mult))
                step_link(nc.vector.tensor_reduce(r_sum[:, :], r_w[:, :, :], AX, ALU.add))
                nc.vector.reciprocal(r_sum[:, :], r_sum[:, :]).then_inc(r_rec, 1)
                dve.wait_ge(r_rec, at(r_rec, b))
                for t in range(TT):
                    last = nc.vector.tensor_scalar(comb[:, t, 0:E1], r_w[:, t, :], r_sum[:, t:t + 1], None, ALU.mult)
                last.then_inc(cb_ok, 1)

            def chunk(b, k, cur=True, prev=True):
                if k == 1 and cur:
                    dve.wait_ge(cb_hi, at(cb_hi, b))
                    nc.vector.tensor_tensor(comb_r[:, 1], bank[3][0:E1, 0:T], comb_r[:, 0].bitcast(F32), ALU.subtract
                                            ).then_inc(cb_lo, 1)
                if k == EK - 1 and cur:
                    prep_low(b + 3 * B + 1, free=(eg_full, b, EK - 1))
                if cur:
                    dve.wait_ge(eg_silu, at(eg_silu, b, k))
                    dve.wait_ge(eg_lo, at(eg_lo, b, last_user(k, 4, EK)))
                    nc.vector.tensor_tensor(gated(k), sg[:, k % 2, :], bank[k % 3][:, T:2 * T], ALU.mult
                                            ).then_inc(eg_up, 1)
                n = k - 1
                if n >= 0 and cur or n < 0 and prev:
                    dve.wait_ge(bc_full, at(bc_full, b, n))
                    dve.sem_inc(carrier, 1)
                    dve.wait_ge(eg_up, at(eg_up, b, n))
                    nc.vector.tensor_tensor(gated(n % EK), gated(n % EK), bank[4 + n % EK % 2][:, 0:T], ALU.mult
                                            ).then_inc(eg_mul, 1)
                n = k - 2
                if n >= 0 and cur or n < 0 and prev:
                    dve.wait_ge(eg_hi, at(eg_hi, b, n))
                    nc.vector.tensor_tensor(gu_slot(n % EK, 1), gated(n % EK),
                                            gu_slot(n % EK, 0).bitcast(F32), ALU.subtract).then_inc(eg_lo, 1)
                if k == 1 and prev:
                    gate(b + 3 * B - 1)
                if k == 4 and prev:
                    finish(b + 3 * B - 1, late=True)
                if k == 1 and cur:
                    dve.wait_ge(early_in, at(early_in, b + 2 * B, 15))
                    dve.sem_inc(carrier, 1)
                    prep_stats(b + 3 * B + 1, x_early)
                if k == 2 and cur:
                    prep_apply(b + 3 * B + 1, x_early, xn_early)
                if k == 6 and cur:
                    router_logits(b + 1)
                if k in (8, 9) and cur:
                    router_weights(b + 1, k - 8)

            def tail(*steps):
                for i in steps:
                    head_step(B, i, cur=False, following=False)

            tail(0, 1)
            router_logits(0)
            tail(2)
            nc.vector.memset(comb[:, :, :], 0.0).then_inc(comb_clear, 1)
            dve.wait_ge(comb_clear, 1)
            router_weights(0, 0)
            router_weights(0, 1)
            tail(3, 4)
            for k in range(EK):
                if k == 3:
                    tail(*range(5, DIFF_AT + 5))
                chunk(0, k, prev=False)
            with dve.Fori(1, B) as b:
                for k in range(EK):
                    chunk(b, k)
            for k in range(5):
                chunk(B, k, cur=False)

        @block.tensor
        def _(pe):
            for s_ in (proj_done, av_done, down_done, edown, bc_full):
                pe.sem_inc(s_, OFF)
            pe.wait_ge(c_silu, 1)

            def modulation(x):
                n = pieces.index(x)
                l = int(x[0])
                ps = bank[1] if x == ("0", 0) else tr_ps[:, 96 * l:96 * (l + 1)]
                pe.wait_ge(raw_in[n % RING], 16 * (n // RING + 1))
                for j in range(4):
                    k = 4 * x[1] + j
                    for c in range(CC):
                        last = nc.tensor.matmul(ps[:, 8 * k:8 * k + 8], slot(n)[:, c, P * j:P * (j + 1)],
                                                cs[:, l, c, :], start=(c == 0), stop=(c == CC - 1))
                last.then_inc(mod_ps, 1)

            def three(ps, w, m, n, first=True, last=True, **kw):
                parts = [(0, 0), (0, 1), (1, 0)]
                for j in range(n):
                    for a, (wp, mp) in enumerate(parts):
                        ins = nc.tensor.matmul(ps, w(j, wp), m(j, mp), start=(first and j == 0 and a == 0),
                                               stop=(last and j == n - 1 and a == 2), **kw)
                return ins

            def prep(s, xn=xn, tr_ps=tr_ps):
                pe.wait_ge(xn_ok, at(xn_ok, s))
                if tr_ps is bank[6]:
                    pe.wait_ge(x_moved, at(x_moved, s - 2))
                else:
                    pe.wait_ge(h_hi, at(h_hi, s - 1))
                for c in range(CC):
                    for t in range(TT):
                        last = nc.tensor.transpose(tr_ps[:, c * T + t * P:c * T + (t + 1) * P],
                                                   xn[:, t, c * P:(c + 1) * P], ident[:, :])
                last.then_inc(xnt_full, 1)

            def finish(s):
                pe.wait_ge(y_ev, at(y_ev, s))
                pe.wait_ge(h_hi, at(h_hi, s + 1))
                for t in range(TT):
                    for c in range(CC):
                        last = nc.tensor.transpose(tr_ps[:, t * C + c * P:t * C + (c + 1) * P],
                                                   y_t[:, c, t * P:(t + 1) * P], ident[:, :])
                last.then_inc(yt_full, 1)

            pe.wait_ge(s_const, 1)
            prep(0)
            modulation(first_pieces[0])

            def head_step(b, i, cur=True, prev=True):
                if cur:
                    if i == 0:
                        pe.wait_ge(h_ok, at(h_ok, b))
                    if not prev and i % 4 == 0:
                        pe.wait_ge(raw_used, splits.index(("k", i // 4)) + 1)
                    pe.wait_ge(qk_lo, at(qk_lo, b, i - 2))
                    for m in range(2):
                        last = three(bank[i % 2][:, m * T:(m + 1) * T],
                                     lambda j, a: WQK[:, a, j, m, i * P:(i + 1) * P],
                                     lambda j, a: h[:, a, j, :], CC)
                    last.then_inc(qk_full, 1)
                n = i - 1
                if n >= 0 and cur or n < 0 and prev:
                    pe.wait_ge(qk_lo, at(qk_lo, b, n))
                    pe.wait_ge(s_exp, at(s_exp, b, n - 1))
                    for q in range(TT):
                        last = three(bank[2][:, q * T:(q + 1) * T],
                                     lambda j, a: qk[:, n % 2, a, 0, q * P:(q + 1) * P],
                                     lambda j, a: qk[:, n % 2, a, 1, :], 1)
                    last.then_inc(s_full, 1)
                n = i - 3
                if n >= 0 and cur or n < 0 and prev:
                    pe.wait_ge(pt_lo, at(pt_lo, b, n))
                    pe.wait_ge(o_lo, at(o_lo, b, n - 1))
                    if n % 4 == 0:
                        pe.wait_ge(v_lo, at(v_lo, b, 2 * (n // 4) + 1))
                    three(bank[4][:, 0:T],
                          lambda j, a: v[:, n // 4 % 2, a, j, (n % 4) * P:(n % 4 + 1) * P],
                          lambda j, a: pt[:, n % 2, a, j, :], TT).then_inc(o_full, 1)
                if cur and i % 2 == 0:
                    g, t = i // 4, i // 2 % 2
                    if not prev and i % 4 == 0:
                        pe.wait_ge(raw_used, splits.index(("v", i // 4)) + 1)
                    pe.wait_ge(v_lo, at(v_lo, b, i // 2 - 1))
                    three(bank[5][:, :], lambda j, a: h[:, a, j, t * P:(t + 1) * P],
                          lambda j, a: WV[:, a, j, 512 * g:512 * (g + 1)], CC).then_inc(v_full, 1)
                n = i - 2
                if n >= 0 and cur or n < 0 and prev:
                    pe.wait_ge(s_norm, at(s_norm, b, n))
                    pe.wait_ge(pt_lo, at(pt_lo, b, n - 1))
                    for k in range(TT):
                        for q in range(TT):
                            last = nc.tensor.transpose(bank[3][:, k * T + q * P:k * T + (q + 1) * P],
                                                       probs[:, n % 2, q, k * P:(k + 1) * P], ident[:, :])
                    last.then_inc(pt_full, 1)
                n = i - 4
                if n >= 0 and cur or n < 0 and prev:
                    pe.wait_ge(o_lo, at(o_lo, b, n))
                    if not prev and n % 4 == 0:
                        pe.wait_ge(raw_used, splits.index(("o", n // 4)) + 1)
                    if n == 0:
                        pe.wait_ge(y_ev, at(y_ev, b - 1))
                    for c in range(CC):
                        last = three(y_ps[:, c * T:(c + 1) * T],
                                     lambda j, a: WO[:, a, n % H0, c * P:(c + 1) * P],
                                     lambda j, a: ot[:, n % 4, a, :], 1, first=(n == 0 and c == 0),
                                     last=(n == -1), skip_group_check=True)
                    last.then_inc(proj_done, 1)
                if i == 4 and prev:
                    finish(b - 1)
                if i == 14 and cur:
                    prep(b + 1)

            for i in range(H0):
                head_step(0, i, prev=False)
                for x in late_pieces.get(i, []):
                    if x in mods:
                        if x == ("0", 1):
                            pe.wait_ge(h_hi, at(h_hi, 0))
                        modulation(x)
            with pe.Fori(1, B) as b:
                for i in range(H0):
                    head_step(b, i)
            for i in range(5):
                head_step(B, i, cur=False)

            pe.wait_ge(raw2_used, NB)
            def down(b, n):
                pe.wait_ge(gu_lo, at(gu_lo, b, n))
                if n == 0:
                    pe.wait_ge(y_ev, at(y_ev, b + B - 1))
                for c in range(CC):
                    last = three(y_ps[:, c * T:(c + 1) * T], lambda j, a: WD[:, a, n % FK, c * P:(c + 1) * P],
                                 lambda j, a: gu_slot(n % FK, a), 1, first=(n == 0 and c == 0),
                                 last=(n % FK == FK - 1), skip_group_check=True)
                last.then_inc(down_done, 1)

            def chunk(b, k, cur=True, prev=True):
                if cur:
                    if k == 0:
                        pe.wait_ge(h_ok, at(h_ok, b + B))
                    pe.wait_ge(gu_mul, at(gu_mul, b, last_user(k, 4, FK)))
                    for x, w in enumerate((WG, WU)):
                        last = three(bank[k % 4][:, x * T:(x + 1) * T],
                                     lambda j, a: w[:, a, j, k * P:(k + 1) * P], lambda j, a: h[:, a, j, :], CC)
                    last.then_inc(gu_full, 1)
                if k < 2 and prev:
                    down(b, k - 2)
                if k == 3 and prev:
                    finish(b + B - 1)
                if k == 3 and cur:
                    prep(b + B + 1, xn_early, bank[4])
                if k == 3 and cur:
                    down(b, 0)
                if k >= 3 and cur:
                    down(b, k - 2)

            for k in range(FK):
                chunk(0, k, prev=False)
            with pe.Fori(1, B) as b:
                for k in range(FK):
                    chunk(b, k)
            for k in range(4):
                chunk(B, k, cur=False)

            pe.wait_ge(wc_ok, 5)
            def narrow(b, g, m, x):
                if g == 0:
                    pe.wait_ge(h_ok, at(h_ok, b + 2 * B))
                if x == 0:
                    pe.wait_ge(c_ok, at(c_ok, b, 2 * g + m - 1 - ((g, m) in ((0, 1), (1, 0)))))
                last = three(narrow_ps(g, m)[:, x * T:(x + 1) * T],
                             lambda j, a: WC[:, a, 2 * m + x, j, g * P:(g + 1) * P],
                             lambda j, a: h[:, a, j, :], CC)
                if x:
                    last.then_inc(c_full, 1)

            def narrow_first(b):
                for m in range(2):
                    for x in range(2):
                        narrow(b, 0, m, x)
                narrow(b, 1, 0, 0)

            def head_step(b, i, cur=True, prev=True, following=True):
                if cur:
                    g, lo = i // 4, 32 * (i % 4)
                    if i % 4 == 0:
                        pe.wait_ge(c_ok, at(c_ok, b, 2 * g + 1))
                    pe.wait_ge(e_exp, at(e_exp, b, i - 2))
                    for t in range(TT):
                        keys = (t + 1) * P
                        ps = bank[(1, 3)[i % 2] if t else (2, 5)[i % 2]]
                        for m in range(2):
                            nc.tensor.matmul(ps[:, m * keys:(m + 1) * keys],
                                             v[lo:lo + 32, g % 2, m, 0, t * P:(t + 1) * P],
                                             v[lo:lo + 32, g % 2, m, 1, 0:keys], start=(m == 0), stop=False,
                                             skip_group_check=True)
                    for t in range(TT):
                        keys = (t + 1) * P
                        ps = bank[(1, 3)[i % 2] if t else (2, 5)[i % 2]]
                        masked = ps[:, 0:2 * keys].rearrange("p (m n) -> p m n", m=2)[:, :, keys - P:]
                        last = nc.tensor.matmul(masked, ident_r[:, :], repeat(mask_r[:, :], 1, 2),
                                                start=False, stop=True, skip_group_check=True)
                    last.then_inc(e_full, 1)
                if cur and i in NARROW_AT:
                    narrow(b, *NARROW_AT[i], 1)
                n = i - 2
                if n >= 0 and cur or n < 0 and prev:
                    pe.wait_ge(e_diff, at(e_diff, b, n))
                    pe.wait_ge(t_ok, at(t_ok, b, n - 1))
                    for k, lo in enumerate((0, P, 2 * P)):
                        last = nc.tensor.transpose(bank[4][:, k * P:(k + 1) * P], pc[:, n % 2, 0, lo:lo + P],
                                                   ident[:, :])
                    last.then_inc(t_full, 1)
                n = i - 3
                if n >= 0 and cur or n < 0 and prev:
                    pe.wait_ge(t_ok, at(t_ok, b, n))
                    if n == 0:
                        pe.wait_ge(v1_ok, at(v1_ok, b))
                        pe.wait_ge(y_ev, at(y_ev, 2 * B - 1))
                        pe.wait_ge(d_read, at(d_read, b - 1))
                    o = n % H1 * 16
                    e = min(o + P, C)
                    nc.tensor.matmul(y_ps[:, o:e], ptf[:, n % 2, 0:P], v1[:, 0, o:e], start=True, stop=True)
                    nc.tensor.matmul(y_ps[:, T + o:T + e], ptf[:, n % 2, P:2 * P], v1[:, 0, o:e],
                                     start=True, stop=False)
                    nc.tensor.matmul(y_ps[:, T + o:T + e], ptf[:, n % 2, 2 * P:3 * P], v1[:, 1, o:e],
                                     start=False, stop=True).then_inc(av_done, 1)
                if i == 0 and cur:
                    pe.wait_ge(c_ok, at(c_ok, b, 1))
                    for t in range(TT):
                        last = three(tr_ps[:, t * C:(t + 1) * C], lambda j, a: h[:, a, j, t * P:(t + 1) * P],
                                     lambda j, a: WV1[:, a, j, :], CC)
                    last.then_inc(v1_full, 1)
                if i == PREP_AT + 1 and cur:
                    pe.wait_ge(c_ok, at(c_ok, b, 7))
                    prep(b + 2 * B + 1, xn_early, bank[0])
                if cur and i + 1 in NARROW_AT:
                    narrow(b, *NARROW_AT[i + 1], 0)
                if following and 13 <= i <= 14:
                    narrow(b + 1, 0, i - 13, 0)
                    narrow(b + 1, 0, i - 13, 1)
                if following and i == 15:
                    narrow(b + 1, 1, 0, 0)
                if i == DIFF_AT and prev:
                    pe.wait_ge(d_ok, at(d_ok, b - 1))
                    if cur:
                        pe.wait_ge(v1_ok, at(v1_ok, b))
                    for c in range(CC):
                        for t in range(TT):
                            last = nc.tensor.transpose(tr_ps[:, c * T + t * P:c * T + (t + 1) * P],
                                                       y_t[:, t, c * P:(c + 1) * P], ident[:, :])
                    last.then_inc(dt_full, 1)
                if i == DIFF_AT + 1 and prev:
                    pe.wait_ge(dr_lo, at(dr_lo, b - 1))
                    for c in range(CC):
                        last = three(tr_ps[:, c * T:(c + 1) * T], lambda j, a: WP1[:, a, j, c * P:(c + 1) * P],
                                     lambda j, a: dr[:, a, j, :], CC)
                    last.then_inc(y_full, 1)
                if i == DIFF_AT + 3 and prev:
                    finish(b + 2 * B - 1)

            pe.wait_ge(x_moved, at(x_moved, 2 * B - 1))
            narrow_first(0)
            for i in range(H1):
                head_step(0, i, prev=False)
            with pe.Fori(1, B - 1) as b:
                for i in range(H1):
                    head_step(b, i)
            for i in range(H1):
                head_step(B - 1, i, following=False)

            pe.wait_ge(wd_ok, NGU + 3)
            def router(b):
                pe.wait_ge(h_hi, at(h_hi, b + 3 * B))
                pe.wait_ge(cb_lo, at(cb_lo, b - 1))
                for t in range(TT):
                    for c in range(CC):
                        last = nc.tensor.matmul(bank[3][:, t * E1:(t + 1) * E1], h_f[:, c, t * P:(t + 1) * P],
                                                gw_sb[:, c, :], start=(c == 0), stop=(c == CC - 1))
                last.then_inc(lg_full, 1)

            def weights_transposed(b):
                pe.wait_ge(cb_ok, at(cb_ok, b))
                for t in range(TT):
                    last = nc.tensor.transpose(bank[3][:, t * P:(t + 1) * P], comb[:, t, :], ident[:, :])
                last.then_inc(cbt_full, 1)

            def spread(b, k):
                k %= EK
                pe.wait_ge(eg_mul, at(eg_mul, b, last_user(k, 2, EK)))
                for a in range(2):
                    last = nc.tensor.matmul(bank[4 + k % 2][:, 0:T], sel[:, k * P:(k + 1) * P], comb_r[:, a],
                                            start=(a == 0), stop=(a == 1))
                last.then_inc(bc_full, 1)

            def down(b, n):
                pe.wait_ge(eg_lo, at(eg_lo, b, n))
                if n == 0:
                    pe.wait_ge(y_ev, at(y_ev, b + 3 * B - 1))
                for c in range(CC):
                    last = three(y_ps[:, c * T:(c + 1) * T], lambda j, a: WD1[:, a, n % EK, c * P:(c + 1) * P],
                                 lambda j, a: gu_slot(n % EK, a), 1, first=(n == 0 and c == 0),
                                 last=(n % EK == EK - 1), skip_group_check=True)
                last.then_inc(edown, 1)

            def chunk(b, k, cur=True, prev=True):
                if cur:
                    if k == 0:
                        pe.wait_ge(h_ok, at(h_ok, b + 3 * B))
                    pe.wait_ge(eg_up, at(eg_up, b, last_user(k, 3, EK)))
                    for x, w in enumerate((WG1, WU1)):
                        last = three(bank[k % 3][:, x * T:(x + 1) * T],
                                     lambda j, a: w[:, a, j, k * P:(k + 1) * P], lambda j, a: h[:, a, j, :], CC)
                    last.then_inc(eg_full, 1)
                if k == 0 and prev:
                    spread(b - 1, EK - 1)
                if k == 0 and cur:
                    weights_transposed(b)
                if k >= 1 and cur:
                    if k == 1:
                        pe.wait_ge(cb_lo, at(cb_lo, b))
                    spread(b, k - 1)
                n = k - 3
                if n >= 0 and cur or n < 0 and prev:
                    down(b, n)
                if k == 4 and prev:
                    finish(b + 3 * B - 1)
                if k == 3 and cur:
                    prep(b + 3 * B + 1, xn_early, bank[3])
                if k == 5 and cur:
                    router(b + 1)

            def tail(*steps):
                for i in steps:
                    head_step(B, i, cur=False, following=False)

            tail(0, 1)
            pe.wait_ge(e_exp, at(e_exp, B - 1, H1 - 1))
            router(0)
            tail(2)
            for k in range(EK):
                if k == 3:
                    tail(*range(3, DIFF_AT + 4))
                chunk(0, k, prev=False)
            with pe.Fori(1, B) as b:
                for k in range(EK):
                    chunk(b, k)
            for k in range(5):
                chunk(B, k, cur=False)


def kernel(**inputs):
    import numpy as np
    import concourse.bacc as bacc
    from concourse.bass_utils import run_bass_kernel_spmd

    i = {k: np.asarray(a) for k, a in inputs.items()}
    t = np.ascontiguousarray
    pad = lambda a, n, ax, val: np.concatenate([a, np.full([n - a.shape[d] if d == ax else a.shape[d]
                                                            for d in range(a.ndim)], val, a.dtype)], ax)
    w1 = i["L1_ffn_w1"]
    chunks = lambda a: a.reshape(-1, P, a.shape[1]).transpose(1, 0, 2).reshape(P, -1)
    arrays = {
        "x_in": t(i["L0_attn_x"].reshape(B * T, C)),
        "c_t": t(np.concatenate([chunks(i["L0_c"].T), chunks(i["L1_c"].T)], 1)),
        "wmod0": t(i["L0_wmod"]), "wmod1": t(i["L1_wmod"]),
        "wqkv0": t(i["L0_attn_w_qkv"]), "wout0": t(i["L0_attn_w_out"]),
        "lut_b": t(np.broadcast_to(i["L0_ffn_lut"][None, :], (P, LUT))),
        "ffn_idx": t(np.concatenate([chunks(pad(i["L0_ffn_gate_idx"], FP, 0, LUT).T),
                                     chunks(pad(i["L0_ffn_up_idx"], FP, 0, LUT).T),
                                     chunks(pad(i["L0_ffn_down_idx"], FP, 1, LUT).T),
                                     np.zeros((P, B * PART - FLAT_B), i["L0_ffn_gate_idx"].dtype)], 1)),
        "w_c": t(i["L1_attn_Wqkv"][:, :4 * P].reshape(CC, P, 4, P).transpose(1, 2, 0, 3).reshape(P, -1)),
        "w_vp": t(np.concatenate([chunks(i["L1_attn_Wqkv"][:, 4 * P:]), chunks(i["L1_attn_Wproj"])], 1)),
        "lam_v": t(np.broadcast_to(np.concatenate([i["L1_attn_lambda_" + k] for k in ("q1", "k1", "q2", "k2")])[None],
                                   (P, 4 * D1))),
        "gatew": t(chunks(i["L1_ffn_gate_w"].T)),
        "w_gu": t(np.concatenate([chunks(w1[:, :I1].reshape(EI, C).T), chunks(w1[:, I1:].reshape(EI, C).T)], 1)),
        "w_d": t(chunks(i["L1_ffn_w2"].transpose(0, 2, 1).reshape(EI, C))),
    }
    nc = bacc.Bacc("TRN2", target_bir_lowering=False, num_devices=1)
    args = [nc.dram_tensor(k, a.shape, mybir.dt.from_np(a.dtype), kind="ExternalInput").ap() for k, a in arrays.items()]
    args.append(nc.dram_tensor("out", *[(B * T, C), F32], kind="ExternalOutput").ap())
    program(nc, *args)
    r = run_bass_kernel_spmd(nc, [arrays], core_ids=[0])
    return r.results[0]["out"].reshape(B, T, C)
```
